# Optimizing a Trainium2 kernel written in Bass

```python
import numpy as np
import jax
import jax.numpy as jnp

def _softmax(x, axis=-1):
    return jax.nn.softmax(x, axis=axis)

def _gelu(x):
    return jax.nn.gelu(x, approximate=True)

def _silu(x):
    return jax.nn.silu(x)

def _sigmoid(x):
    return jax.nn.sigmoid(x)

def _layernorm(x, axis=-1, eps=1e-05):
    m = jnp.mean(x, axis=axis, keepdims=True)
    v = jnp.var(x, axis=axis, keepdims=True)
    return (x - m) / jnp.sqrt(v + eps)

def _scatter_add(tgt, idx, src, axis=0):
    return tgt.at[idx].add(src)

def _segment_sum(src, seg, n):
    return jax.ops.segment_sum(src, seg, n)
kernel_name = 'mk_sandwich_d2_jaxref_r8_24cd88'

def setup_inputs(seed: int=0):
    np.random.seed(seed)
    _w = jnp.asarray

    def _L0_attn_setup():
        import jax, jax.numpy as jnp
        import numpy as np
        D_MODEL = 256
        N_HEADS = 16
        HEAD_DIM = 128
        WINDOW = 64
        ROPE_BASE = 10000.0
        B, N = (2, 256)
        INNER = N_HEADS * HEAD_DIM

        def _rotate_half(t):
            t1, t2 = jnp.split(t, 2, axis=-1)
            return jnp.concatenate([-t2, t1], axis=-1)

        def _rope(q, k, offset=0):
            D = q.shape[-1]
            inv_freq = 1.0 / ROPE_BASE ** (jnp.arange(0, D, 2, dtype=jnp.float32) / D)
            pos = jnp.arange(q.shape[2], dtype=jnp.float32) + offset
            ang = pos[:, None] * inv_freq[None, :]
            cos = jnp.concatenate([jnp.cos(ang), jnp.cos(ang)], axis=-1)
            sin = jnp.concatenate([jnp.sin(ang), jnp.sin(ang)], axis=-1)
            q_r = q * cos + _rotate_half(q) * sin
            k_r = k * cos + _rotate_half(k) * sin
            return (q_r, k_r)
        key = jax.random.key(seed)
        k1, k2, k3 = jax.random.split(key, 3)
        x = jax.random.normal(k1, (B, N, D_MODEL), dtype=jnp.float32)
        w_qkv = jax.random.normal(k2, (3 * INNER, D_MODEL), dtype=jnp.float32) / np.sqrt(D_MODEL)
        w_o = jax.random.normal(k3, (D_MODEL, INNER), dtype=jnp.float32) / np.sqrt(INNER)
        return {'x': x, 'w_qkv': w_qkv, 'w_o': w_o}
    _L0_attn_in = _L0_attn_setup()

    def _L0_ffn_setup():
        import jax, jax.numpy as jnp
        import numpy as np
        EPS = 1e-05
        ROPE_BASE = 150000.0
        NHEADS = 32
        KVHEADS = 8
        HEAD_DIM = 64
        TOP_K = 4

        def _rms(x, w):
            return x * jax.lax.rsqrt(jnp.mean(x * x, -1, keepdims=True) + EPS) * w

        def _rope(q, k):
            S, hd = (q.shape[1], q.shape[-1])
            half = hd // 2
            inv = 1.0 / ROPE_BASE ** (jnp.arange(half, dtype=jnp.float32) / half)
            ang = jnp.arange(S, dtype=jnp.float32)[:, None] * inv
            cos = jnp.concatenate([jnp.cos(ang), jnp.cos(ang)], -1)[None, :, None, :]
            sin = jnp.concatenate([jnp.sin(ang), jnp.sin(ang)], -1)[None, :, None, :]

            def rot(t):
                t1, t2 = (t[..., :half], t[..., half:])
                return jnp.concatenate([-t2, t1], -1)
            return (q * cos + rot(q) * sin, k * cos + rot(k) * sin)
        key = jax.random.key(seed)
        ks = jax.random.split(key, 12)
        B, S, D, H, E = (1, 128, 256, 256, 16)
        s = 0.02
        return {'x': jax.random.normal(ks[0], (B, S, D), jnp.float32), 'ln_w': jnp.ones((D,), jnp.float32), 'ff_ln_w': jnp.ones((D,), jnp.float32), 'wq': jax.random.normal(ks[1], (D, NHEADS * HEAD_DIM), jnp.float32) * s, 'wk': jax.random.normal(ks[2], (D, KVHEADS * HEAD_DIM), jnp.float32) * s, 'wv': jax.random.normal(ks[3], (D, KVHEADS * HEAD_DIM), jnp.float32) * s, 'wo': jax.random.normal(ks[4], (NHEADS * HEAD_DIM, D), jnp.float32) * s, 'wg': jax.random.normal(ks[5], (D, E), jnp.float32) * s, 'w1': jax.random.normal(ks[6], (E, D, H), jnp.float32) * s, 'w3': jax.random.normal(ks[7], (E, D, H), jnp.float32) * s, 'w2': jax.random.normal(ks[8], (E, H, D), jnp.float32) * s}
    _L0_ffn_in = _L0_ffn_setup()

    def _L1_attn_setup():
        import jax, jax.numpy as jnp
        import numpy as np
        DIMS = 256
        HEAD = 16
        HD = DIMS // HEAD
        HD2 = HD // 2
        B, C = (1, 256)

        def layernorm(x, g, b, eps=1e-05):
            mu = x.mean(-1, keepdims=True)
            var = x.var(-1, keepdims=True)
            return (x - mu) / jnp.sqrt(var + eps) * g + b

        def rotary_freqs():
            f = (8000.0 / 200.0) ** jnp.linspace(0.0, 1.0, HD2) * 200.0 / 1000.0
            return 200.0 * f / 1000.0

        def apply_rotary(y, xa):
            t = jnp.arange(y.shape[2], dtype=jnp.float32)
            ang = jnp.einsum('i,j->ij', t, rotary_freqs())
            m = jnp.linalg.norm(xa, axis=-1)
            rr = (m[..., None] * jnp.cos(ang))[:, None]
            ri = (m[..., None] * jnp.sin(ang))[:, None]
            yp = y.reshape(*y.shape[:-1], HD2, 2)
            yr, yi = (yp[..., 0], yp[..., 1])
            out_r = yr * rr - yi * ri
            out_i = yr * ri + yi * rr
            return jnp.stack([out_r, out_i], axis=-1).reshape(y.shape)
        key = jax.random.key(seed)
        ks = jax.random.split(key, 4)
        s = 0.02
        return {'x': jax.random.normal(ks[0], (B, C, DIMS), jnp.float32), 'ln_q_g': jnp.ones((DIMS,), jnp.float32), 'ln_q_b': jnp.zeros((DIMS,), jnp.float32), 'Wq': jax.random.normal(ks[1], (DIMS, DIMS), jnp.float32) * s, 'bq': jnp.zeros((DIMS,), jnp.float32), 'ln_kv_g': jnp.ones((DIMS,), jnp.float32), 'ln_kv_b': jnp.zeros((DIMS,), jnp.float32), 'Wkv': jax.random.normal(ks[2], (DIMS, 2 * DIMS), jnp.float32) * s, 'bkv': jnp.zeros((2 * DIMS,), jnp.float32), 'ln_h_g': jnp.ones((HD,), jnp.float32), 'ln_h_b': jnp.zeros((HD,), jnp.float32), 'Wo': jax.random.normal(ks[3], (DIMS, DIMS), jnp.float32) * s, 'bo': jnp.zeros((DIMS,), jnp.float32)}
    _L1_attn_in = _L1_attn_setup()

    def _L1_ffn_setup():
        import jax, jax.numpy as jnp
        import numpy as np
        H = 256
        I = 176
        E = 16
        TOP_K = 4
        N_GROUP = 4
        TOPK_GROUP = 2
        SCALE = 16.0
        N_SHARED = 2
        SI = I * N_SHARED
        B, S = (1, 256)

        def _silu_and_mul(gu):
            g, u = jnp.split(gu, 2, axis=-1)
            return jax.nn.silu(g) * u
        key = jax.random.key(seed)
        ks = jax.random.split(key, 6)
        inv_h = 1.0 / np.sqrt(H)
        inv_i = 1.0 / np.sqrt(I)
        inv_si = 1.0 / np.sqrt(SI)
        return {'hidden_states': jax.random.normal(ks[0], (B, S, H), jnp.float32), 'gate_w': jax.random.normal(ks[1], (E, H), jnp.float32) * inv_h, 'w_gate_up': jax.random.normal(ks[2], (E, H, 2 * I), jnp.float32) * inv_h, 'w_down': jax.random.normal(ks[3], (E, I, H), jnp.float32) * inv_i, 'shared_gate_up': jax.random.normal(ks[4], (H, 2 * SI), jnp.float32) * inv_h, 'shared_down': jax.random.normal(ks[5], (SI, H), jnp.float32) * inv_si}
    _L1_ffn_in = _L1_ffn_setup()
    _d = {'L0_attn_x': _L0_attn_in['x'], 'L0_attn_w_qkv': _L0_attn_in['w_qkv'], 'L0_attn_w_o': _L0_attn_in['w_o'], 'L0_ffn_ln_w': _L0_ffn_in['ln_w'], 'L0_ffn_ff_ln_w': _L0_ffn_in['ff_ln_w'], 'L0_ffn_wq': _L0_ffn_in['wq'], 'L0_ffn_wk': _L0_ffn_in['wk'], 'L0_ffn_wv': _L0_ffn_in['wv'], 'L0_ffn_wo': _L0_ffn_in['wo'], 'L0_ffn_wg': _L0_ffn_in['wg'], 'L0_ffn_w1': _L0_ffn_in['w1'], 'L0_ffn_w3': _L0_ffn_in['w3'], 'L0_ffn_w2': _L0_ffn_in['w2'], 'L1_attn_ln_q_g': _L1_attn_in['ln_q_g'], 'L1_attn_ln_q_b': _L1_attn_in['ln_q_b'], 'L1_attn_Wq': _L1_attn_in['Wq'], 'L1_attn_bq': _L1_attn_in['bq'], 'L1_attn_ln_kv_g': _L1_attn_in['ln_kv_g'], 'L1_attn_ln_kv_b': _L1_attn_in['ln_kv_b'], 'L1_attn_Wkv': _L1_attn_in['Wkv'], 'L1_attn_bkv': _L1_attn_in['bkv'], 'L1_attn_ln_h_g': _L1_attn_in['ln_h_g'], 'L1_attn_ln_h_b': _L1_attn_in['ln_h_b'], 'L1_attn_Wo': _L1_attn_in['Wo'], 'L1_attn_bo': _L1_attn_in['bo'], 'L1_ffn_gate_w': _L1_ffn_in['gate_w'], 'L1_ffn_w_gate_up': _L1_ffn_in['w_gate_up'], 'L1_ffn_w_down': _L1_ffn_in['w_down'], 'L1_ffn_shared_gate_up': _L1_ffn_in['shared_gate_up'], 'L1_ffn_shared_down': _L1_ffn_in['shared_down']}
    _x0 = _d['L0_attn_x']
    _d['L0_attn_x'] = jax.random.normal(jax.random.fold_in(jax.random.key(seed), 1), (4, 512, 256), dtype=_x0.dtype)
    del _x0
    return _d

def reference(L0_attn_x, L0_attn_w_qkv, L0_attn_w_o, L0_ffn_ln_w, L0_ffn_ff_ln_w, L0_ffn_wq, L0_ffn_wk, L0_ffn_wv, L0_ffn_wo, L0_ffn_wg, L0_ffn_w1, L0_ffn_w3, L0_ffn_w2, L1_attn_ln_q_g, L1_attn_ln_q_b, L1_attn_Wq, L1_attn_bq, L1_attn_ln_kv_g, L1_attn_ln_kv_b, L1_attn_Wkv, L1_attn_bkv, L1_attn_ln_h_g, L1_attn_ln_h_b, L1_attn_Wo, L1_attn_bo, L1_ffn_gate_w, L1_ffn_w_gate_up, L1_ffn_w_down, L1_ffn_shared_gate_up, L1_ffn_shared_down):

    def _L0_attn_ref(x, w_qkv, w_o):
        import jax, jax.numpy as jnp
        import numpy as np
        D_MODEL = 256
        N_HEADS = 16
        HEAD_DIM = 128
        WINDOW = 64
        ROPE_BASE = 10000.0
        B, N = (2, 256)
        INNER = N_HEADS * HEAD_DIM

        def _rotate_half(t):
            t1, t2 = jnp.split(t, 2, axis=-1)
            return jnp.concatenate([-t2, t1], axis=-1)

        def _rope(q, k, offset=0):
            D = q.shape[-1]
            inv_freq = 1.0 / ROPE_BASE ** (jnp.arange(0, D, 2, dtype=jnp.float32) / D)
            pos = jnp.arange(q.shape[2], dtype=jnp.float32) + offset
            ang = pos[:, None] * inv_freq[None, :]
            cos = jnp.concatenate([jnp.cos(ang), jnp.cos(ang)], axis=-1)
            sin = jnp.concatenate([jnp.sin(ang), jnp.sin(ang)], axis=-1)
            q_r = q * cos + _rotate_half(q) * sin
            k_r = k * cos + _rotate_half(k) * sin
            return (q_r, k_r)
        Bq, Nq, _ = x.shape
        qkv = jnp.einsum('bnd,ed->bne', x, w_qkv)
        q, k, v = jnp.split(qkv, 3, axis=-1)

        def to_heads(t):
            return t.reshape(Bq, Nq, N_HEADS, HEAD_DIM).transpose(0, 2, 1, 3)
        q, k, v = (to_heads(q), to_heads(k), to_heads(v))
        q, k = _rope(q, k, offset=0)
        i = jnp.arange(Nq)[:, None]
        j = jnp.arange(Nq)[None, :]
        valid = (j > i - WINDOW) & (j <= i)
        scale = 1.0 / np.sqrt(HEAD_DIM)
        scores = jnp.einsum('bhnd,bhkd->bhnk', q, k) * scale
        scores = jnp.where(valid[None, None], scores, -jnp.inf)
        att = jax.nn.softmax(scores, axis=-1)
        out = jnp.einsum('bhnk,bhkd->bhnd', att, v)
        out = out.transpose(0, 2, 1, 3).reshape(Bq, Nq, INNER)
        y = jnp.einsum('bni,di->bnd', out, w_o)
        return y

    def _L0_ffn_ref(x, ln_w, ff_ln_w, wq, wk, wv, wo, wg, w1, w3, w2):
        import jax, jax.numpy as jnp
        import numpy as np
        EPS = 1e-05
        ROPE_BASE = 150000.0
        NHEADS = 32
        KVHEADS = 8
        HEAD_DIM = 64
        TOP_K = 4

        def _rms(x, w):
            return x * jax.lax.rsqrt(jnp.mean(x * x, -1, keepdims=True) + EPS) * w

        def _rope(q, k):
            S, hd = (q.shape[1], q.shape[-1])
            half = hd // 2
            inv = 1.0 / ROPE_BASE ** (jnp.arange(half, dtype=jnp.float32) / half)
            ang = jnp.arange(S, dtype=jnp.float32)[:, None] * inv
            cos = jnp.concatenate([jnp.cos(ang), jnp.cos(ang)], -1)[None, :, None, :]
            sin = jnp.concatenate([jnp.sin(ang), jnp.sin(ang)], -1)[None, :, None, :]

            def rot(t):
                t1, t2 = (t[..., :half], t[..., half:])
                return jnp.concatenate([-t2, t1], -1)
            return (q * cos + rot(q) * sin, k * cos + rot(k) * sin)
        B, S, D = x.shape
        h = _rms(x, ln_w)
        q = (h @ wq).reshape(B, S, NHEADS, HEAD_DIM)
        k = (h @ wk).reshape(B, S, KVHEADS, HEAD_DIM)
        v = (h @ wv).reshape(B, S, KVHEADS, HEAD_DIM)
        q, k = _rope(q, k)
        g = NHEADS // KVHEADS
        k = jnp.repeat(k, g, axis=2)
        v = jnp.repeat(v, g, axis=2)
        scores = jnp.einsum('bqhd,bkhd->bhqk', q, k) / np.float32(np.sqrt(HEAD_DIM))
        causal = jnp.tril(jnp.ones((S, S), bool))
        scores = jnp.where(causal[None, None], scores, jnp.float32(-1e+30))
        attn = jax.nn.softmax(scores, -1)
        o = jnp.einsum('bhqk,bkhd->bqhd', attn, v).reshape(B, S, NHEADS * HEAD_DIM)
        x = x + o @ wo
        h = _rms(x, ff_ln_w)
        logits = h @ wg
        topv, topi = jax.lax.top_k(logits, TOP_K)
        gate = jax.nn.softmax(topv, -1)
        bidx = jnp.arange(B)[:, None, None]
        sidx = jnp.arange(S)[None, :, None]
        weights = jnp.zeros_like(logits).at[bidx, sidx, topi].set(gate)
        a = jax.nn.silu(jnp.einsum('bsd,edh->bseh', h, w1)) * jnp.einsum('bsd,edh->bseh', h, w3)
        y = jnp.einsum('bseh,ehd->bsed', a, w2)
        moe = jnp.einsum('bsed,bse->bsd', y, weights)
        return x + moe

    def _L1_attn_ref(x, ln_q_g, ln_q_b, Wq, bq, ln_kv_g, ln_kv_b, Wkv, bkv, ln_h_g, ln_h_b, Wo, bo):
        import jax, jax.numpy as jnp
        import numpy as np
        DIMS = 256
        HEAD = 16
        HD = DIMS // HEAD
        HD2 = HD // 2
        B, C = (1, 256)

        def layernorm(x, g, b, eps=1e-05):
            mu = x.mean(-1, keepdims=True)
            var = x.var(-1, keepdims=True)
            return (x - mu) / jnp.sqrt(var + eps) * g + b

        def rotary_freqs():
            f = (8000.0 / 200.0) ** jnp.linspace(0.0, 1.0, HD2) * 200.0 / 1000.0
            return 200.0 * f / 1000.0

        def apply_rotary(y, xa):
            t = jnp.arange(y.shape[2], dtype=jnp.float32)
            ang = jnp.einsum('i,j->ij', t, rotary_freqs())
            m = jnp.linalg.norm(xa, axis=-1)
            rr = (m[..., None] * jnp.cos(ang))[:, None]
            ri = (m[..., None] * jnp.sin(ang))[:, None]
            yp = y.reshape(*y.shape[:-1], HD2, 2)
            yr, yi = (yp[..., 0], yp[..., 1])
            out_r = yr * rr - yi * ri
            out_i = yr * ri + yi * rr
            return jnp.stack([out_r, out_i], axis=-1).reshape(y.shape)
        b, c, d = x.shape
        q = (layernorm(x, ln_q_g, ln_q_b) @ Wq + bq).reshape(b, c, HEAD, HD).transpose(0, 2, 1, 3)
        kv = (layernorm(x, ln_kv_g, ln_kv_b) @ Wkv + bkv).reshape(b, c, 2, HEAD, HD)
        k = kv[:, :, 0].transpose(0, 2, 1, 3)
        v = kv[:, :, 1].transpose(0, 2, 1, 3)
        scale = HD ** (-0.25)
        q = q * scale
        k = k * scale
        q = apply_rotary(q, x)
        k = apply_rotary(k, x)
        qn = layernorm(q, ln_h_g, ln_h_b)
        kn = layernorm(k, ln_h_g, ln_h_b)
        logits = jnp.einsum('bhqd,bhkd->bhqk', qn, kn) / jnp.sqrt(jnp.float32(HD))
        att = jax.nn.softmax(logits, axis=-1)
        a = jnp.einsum('bhqk,bhkd->bhqd', att, v)
        a = a.transpose(0, 2, 1, 3).reshape(b, c, d)
        return a @ Wo + bo

    def _L1_ffn_ref(hidden_states, gate_w, w_gate_up, w_down, shared_gate_up, shared_down):
        import jax, jax.numpy as jnp
        import numpy as np
        H = 256
        I = 176
        E = 16
        TOP_K = 4
        N_GROUP = 4
        TOPK_GROUP = 2
        SCALE = 16.0
        N_SHARED = 2
        SI = I * N_SHARED
        B, S = (1, 256)

        def _silu_and_mul(gu):
            g, u = jnp.split(gu, 2, axis=-1)
            return jax.nn.silu(g) * u
        b, s, h = hidden_states.shape
        x = hidden_states.reshape(-1, h)
        T = x.shape[0]
        logits = x @ gate_w.T
        grouped = logits.reshape(T, N_GROUP, E // N_GROUP)
        group_scores = grouped.max(axis=-1)
        _, group_idx = jax.lax.top_k(group_scores, TOPK_GROUP)
        rows = jnp.arange(T)[:, None]
        keep = jnp.zeros((T, N_GROUP), bool).at[rows, group_idx].set(True)
        grouped = jnp.where(keep[..., None], grouped, 0.0)
        logits = grouped.reshape(T, E)
        probs = jax.nn.softmax(logits, axis=-1)
        topk_w, topk_ids = jax.lax.top_k(probs, TOP_K)
        topk_w = topk_w * SCALE
        combine = jnp.zeros((T, E), x.dtype).at[rows, topk_ids].add(topk_w)

        def step(acc, ws):
            wgu, wd, c = ws
            y = _silu_and_mul(x @ wgu) @ wd
            return (acc + c[:, None] * y, None)
        out, _ = jax.lax.scan(step, jnp.zeros_like(x), (w_gate_up, w_down, combine.T))
        out = out + _silu_and_mul(x @ shared_gate_up) @ shared_down
        return out.reshape(b, s, h)
    x = L0_attn_x
    x = x + _layernorm(_L0_attn_ref(_layernorm(x, axis=-1), L0_attn_w_qkv, L0_attn_w_o), axis=-1)
    x = x + _layernorm(_L0_ffn_ref(_layernorm(x, axis=-1), L0_ffn_ln_w, L0_ffn_ff_ln_w, L0_ffn_wq, L0_ffn_wk, L0_ffn_wv, L0_ffn_wo, L0_ffn_wg, L0_ffn_w1, L0_ffn_w3, L0_ffn_w2), axis=-1)
    x = x + _layernorm(_L1_attn_ref(_layernorm(x, axis=-1), L1_attn_ln_q_g, L1_attn_ln_q_b, L1_attn_Wq, L1_attn_bq, L1_attn_ln_kv_g, L1_attn_ln_kv_b, L1_attn_Wkv, L1_attn_bkv, L1_attn_ln_h_g, L1_attn_ln_h_b, L1_attn_Wo, L1_attn_bo), axis=-1)
    x = x + _layernorm(_L1_ffn_ref(_layernorm(x, axis=-1), L1_ffn_gate_w, L1_ffn_w_gate_up, L1_ffn_w_down, L1_ffn_shared_gate_up, L1_ffn_shared_down), axis=-1)
    return x

_drawn_inputs = setup_inputs


def setup_inputs(seed=0):
    import zlib

    import numpy as np

    out = dict(_drawn_inputs(seed))
    spreads = {'L0_ffn_ln_w': (1.0, 0.6),
     'L0_ffn_ff_ln_w': (1.0, 0.6),
     'L1_attn_ln_q_g': (1.0, 0.6),
     'L1_attn_ln_q_b': (0.0, 0.572),
     'L1_attn_bq': (0.0, 0.291),
     'L1_attn_ln_kv_g': (1.0, 0.2),
     'L1_attn_ln_kv_b': (0.0, 0.1),
     'L1_attn_bkv': (0.0, 0.1),
     'L1_attn_ln_h_g': (1.0, 0.2),
     'L1_attn_ln_h_b': (0.0, 0.346),
     'L1_attn_bo': (0.0, 0.1)}
    factors = {'L0_ffn_wq': 5.382,
     'L0_ffn_wk': 7.851,
     'L0_ffn_wg': 3.715,
     'L0_ffn_w1': 3.697,
     'L0_ffn_w3': 4.07,
     'L0_ffn_w2': 3.479}
    for name, (base, spread) in spreads.items():
        noise = np.random.default_rng([zlib.crc32(name.encode()), seed]).standard_normal(out[name].shape)
        drawn = base * np.exp(spread * noise) if base else spread * noise
        out[name] = jnp.asarray(drawn.astype(out[name].dtype))
    for name, factor in factors.items():
        out[name] = (out[name] * factor).astype(out[name].dtype)
    return out
```

```python
import numpy as np
from contextlib import ExitStack
import concourse.bass as bass
from concourse import mybir

F32 = mybir.dt.float32
F32R = mybir.dt.float32r
ALU = mybir.AluOpType
ACT = mybir.ActivationFunctionType
AX = mybir.AxisListType
ds = bass.ds

P = 128
BATCH, SEQ, DIM = 4, 512, 256
TOKENS = BATCH * SEQ
TILES = TOKENS // P
TB = SEQ // P
KD = DIM // P
EPS = 1e-5

A_HEADS, A_HD, WINDOW = 16, 128, 64
A_SPAN = P + WINDOW
A_SCALE = float(1.0 / np.sqrt(A_HD))
NEG = -1e30

EXPERTS, SHARED = 16, 2
M0_HIDDEN, M1_HIDDEN = 256, 176


class Chain:

    def __init__(self, eng, sem):
        self.eng, self.sem, self.n, self.base = eng, sem, 0, 0

    def add(self, ins):
        ins.then_inc(self.sem, 1)
        self.n += 1
        return self.n + self.base

    def wait(self, mark=None):
        self.eng.wait_ge(self.sem, self.n + self.base if mark is None else mark)


class Core:

    def __init__(self, nc, ctx):
        self.nc, self.ctx, self.sems = nc, ctx, []
        self.tick = self.sb("tick", [P, 2])

    def sb(self, name, shape, dt=F32):
        return self.ctx.enter_context(self.nc.sbuf_tensor(name, shape, dt))

    def sem(self, name):
        self.sems.append(self.nc.alloc_semaphore(name=name))
        return self.sems[-1]

    def free_semaphores(self):
        self.nc.clear_and_free_semaphores(self.sems)
        self.nc.all_engine_barrier()
        self.sems = []


def attention0(nc, c, w_dram, wo_dram):
    PAIRS = A_HEADS // 2
    U = 2 * BATCH
    with ExitStack() as st:
        def sb(name, shape, dt=F32):
            return st.enter_context(nc.sbuf_tensor(name, shape, dt))

        def pb(name, shape, dt=F32):
            return st.enter_context(nc.psum_tensor(name, shape, dt))
        sem = c.sem
        w = sb("a_w", [P, 2, KD, 3, P])
        wo = sb("a_wo", [P, 2, DIM])
        q_r = sb("a_q", [P, 2, SEQ])
        k_r = sb("a_k", [P, 2, SEQ])
        v_s = sb("a_v", [P, 2, TB, A_HD])
        prod = sb("a_prod", [P, 4, SEQ])
        s_m = sb("a_s", [P, TB, A_SPAN])
        s_p = sb("a_p", [P, TB, A_SPAN])
        mx = sb("a_mx", [P, TB])
        nmx = sb("a_nmx", [P, TB])
        den = sb("a_den", [P, TB])
        rden = sb("a_rden", [P, TB])
        pt = sb("a_pt", [P, TB, A_SPAN])
        ot = sb("a_ot", [P, 2, TOKENS])
        p_q, p_k, p_v = pb("p_q", [P, SEQ]), pb("p_k", [P, SEQ]), pb("p_v", [P, SEQ])
        p_s = pb("p_s", [P, 2, SEQ])
        p_t, p_t2 = pb("p_t", [P, SEQ]), pb("p_t2", [P, SEQ])
        p_o = pb("p_o", [P, SEQ])
        scores = p_s[:, :, 0:2 * A_SPAN].rearrange("p a (b n) -> p a b n", b=2)
        yps = p_s[:, :, :].rearrange("p a (b n) -> p a b n", b=2)

        s_w = [sem("a_s_w_even"), sem("a_s_w_odd")]
        s_wo = sem("a_s_wo")
        s_proj = sem("a_s_proj")
        s_rope = sem("a_s_rope")
        s_prod = sem("a_s_prod")
        s_v = sem("a_s_v")
        s_sc = sem("a_s_sc")
        s_mx = sem("a_s_mx")
        s_exp = sem("a_s_exp")
        s_rd = sem("a_s_rd")
        s_pn = sem("a_s_pn")
        s_tr = sem("a_s_tr")
        s_pto = sem("a_s_pto")
        s_ptn = sem("a_s_ptn")
        s_ov = sem("a_s_ov")
        s_ot = sem("a_s_ot")
        s_y = sem("a_s_y")
        s_ya = sem("a_s_ya")
        s_z = sem("a_s_z")
        s_d = sem("a_s_d")

        with nc.Block() as block:
            @block.sync
            def _(sp):
                def load_w(h, slot):
                    sp.dma_start(w[:, slot, :, :, :], w_dram[ds(h, 1)].rearrange("o p k j n -> (o p) k j n")).then_inc(s_w[slot], 16)

                def load_wo(h):
                    sp.dma_start(wo[:, :, :], wo_dram[ds(h, 2)].rearrange("o p n -> p o n")).then_inc(s_wo, 16)
                load_w(0, 0)
                load_w(1, 1)
                load_wo(0)
                with sp.Fori(1, PAIRS) as i:
                    sp.wait_ge(s_proj, i * (3 * U) - 3 * BATCH)
                    load_w(i * 2, 0)
                    sp.wait_ge(s_proj, i * (3 * U))
                    load_w(i * 2 + 1, 1)
                    sp.wait_ge(s_y, i * BATCH)
                    load_wo(i * 2)

            def passes(eng, before, body):
                before()
                with eng.Fori(0, PAIRS - 1) as i:
                    body(i, False)
                body(PAIRS - 1, True)

            @block.tensor
            def _(pe):
                def project(i, u):
                    n = i * U + u
                    slot, b = (u % U) // BATCH, u % BATCH
                    pe.wait_ge(s_w[slot], i * 16 + (32 if u == U else 16))
                    first = isinstance(i, int) and i == 0 and u == 0
                    for j, bank in enumerate((p_q, p_k)):
                        if not first:
                            pe.wait_ge(s_prod, 2 * n - 1 + j)
                        for k in range(KD):
                            mm = pe.matmul(bank[:, :], w[:, slot, k, j, :], c.HT[:, k, b * SEQ:(b + 1) * SEQ],
                                           start=(k == 0), stop=(k == KD - 1))
                        mm.then_inc(s_proj, 1)
                    if not first:
                        pe.wait_ge(s_v, n)
                    for t in range(TB):
                        for k in range(KD):
                            mm = pe.matmul(p_v[:, t * P:(t + 1) * P], c.HT[:, k, b * SEQ + t * P:b * SEQ + (t + 1) * P],
                                           w[:, slot, k, 2, :], start=(k == 0), stop=(k == KD - 1))
                    mm.then_inc(s_proj, 1)

                def body(i, last):
                    for u in range(U):
                        n = i * U + u
                        h = n % 2 if isinstance(n, int) else u % 2
                        slot, b = u // BATCH, u % BATCH
                        pe.wait_ge(s_rope, 2 * n + 2)
                        pe.wait_ge(s_mx, n)
                        pe.wait_ge(s_ya, i * BATCH + max(u - BATCH - 1, 0))
                        for t in range(TB):
                            lo = WINDOW if t == 0 else 0
                            mm = pe.matmul(scores[:, t // 2, t % 2, lo:A_SPAN], q_r[:, u % 2, t * P:(t + 1) * P],
                                           k_r[:, u % 2, t * P - WINDOW + lo:(t + 1) * P], start=True, stop=True)
                        mm.then_inc(s_sc, 1)
                        if not (last and u == U - 1):
                            project(i, u + 1)
                        pe.wait_ge(s_pn, n + 1)
                        pe.wait_ge(s_pto, n)
                        pe.wait_ge(s_ptn, n)
                        for t in range(TB):
                            pe.transpose(p_t[:, t * P:(t + 1) * P], s_p[:, t, WINDOW:A_SPAN], c.ident[:, :])
                        for t in range(1, TB):
                            mm = pe.transpose(p_t2[0:WINDOW, t * P:(t + 1) * P], s_p[:, t, 0:WINDOW], c.ident[:, :])
                        mm.then_inc(s_tr, 1)
                        if slot == 1 and b > 0:
                            out_proj(i, b - 1)
                        pe.wait_ge(s_v, n + 1)
                        pe.wait_ge(s_ot, n)
                        pe.wait_ge(s_pto, n + 1)
                        pe.wait_ge(s_ptn, n + 1)
                        for t in range(TB):
                            width = P if t == TB - 1 else A_SPAN
                            mm = pe.matmul(p_o[:, t * P:t * P + width], v_s[:, u % 2, t, :], pt[:, t, 0:width],
                                           start=(t == 0), stop=(t == TB - 1), skip_group_check=True)
                        mm.then_inc(s_ov, 1)
                    out_proj(i, BATCH - 1)

                def out_proj(i, b):
                    m = i * BATCH + b
                    pe.wait_ge(s_ya, m)
                    pe.wait_ge(s_wo, i * 16 + 16)
                    pe.wait_ge(s_ot, i * U + BATCH + b + 1)
                    pe.wait_ge(s_mx, i * U + BATCH + b + 1)
                    for t in range(TB):
                        for slot in range(2):
                            tok = b * SEQ + t * P
                            mm = pe.matmul(yps[:, t // 2, t % 2, :], ot[:, slot, tok:tok + P], wo[:, slot, :],
                                           start=(slot == 0), stop=(slot == 1))
                    mm.then_inc(s_y, 1)

                passes(pe, lambda: project(0, 0), body)

            @block.scalar
            def _(act):
                def copy_v(n, u):
                    act.wait_ge(s_proj, 3 * n + 3)
                    act.activation(v_s[:, u % 2, :, :].rearrange("p t n -> p (t n)"), p_v[:, :], ACT.Copy).then_inc(s_v, 1)

                def body(i, last):
                    for u in range(U):
                        n = i * U + u
                        act.wait_ge(s_mx, n + 1)
                        act.wait_ge(s_pn, n)
                        for t in range(TB):
                            lo = WINDOW if t == 0 else 0
                            x = act.activation(s_m[:, t, lo:], s_m[:, t, lo:], ACT.Exp, bias=nmx[:, t:t + 1],
                                               scale=A_SCALE, accum_out=den[:, t:t + 1])
                        x.then_inc(s_exp, 1)
                        if not (last and u == U - 1):
                            copy_v(n + 1, u + 1)
                        act.wait_ge(s_tr, n + 1)
                        act.wait_ge(s_ov, n)
                        act.activation(pt[:, :, 0:P], p_t[:, :].rearrange("p (t n) -> p t n", t=TB), ACT.Copy).then_inc(s_pto, 1)
                        act.wait_ge(s_ov, n + 1)
                        if u == 0:
                            act.wait_ge(s_y, i * BATCH)
                        act.activation(ot[:, u // BATCH, (u % BATCH) * SEQ:(u % BATCH + 1) * SEQ], p_o[:, :], ACT.Copy).then_inc(s_ot, 1)

                passes(act, lambda: copy_v(0, 0), body)

            @block.vector
            def _(dve):
                def rope(n, u):
                    for j, bank in enumerate((p_q, p_k)):
                        dve.wait_ge(s_proj, 3 * n + 1 + j)
                        if not (isinstance(n, int) and n == 0):
                            dve.wait_ge(s_rope, 2 * n - 1 + j)
                        dve.tensor_tensor(prod[:, 2 * j, :], bank[:, :], c.cosA[:, :], ALU.mult)
                        H = P // 2
                        dve.tensor_tensor(prod[0:H, 2 * j + 1, :], bank[H:P, :], c.sinA[H:P, :], ALU.mult)
                        dve.tensor_tensor(prod[H:P, 2 * j + 1, :], bank[0:H, :], c.sinA[0:H, :], ALU.mult).then_inc(s_prod, 1)

                def body(i, last):
                    for u in range(U):
                        n = i * U + u
                        slot, b = u // BATCH, u % BATCH
                        dve.wait_ge(s_sc, n + 1)
                        dve.wait_ge(s_exp, n)
                        dve.wait_ge(s_pn, n)
                        dve.memset(c.tick[:, :], 0.0)
                        for t in range(TB):
                            lo = WINDOW if t == 0 else 0
                            x = dve.tensor_tensor_reduce(s_m[:, t, lo:], scores[:, t // 2, t % 2, lo:], c.maskA[:, lo:], 1.0,
                                                         3 * NEG, ALU.add, ALU.max, mx[:, t:t + 1])
                        x.then_inc(s_d, 1)
                        dve.wait_ge(s_d, n + 1)
                        dve.tensor_scalar(nmx[:, :], mx[:, :], -A_SCALE, None, ALU.mult).then_inc(s_mx, 1)
                        if not (last and u == U - 1):
                            rope(n + 1, u + 1)
                        dve.wait_ge(s_exp, n + 1)
                        dve.wait_ge(s_pn, n)
                        dve.reciprocal(rden[:, :], den[:, :]).then_inc(s_rd, 1)
                        dve.wait_ge(s_tr, n + 1)
                        dve.wait_ge(s_ov, n)
                        dve.tensor_copy(pt[WINDOW:P, 0:TB - 1, P:A_SPAN],
                                        p_t2[0:WINDOW, P:].rearrange("p (t n) -> p t n", t=TB - 1)[:, :, 0:WINDOW]).then_inc(s_ptn, 1)
                        if slot == 1 and b > 0:
                            add_y(i, b - 1)
                    add_y(i, BATCH - 1)

                def add_y(i, b):
                    m = i * BATCH + b
                    dve.wait_ge(s_y, m + 1)
                    y = c.Y[:, b * TB:(b + 1) * TB, :].rearrange("p (a b) n -> p a (b n)", a=2)
                    for a in range(2):
                        x = dve.tensor_tensor(y[:, a, :], p_s[:, a, :], y[:, a, :], ALU.add)
                    x.then_inc(s_ya, 1)

                def before():
                    dve.memset(c.Y[:, :, :], 0.0)
                    dve.memset(s_m[:, 0, 0:WINDOW], 0.0)
                    dve.memset(pt[0:WINDOW, :, P:A_SPAN], 0.0).then_inc(s_z, 1)
                    dve.wait_ge(s_z, 1)
                    rope(0, 0)
                passes(dve, before, body)

            @block.gpsimd
            def _(pool):
                def rope(n, u):
                    for j, dst in enumerate((q_r, k_r)):
                        pool.wait_ge(s_prod, 2 * n + 1 + j)
                        if not (isinstance(n, int) and n == 0):
                            pool.wait_ge(s_sc, n - 1)
                        pool.tensor_tensor(dst[:, u % 2, :], prod[:, 2 * j, :], prod[:, 2 * j + 1, :], ALU.add).then_inc(s_rope, 1)

                def body(i, last):
                    for u in range(U):
                        n = i * U + u
                        if not (last and u == U - 1):
                            rope(n + 1, u + 1)
                        pool.wait_ge(s_z, 1)
                        pool.wait_ge(s_rd, n + 1)
                        pool.wait_ge(s_tr, n)
                        pool.tensor_tensor(s_p[:, :, :], s_m[:, :, :],
                                           rden[:, :].rearrange("p (t o) -> p t o", o=1).to_broadcast([P, TB, A_SPAN]),
                                           ALU.mult).then_inc(s_pn, 1)
                passes(pool, lambda: rope(0, 0), body)


GROUPS = TILES // TB


def skewed(steps):
    for at in range(GROUPS + max(steps)):
        for level in sorted(steps):
            if 0 <= at - level < GROUPS:
                steps[level](at - level)


def norm_stage(nc, c, name, x_dram=None, add=None, residual=True, post=None, outs=(), out_dram=None):
    with ExitStack() as st:
        def sb(n, shape, dt=F32):
            return st.enter_context(nc.sbuf_tensor(f"{name}_{n}", shape, dt))

        def sem(n):
            return c.sem(f"{name}_{n}")
        rows = sb("rows", [P, GROUPS, TB, DIM]) if post else None
        scratch = sb("scratch", [P, 2, DIM])
        sty, stx, stn = sb("sty", [P, TILES, 6]), sb("stx", [P, TILES, 6]), sb("stn", [P, TILES, 6])
        mvy, mvx, mvn = sb("mvy", [P, TILES, 2]), sb("mvx", [P, TILES, 2]), sb("mvn", [P, TILES, 2])
        sdy, sdx, sdn = sb("sdy", [P, TILES]), sb("sdx", [P, TILES]), sb("sdn", [P, TILES])
        rsy, rsx, rsn = sb("rsy", [P, TILES]), sb("rsx", [P, TILES]), sb("rsn", [P, TILES])
        p_t = [st.enter_context(nc.psum_tensor(f"{name}_pt{i}", [P, SEQ], F32)) for i in range(4)]

        final = out_dram is not None
        has_y = residual and x_dram is None
        has_xn = residual and not final
        split = any(isinstance(o[0], tuple) for o in outs)

        def sems(used, *names):
            return [sem(n) if used else None for n in names]
        s_ld, = sems(x_dram is not None, "loaded")
        s_add, = sems(add is not None, "added")
        s_sty, s_mvy, s_sdy, s_rsy, s_yn, s_x = sems(has_y, "stat_y", "mean_y", "std_y", "rstd_y", "y_norm", "x_sum")
        s_stx, s_mvx, s_sdx, s_rsx, s_xn = sems(has_xn, "stat_x", "mean_x", "std_x", "rstd_x", "x_norm")
        s_scr, s_sdn, s_rsn, s_rows = sems(post is not None, "squares", "std_n", "rstd_n", "rows")
        s_sq, s_stn, s_mvn = sems(post == "ln", "norm_of_x", "stat_n", "mean_n")
        s_tr, s_ht = sems(not final, "transposed", "copied")
        s_hi, = sems(split, "high_part")
        s_out, = sems(final, "stored")

        def tiles(g):
            return range(g * TB, (g + 1) * TB)

        def src_rows(t):
            return rows[:, t // TB, t % TB, :] if post else c.XN[:, t, :]

        with nc.Block() as block:
            @block.sync
            def _(sp):
                if x_dram is not None:
                    for g in range(GROUPS):
                        sp.dma_start(c.X[:, g * TB:(g + 1) * TB, :],
                                     x_dram[g].rearrange("(t p) d -> p t d", p=P)).then_inc(s_ld, 16)
                        sp.wait_ge(s_ld, 16 * (g + 1))
                if final:
                    for g in range(GROUPS):
                        sp.wait_ge(s_x, g + 1)
                        sp.dma_start(out_dram[g].rearrange("(t p) d -> p t d", p=P),
                                     c.X[:, g * TB:(g + 1) * TB, :]).then_inc(s_out, 16)
                    sp.wait_ge(s_out, 16 * GROUPS)

            @block.vector
            def _(dve):
                def stats(src, st_, done, ready, unit=1):
                    def do(g):
                        if ready is not None:
                            dve.wait_ge(ready, unit * (g + 1))
                        for t in tiles(g):
                            x = dve.bn_stats(st_[:, t, :], src[:, t, :])
                        x.then_inc(done, 1)
                    return do

                def mean(st_, stated, mv, done):
                    def do(g):
                        dve.wait_ge(stated, g + 1)
                        for t in tiles(g):
                            x = dve.bn_aggr(mv[:, t, :], st_[:, t, :])
                        x.then_inc(done, 1)
                    return do

                def inverse(sd, ready, rs, done):
                    def do(g):
                        dve.wait_ge(ready, g + 1)
                        dve.reciprocal(rs[:, g * TB:(g + 1) * TB], sd[:, g * TB:(g + 1) * TB]).then_inc(done, 1)
                    return do

                def scaled(src, mv, rs, ready, dst, done):
                    def do(g):
                        dve.wait_ge(ready, g + 1)
                        for t in tiles(g):
                            x = dve.tensor_scalar(dst(t), src[:, t, :], mv[:, t, 0:1], rs[:, t:t + 1],
                                                  ALU.subtract, ALU.mult)
                        x.then_inc(done, 1)
                    return do

                def copy_out(g):
                    dve.wait_ge(s_tr, g + 1)
                    for dst, scale, shift in outs:
                        if isinstance(dst, tuple):
                            dve.wait_ge(s_hi, g + 1)
                            hi, lo = dst
                            for k in range(KD):
                                x = dve.scalar_tensor_tensor(lo[:, k, g * SEQ:(g + 1) * SEQ], p_t[2 * (g % 2) + k][:, :],
                                                             1.0 if scale is None else scale[:, k:k + 1],
                                                             hi[:, k, g * SEQ:(g + 1) * SEQ].bitcast(F32),
                                                             ALU.mult, ALU.subtract)
                            continue
                        for k in range(KD):
                            to, src = dst[:, k, g * SEQ:(g + 1) * SEQ], p_t[2 * (g % 2) + k][:, :]
                            if scale is None:
                                x = dve.tensor_copy(to, src)
                            elif shift is None:
                                x = dve.tensor_scalar(to, src, scale[:, k:k + 1], None, ALU.mult)
                            else:
                                x = dve.tensor_scalar(to, src, scale[:, k:k + 1], shift[:, k:k + 1], ALU.mult, ALU.add)
                    x.then_inc(s_ht, 1)

                steps = {}
                y_ready = s_add if add == "y" else None
                if has_y:
                    steps[0] = stats(c.Y, sty, s_sty, y_ready)
                    steps[1] = mean(sty, s_sty, mvy, s_mvy)
                    steps[3] = inverse(sdy, s_sdy, rsy, s_rsy)
                    steps[4] = scaled(c.Y, mvy, rsy, s_rsy, lambda t: c.Y[:, t, :], s_yn)
                if has_xn:
                    steps[6] = stats(c.X, stx, s_stx, s_x if has_y else s_ld, 1 if has_y else 16)
                    steps[7] = mean(stx, s_stx, mvx, s_mvx)
                    steps[9] = inverse(sdx, s_sdx, rsx, s_rsx)
                    steps[10] = scaled(c.X, mvx, rsx, s_rsx, lambda t: c.XN[:, t, :], s_xn)
                if post == "rms":
                    steps[14] = inverse(sdn, s_sdn, rsn, s_rsn)
                if post == "ln":
                    steps[11] = stats(c.XN, stn, s_stn, s_xn)
                    steps[12] = mean(stn, s_stn, mvn, s_mvn)
                    steps[14] = inverse(sdn, s_sdn, rsn, s_rsn)
                    steps[15] = scaled(c.XN, mvn, rsn, s_rsn, src_rows, s_rows)
                if not final:
                    steps[16] = copy_out
                skewed(steps)

            @block.gpsimd
            def _(pool):
                def grp(b, g):
                    return b[:, g * TB:(g + 1) * TB, :]
                for g in range(GROUPS):
                    if add == "y":
                        pool.tensor_tensor(grp(c.Y, g), grp(c.Y, g), grp(c.XN, g), ALU.add).then_inc(s_add, 1)
                    if add == "xn":
                        pool.tensor_tensor(grp(c.XN, g), grp(c.XN, g), grp(c.Y, g), ALU.add).then_inc(s_add, 1)
                if has_y:
                    for g in range(GROUPS):
                        pool.wait_ge(s_yn, g + 1)
                        pool.tensor_tensor(grp(c.X, g), grp(c.X, g), grp(c.Y, g), ALU.add).then_inc(s_x, 1)

            @block.scalar
            def _(act):
                def root(mv, ready, sd, done):
                    def do(g):
                        act.wait_ge(ready, g + 1)
                        a, b = g * TB, (g + 1) * TB
                        act.activation(sd[:, a:b], mv[:, a:b, 1], ACT.Sqrt, bias=c.eps[:, :]).then_inc(done, 1)
                    return do

                def squares(g):
                    if add == "xn" or residual:
                        act.wait_ge(s_add if add == "xn" else s_xn, g + 1)
                    for t in tiles(g):
                        if t >= 2:
                            act.wait_ge(s_scr, t - 1)
                        act.activation(scratch[:, t % 2, :], c.XN[:, t, :], ACT.Square,
                                       accum_out=mvn[:, t, 0:1] if post == "rms" else c.NORM2[:, t:t + 1]).then_inc(s_scr, 1)

                def rms(g):
                    act.wait_ge(s_scr, TB * (g + 1))
                    a, b = g * TB, (g + 1) * TB
                    act.activation(sdn[:, a:b], mvn[:, a:b, 0], ACT.Sqrt, bias=c.eps[:, :],
                                   scale=1.0 / DIM).then_inc(s_sdn, 1)

                def rms_rows(g):
                    act.wait_ge(s_rsn, g + 1)
                    for t in tiles(g):
                        x = act.activation(src_rows(t), c.XN[:, t, :], ACT.Copy, scale=rsn[:, t:t + 1])
                    x.then_inc(s_rows, 1)

                def norm(g):
                    act.wait_ge(s_scr, TB * (g + 1))
                    a, b = g * TB, (g + 1) * TB
                    act.activation(c.NORM[:, a:b], c.NORM2[:, a:b], ACT.Sqrt).then_inc(s_sq, 1)

                def high_part(g):
                    for dst, scale, shift in outs:
                        if isinstance(dst, tuple):
                            act.wait_ge(s_tr, g + 1)
                            for k in range(KD):
                                x = act.activation(dst[0][:, k, g * SEQ:(g + 1) * SEQ], p_t[2 * (g % 2) + k][:, :],
                                                   ACT.Copy, scale=1.0 if scale is None else scale[:, k:k + 1])
                            x.then_inc(s_hi, 1)

                steps = {}
                if split:
                    steps[16] = high_part
                if has_y:
                    steps[2] = root(mvy, s_mvy, sdy, s_sdy)
                if has_xn:
                    steps[8] = root(mvx, s_mvx, sdx, s_sdx)
                if post == "rms":
                    steps[11], steps[12], steps[15] = squares, rms, rms_rows
                if post == "ln":
                    steps[11], steps[12] = squares, norm
                    steps[13] = root(mvn, s_mvn, sdn, s_sdn)
                skewed(steps)

            if not final:
                @block.tensor
                def _(pe):
                    for g in range(GROUPS):
                        pe.wait_ge(s_rows if post else s_xn, g + 1)
                        if g >= 2:
                            pe.wait_ge(s_ht, g - 1)
                        for k in range(KD):
                            for t in tiles(g):
                                x = pe.transpose(p_t[2 * (g % 2) + k][:, (t % TB) * P:(t % TB + 1) * P],
                                                 src_rows(t)[:, k * P:(k + 1) * P], c.ident[:, :])
                        x.then_inc(s_tr, 1)


B_HEADS, B_KV, B_HD = 32, 8, 64
B_PAIRS = B_KV // 2
B_REP = B_HEADS // B_KV
B_UNITS = B_PAIRS * B_REP


def attention1(nc, c, w_dram, wo_dram, cos_dram, sin_dram):
    ITEMS = 2 * TB
    LAG = 4
    RING = 6
    TOTAL = B_UNITS * ITEMS
    LOADS = {}
    for t in range(TB):
        LOADS["v", t] = t
    n = TB
    for m in range(B_UNITS):
        if m % B_REP == 0:
            LOADS["k", m // B_REP] = n
            n += 1
        LOADS["q", m] = n
        n += 1
    NPROJ = n
    NROPE = NPROJ - TB
    with ExitStack() as st:
        def sb(name, shape, dt=F32):
            return st.enter_context(nc.sbuf_tensor("b_" + name, shape, dt))

        def pb(name):
            return st.enter_context(nc.psum_tensor("b_" + name, [P, SEQ], F32))

        def sem(name):
            return c.sem("b_" + name)
        w = sb("w", [P, KD, B_PAIRS, 2 + B_REP, P])
        wo = sb("wo", [P, B_UNITS, DIM])
        cos, sin = sb("cos", [P, SEQ]), sb("sin", [P, SEQ])
        mask = c.maskB
        h = sb("h", [P, KD, SEQ])
        v_s = sb("v", [P, TB, B_PAIRS * P])
        k_r = sb("k_rot", [P, SEQ])
        kp = sb("k", [P, 2, 2, SEQ])
        q_r = sb("q", [P, 2, SEQ])
        prod = sb("prod", [P, 2, SEQ])
        sm = sb("sm", [P, RING, SEQ])
        mn, den, rden = sb("mn", [P, RING]), sb("den", [P, RING]), sb("rden", [P, RING])
        pt = sb("pt", [P, 2, 2, TB, SEQ])
        ot_halves = (c.Y[:, :, :].rearrange("p (m a) d -> p m (a d)", a=2), sb("ot", [P, B_UNITS // 2, SEQ]))
        p_proj, p_s, p_t = [pb("pj0"), pb("pj1")], [pb("s0"), pb("s1")], [pb("t0"), pb("t1")]
        p_o, p_y = pb("o"), pb("y")

        s_w, s_z, s_h = sem("weights"), sem("zeros"), sem("h_copied")
        s_proj, s_prod, s_rope, s_kp = sem("projected"), sem("read"), sem("rotated"), sem("k_padded")
        s_sc, s_mn, s_exp, s_rd, s_pn = sem("scores"), sem("minimum"), sem("exp"), sem("inverse"), sem("normalised")
        s_tr, s_pa, s_pd = sem("transposed"), sem("pt_by_act"), sem("pt_by_dve")
        s_ov, s_ot, s_y, s_xn = sem("pv"), sem("ot_copied"), sem("out_proj"), sem("added")

        def ot(m, cols):
            return ot_halves[m // (B_UNITS // 2)][:, m % (B_UNITS // 2), cols]

        def item(g):
            return g // ITEMS, g % 2, g % ITEMS // 2

        def keys(t):
            return (t + 1) * P

        with nc.Block() as block:
            @block.sync
            def _(sp):
                sp.dma_start(w[:, :, :, :, :], w_dram).then_inc(s_w, 16)
                sp.dma_start(cos[:, :], cos_dram).then_inc(s_w, 16)
                sp.dma_start(sin[:, :], sin_dram).then_inc(s_w, 16)
                sp.dma_start(wo[:, :, :], wo_dram).then_inc(s_w, 16)
                sp.wait_ge(s_w, 64)

            @block.tensor
            def _(pe):
                def project(b, kind, m):
                    at = LOADS[kind, m]
                    bank = p_proj[at % 2]
                    pe.wait_ge(s_prod, b * NPROJ + (at - 1 if at > 0 else 0))
                    for k in range(KD):
                        if kind == "v":
                            x = pe.matmul(bank[:, :], h[:, k, m * P:(m + 1) * P], w[:, k, :, 1, :],
                                          start=(k == 0), stop=(k == KD - 1))
                        else:
                            pair, j = (m, 0) if kind == "k" else (m // B_REP, 2 + m % B_REP)
                            x = pe.matmul(bank[:, :], w[:, k, pair, j, :], h[:, k, :], start=(k == 0), stop=(k == KD - 1))
                    x.then_inc(s_proj, 1)

                def scores(b, g):
                    m, head, t = item(g)
                    if g % (B_REP * ITEMS) == 0:
                        pe.wait_ge(s_kp, b * B_PAIRS + m // B_REP + 1)
                    if g % ITEMS == 0:
                        pe.wait_ge(s_rope, b * NROPE + LOADS["q", m] - TB + 1)
                    if g >= 2:
                        pe.wait_ge(s_mn, b * TOTAL + g - 1)
                    pe.matmul(p_s[g % 2][:, 0:keys(t)], q_r[:, m % 2, t * P:(t + 1) * P],
                              kp[:, m // B_REP % 2, head, 0:keys(t)], start=True, stop=True).then_inc(s_sc, 1)

                def transposes(b, g):
                    m, head, t = item(g)
                    pe.wait_ge(s_pn, b * TOTAL + g + 1)
                    if g >= 2:
                        pe.wait_ge(s_pd if head else s_pa, b * (TOTAL // 2) + g // 2)
                    for k in range(t + 1):
                        x = pe.transpose(p_t[g % 2][:, k * P:(k + 1) * P], sm[:, g % RING, k * P:(k + 1) * P], c.ident[:, :])
                    x.then_inc(s_tr, 1)

                def values(b, m):
                    pe.wait_ge(s_pa, b * (TOTAL // 2) + (m + 1) * TB)
                    pe.wait_ge(s_pd, b * (TOTAL // 2) + (m + 1) * TB)
                    pe.wait_ge(s_ot, b * B_UNITS + m)
                    pair = m // B_REP
                    for k in range(TB):
                        for head in range(2):
                            r = head * B_HD
                            x = pe.matmul(p_o[r:r + B_HD, k * P:SEQ], v_s[:, k, pair * P + r:pair * P + r + B_HD],
                                          pt[:, m % 2, head, k, k * P:SEQ], start=(k == 0), stop=(k == TB - 1))
                    x.then_inc(s_ov, 1)

                pe.wait_ge(s_w, 64)
                pe.wait_ge(s_z, 1)
                with pe.Fori(0, BATCH) as b:
                    pe.wait_ge(s_h, b + 1)
                    for t in range(TB):
                        project(b, "v", t)
                    project(b, "k", 0)
                    project(b, "q", 0)
                    for g in range(TOTAL + LAG):
                        m, n = g // ITEMS, g % ITEMS
                        if g < TOTAL:
                            scores(b, g)
                            if n == 1 and m + 1 < B_UNITS:
                                if (m + 1) % B_REP == 0:
                                    project(b, "k", (m + 1) // B_REP)
                                project(b, "q", m + 1)
                        if g >= LAG:
                            transposes(b, g - LAG)
                        if n == LAG + 1 and 0 < m:
                            values(b, m - 1)
                    values(b, B_UNITS - 1)
                    pe.wait_ge(s_ot, b * B_UNITS + B_UNITS)
                    for t in range(TB):
                        pe.wait_ge(s_xn, b * TB + t)
                        for m in range(B_UNITS):
                            x = pe.matmul(p_y[:, 0:DIM], ot(m, slice(t * P, (t + 1) * P)), wo[:, m, :],
                                          start=(m == 0), stop=(m == B_UNITS - 1))
                        x.then_inc(s_y, 1)

            @block.scalar
            def _(act):
                def pad(b, i):
                    act.wait_ge(s_rope, b * NROPE + LOADS["k", i] - TB + 1)
                    if i >= 2:
                        act.wait_ge(s_sc, b * TOTAL + (i - 1) * B_REP * ITEMS)
                    for head in range(2):
                        x = act.activation(kp[:, i % 2, head, :], k_r[:, :], ACT.Copy, scale=c.rowsB[:, head:head + 1])
                    x.then_inc(s_kp, 1)

                def copy_out(b, m):
                    act.wait_ge(s_ov, b * B_UNITS + m + 1)
                    act.activation(ot(m, slice(0, SEQ)), p_o[:, :], ACT.Copy).then_inc(s_ot, 1)

                with act.Fori(0, BATCH) as b:
                    act.wait_ge(s_y, b * TB)
                    x = act.activation(h[:, :, :], c.HT[:, :, ds(b * SEQ, SEQ)], ACT.Copy).then_inc(s_h, 1)
                    pad(b, 0)
                    for g in range(TOTAL + LAG):
                        if g < TOTAL:
                            if g % (B_REP * ITEMS) == (B_REP - 1) * ITEMS + 3 and g // (B_REP * ITEMS) + 1 < B_PAIRS:
                                pad(b, g // (B_REP * ITEMS) + 1)
                            _, _, t = item(g)
                            act.wait_ge(s_mn, b * TOTAL + g + 1)
                            act.activation(sm[:, g % RING, 0:keys(t)], sm[:, g % RING, 0:keys(t)], ACT.Exp, scale=-1.0,
                                           bias=mn[:, g % RING:g % RING + 1],
                                           accum_out=den[:, g % RING:g % RING + 1]).then_inc(s_exp, 1)
                        if g >= LAG and item(g - LAG)[1] == 0:
                            m, head, t = item(g - LAG)
                            act.wait_ge(s_tr, b * TOTAL + g - LAG + 1)
                            if m >= 2:
                                act.wait_ge(s_ov, b * B_UNITS + m - 1)
                            act.activation(pt[:, m % 2, 0, 0:t + 1, t * P:(t + 1) * P],
                                           p_t[(g - LAG) % 2][:, 0:keys(t)].rearrange("p (k n) -> p k n", n=P),
                                           ACT.Copy).then_inc(s_pa, 1)
                        if g % ITEMS == LAG + 2 and g > ITEMS:
                            copy_out(b, g // ITEMS - 1)
                    copy_out(b, B_UNITS - 1)

            @block.vector
            def _(dve):
                def read(b, kind, m):
                    at = LOADS[kind, m]
                    bank = p_proj[at % 2]
                    dve.wait_ge(s_proj, b * NPROJ + at + 1)
                    if kind == "v":
                        dve.tensor_copy(v_s[:, m, :], bank[:, :]).then_inc(s_prod, 1)
                        return
                    r = B_HD
                    dve.wait_ge(s_rope, b * NROPE + at - TB)
                    scale = 1.0 if kind == "k" else -1.0 / 8
                    dve.scalar_tensor_tensor(prod[:, 0, :], bank[:, :], scale, cos[:, :], ALU.mult, ALU.mult)
                    dve.scalar_tensor_tensor(prod[0:r, 1, :], bank[r:P, :], scale, sin[r:P, :], ALU.mult, ALU.mult)
                    dve.scalar_tensor_tensor(prod[r:P, 1, :], bank[0:r, :], scale, sin[0:r, :], ALU.mult,
                                             ALU.mult).then_inc(s_prod, 1)

                dve.memset(c.tick[:, :], 0.0).then_inc(s_z, 1)
                dve.wait_ge(s_w, 64)
                dve.wait_ge(s_z, 1)
                with dve.Fori(0, BATCH) as b:
                    for t in range(TB):
                        read(b, "v", t)
                    read(b, "k", 0)
                    read(b, "q", 0)
                    for g in range(TOTAL + LAG):
                        m, n = g // ITEMS, g % ITEMS
                        if g < TOTAL:
                            _, _, t = item(g)
                            if g >= RING:
                                dve.wait_ge(s_tr, b * TOTAL + g - RING + 1)
                            dve.wait_ge(s_sc, b * TOTAL + g + 1)
                            dve.memset(c.tick[:, g % 2:g % 2 + 1], 0.0)
                            dve.tensor_tensor_reduce(sm[:, g % RING, 0:keys(t)], p_s[g % 2][:, 0:keys(t)],
                                                     mask[:, SEQ - keys(t):SEQ], 1.0, -3 * NEG, ALU.add, ALU.min,
                                                     mn[:, g % RING:g % RING + 1]).then_inc(s_mn, 1)
                        if g >= 1 and g <= TOTAL:
                            s = (g - 1) % RING
                            dve.wait_ge(s_exp, b * TOTAL + g)
                            dve.reciprocal(rden[:, s:s + 1], den[:, s:s + 1]).then_inc(s_rd, 1)
                        if n == 2 and m + 1 < B_UNITS:
                            if (m + 1) % B_REP == 0:
                                read(b, "k", (m + 1) // B_REP)
                            read(b, "q", m + 1)
                        if g >= LAG and item(g - LAG)[1] == 1:
                            m2, _, t2 = item(g - LAG)
                            dve.wait_ge(s_tr, b * TOTAL + g - LAG + 1)
                            if m2 >= 2:
                                dve.wait_ge(s_ov, b * B_UNITS + m2 - 1)
                            dve.tensor_copy(pt[:, m2 % 2, 1, 0:t2 + 1, t2 * P:(t2 + 1) * P],
                                            p_t[(g - LAG) % 2][:, 0:keys(t2)].rearrange("p (k n) -> p k n", n=P)).then_inc(s_pd, 1)
                    for t in range(TB):
                        dve.wait_ge(s_y, b * TB + t + 1)
                        row = c.XN[:, ds(b * TB + t, 1), :].rearrange("p o d -> p (o d)")
                        dve.tensor_tensor(row, p_y[:, 0:DIM], row, ALU.add).then_inc(s_xn, 1)

            @block.gpsimd
            def _(pool):
                def add(b, kind, m):
                    at = LOADS[kind, m] - TB
                    pool.wait_ge(s_prod, b * NPROJ + LOADS[kind, m] + 1)
                    if kind == "q":
                        if m >= 2:
                            pool.wait_ge(s_sc, b * TOTAL + (m - 1) * ITEMS)
                        pool.tensor_tensor(q_r[:, m % 2, :], prod[:, 0, :], prod[:, 1, :], ALU.add).then_inc(s_rope, 1)
                    else:
                        pool.wait_ge(s_kp, b * B_PAIRS + m)
                        pool.tensor_tensor(k_r[:, :], prod[:, 0, :], prod[:, 1, :], ALU.add).then_inc(s_rope, 1)
                pool.wait_ge(s_z, 1)
                with pool.Fori(0, BATCH) as b:
                    add(b, "k", 0)
                    add(b, "q", 0)
                    for g in range(TOTAL):
                        m, n = g // ITEMS, g % ITEMS
                        s = g % RING
                        t = item(g)[2]
                        pool.wait_ge(s_rd, b * TOTAL + g + 1)
                        pool.tensor_tensor(sm[:, s, 0:keys(t)], sm[:, s, 0:keys(t)],
                                           rden[:, s:s + 1].to_broadcast([P, keys(t)]), ALU.mult).then_inc(s_pn, 1)
                        if n == 1 and m + 1 < B_UNITS:
                            if (m + 1) % B_REP == 0:
                                add(b, "k", (m + 1) // B_REP)
                            add(b, "q", m + 1)


TOP_K = 4


def moe(nc, c, name, experts, hidden, routed, w13_dram, w2_dram, gate_dram, grouped):
    REST = hidden - P
    packed = REST <= 64
    UP = 64
    WG = 3 * P - (16 if packed else 0) if packed else 4 * P
    PAIRS = experts // 2
    U = 2 * BATCH
    with ExitStack() as st:
        def sb(n, shape, dt=F32):
            return st.enter_context(nc.sbuf_tensor(f"{name}_{n}", shape, dt))

        def pb(n):
            return st.enter_context(nc.psum_tensor(f"{name}_{n}", [P, SEQ], F32))

        def sem(n):
            return c.sem(f"{name}_{n}")
        WCOLS = KD * WG + 2 * DIM
        w_raw = sb("w_raw", [P, 2, WCOLS])
        w_hi, w_lo = sb("w_hi", [P, 2, WCOLS], F32R), sb("w_lo", [P, 2, WCOLS], F32R)
        sg = sb("sg", [P, 2, SEQ])
        a = sb("a", [P, 2, SEQ])
        a_hi, a_lo = sb("a_hi", [P, 2, 2, SEQ], F32R), sb("a_lo", [P, 2, 2, SEQ], F32R)
        NL = TILES * routed
        gw = sb("gw", [P, KD, routed])
        gw_hi, gw_lo = sb("gw_hi", [P, KD, routed], F32R), sb("gw_lo", [P, KD, routed], F32R)
        lg = sb("lg", [P, TILES, routed])
        ex = sb("ex", [P, TILES, routed])
        wt = sb("wt", [P, TILES, experts])
        wt_e = sb("wt_e", [P, 2, TILES])
        cmp_a, cmp_b = sb("cmp_a", [P, TB, routed, routed]), sb("cmp_b", [P, TB, routed, routed])
        rank = sb("rank", [P, TILES, routed])
        top, tsum, tinv = sb("top", [P, TILES]), sb("tsum", [P, TILES]), sb("tinv", [P, TILES])
        NG = 4
        gmax, grank = sb("gmax", [P, TILES, NG]), sb("grank", [P, TILES, NG])
        p_g, p_u = [pb("g0"), pb("g1")], [pb("u0"), pb("u1")]
        p_y = [pb(f"y{i}") for i in range(4)]

        s_w = [sem("w_even"), sem("w_odd")]
        s_whi, s_wlo = sem("w_high"), sem("w_low")
        s_gw, s_gw1, s_lg, s_lgc = sem("gate_w"), sem("gate_split"), sem("logits"), sem("logits_copied")
        s_dl, s_ex, s_rt = sem("shifted"), sem("exps"), sem("route")
        s_d = sem("dve")
        s_gu = sem("gate_up")
        s_sg, s_a = sem("silu"), sem("act_product")
        s_ahi, s_alo = sem("a_high"), sem("a_low")
        s_y, s_ya, s_z, s_we = sem("down"), sem("y_added"), sem("zeros"), sem("weight_column")

        def w13(part, slot, k, m, up):
            if packed and m == 1:
                return part[:, slot, k * WG + 2 * P:k * WG + 2 * P + UP + REST]
            at = k * WG + (2 * m + up) * P
            return part[:, slot, at:at + P]

        def w2(part, slot, m):
            return part[:, slot, KD * WG + m * DIM:KD * WG + (m + 1) * DIM]

        def product(pe, out, pairs):
            terms = [t for (ah, al), (bh, bl) in pairs for t in ((ah, bh), (ah, bl), (al, bh))]
            for n, (x, y) in enumerate(terms):
                mm = pe.matmul(out, x, y, start=(n == 0), stop=(n == len(terms) - 1))
            return mm

        def passes(eng, before, body):
            before()
            with eng.Fori(0, PAIRS - 1) as i:
                body(i, False)
            body(PAIRS - 1, True)

        with nc.Block() as block:
            @block.sync
            def _(sp):
                def load(e, slot):
                    sp.dma_start(w_raw[:, slot, 0:KD * WG], w13_dram[ds(e, 1)].rearrange("o p n -> (o p) n")).then_inc(s_w[slot], 16)
                    if packed:
                        sp.dma_start(w_raw[:, slot, KD * WG:KD * WG + DIM],
                                     w2_dram[ds(e, 1), 0:P].rearrange("o p n -> (o p) n")).then_inc(s_w[slot], 16)
                        sp.dma_start(w_raw[0:REST, slot, KD * WG + DIM:WCOLS],
                                     w2_dram[ds(e, 1), P:hidden].rearrange("o p n -> (o p) n")).then_inc(s_w[slot], 16)
                    else:
                        sp.dma_start(w_raw[:, slot, KD * WG:WCOLS].rearrange("p (m n) -> p m n", m=2),
                                     w2_dram[ds(e, 1)].rearrange("o (m p) n -> (o p) m n", p=P)).then_inc(s_w[slot], 16)
                sp.dma_start(gw[:, :, :], gate_dram).then_inc(s_gw, 16)
                if packed:
                    sp.wait_ge(s_z, 1)
                load(0, 0)
                load(1, 1)
                with sp.Fori(1, PAIRS) as i:
                    sp.wait_ge(s_wlo, i * 2 - 1)
                    load(i * 2, 0)
                    sp.wait_ge(s_wlo, i * 2)
                    load(i * 2 + 1, 1)
                sp.wait_ge(s_gw, 16)
            LOADED = 48 if packed else 32

            @block.tensor
            def _(pe):
                def logits():
                    pe.wait_ge(s_gw1, 2)
                    for t in range(TILES):
                        if t >= 4:
                            pe.wait_ge(s_lgc, t - 3)
                        rep = DIM // routed
                        parts = [[g[:, k, :].rearrange("p (o n) -> p o n", o=1).to_broadcast([P, rep, routed])
                                  for g in (gw_hi, gw_lo)] for k in range(KD)]
                        hts = [[h[:, k, t * P:(t + 1) * P] for h in (c.HT_hi, c.HT_lo)] for k in range(KD)]
                        out = p_y[t % 4][:, 0:DIM].rearrange("p (o n) -> p o n", o=rep)
                        product(pe, out, list(zip(hts, parts))).then_inc(s_lg, 1)

                def gate_up(i, u):
                    n = i * U + u
                    slot, b = (u % U) // BATCH, u % BATCH
                    pe.wait_ge(s_wlo, i * 2 + (u // BATCH) + 1)
                    hts = [[h[:, k, b * SEQ:(b + 1) * SEQ] for h in (c.HT_hi, c.HT_lo)] for k in range(KD)]
                    for m in range(2):
                        if not (isinstance(n, int) and n == 0):
                            pe.wait_ge(s_a, 2 * n - 1 + m)
                        for up, bank in enumerate((p_g[m], p_u[m])):
                            if packed and m == 1:
                                if up == 0:
                                    x = product(pe, bank[0:UP + REST, :],
                                                [([w13(p, slot, k, m, 0) for p in (w_hi, w_lo)], hts[k]) for k in range(KD)])
                                continue
                            x = product(pe, bank[:, :], [([w13(p, slot, k, m, up) for p in (w_hi, w_lo)], hts[k])
                                                         for k in range(KD)])
                        x.then_inc(s_gu, 1)

                def down(i, u):
                    n = i * U + u
                    slot = u // BATCH
                    pe.wait_ge(s_alo, n + 1)
                    pe.wait_ge(s_ya, i * U + max(u - 1, 0))
                    for t in range(TB):
                        al = [[x[:, u % 2, m, t * P:(t + 1) * P] for x in (a_hi, a_lo)] for m in range(2)]
                        x = product(pe, p_y[2 * (u % 2) + t // 2][:, (t % 2) * DIM:(t % 2 + 1) * DIM],
                                    [(al[m], [w2(p, slot, m) for p in (w_hi, w_lo)]) for m in range(2)])
                    x.then_inc(s_y, 1)

                def body(i, last):
                    for u in range(U):
                        if not (last and u == U - 1):
                            gate_up(i, u + 1)
                        down(i, u)

                def before():
                    logits()
                    pe.wait_ge(s_lgc, TILES)
                    gate_up(0, 0)
                passes(pe, before, body)

            @block.scalar
            def _(act):
                def silu(n, u):
                    for m in range(2):
                        act.wait_ge(s_gu, 2 * n + m + 1)
                        if not (isinstance(n, int) and n == 0):
                            act.wait_ge(s_a, 2 * n - 1 + m)
                        rows = REST if packed and m == 1 else P
                        act.activation(sg[0:rows, m, :], p_g[m][0:rows, :], ACT.Silu).then_inc(s_sg, 1)

                def a_high(i, n, u):
                    act.wait_ge(s_a, 2 * n + 2)
                    act.wait_ge(s_y, i * U + max(u - 1, 0))
                    act.activation(a_hi[:, u % 2, :, :], a[:, :, :], ACT.Copy).then_inc(s_ahi, 1)

                def body(i, last):
                    for u in range(U):
                        n = i * U + u
                        a_high(i, n, u)
                        if not (last and u == U - 1):
                            silu(n + 1, u + 1)
                        if not last and u in (BATCH, U - 1):
                            slot = 0 if u == BATCH else 1
                            act.wait_ge(s_w[slot], i * LOADED + 2 * LOADED)
                            act.wait_ge(s_y, i * U + (BATCH if slot == 0 else U))
                            act.activation(w_hi[:, slot, :], w_raw[:, slot, :], ACT.Copy).then_inc(s_whi, 1)

                def before():
                    act.wait_ge(s_gw, 16)
                    act.activation(gw_hi[:, :, :], gw[:, :, :], ACT.Copy).then_inc(s_gw1, 1)
                    for e in range(2):
                        act.wait_ge(s_w[e], LOADED)
                        act.activation(w_hi[:, e, :], w_raw[:, e, :], ACT.Copy).then_inc(s_whi, 1)
                    act.wait_ge(s_dl, 1)
                    act.activation(ex[:, :, :], ex[:, :, :], ACT.Exp).then_inc(s_ex, 1)
                    silu(0, 0)
                passes(act, before, body)

            @block.gpsimd
            def _(pool):
                def low(e, slot):
                    pool.wait_ge(s_whi, e + 1)
                    pool.tensor_tensor(w_lo[:, slot, :], w_raw[:, slot, :], w_hi[:, slot, :].bitcast(F32),
                                       ALU.subtract).then_inc(s_wlo, 1)

                def a_low(i, u):
                    n = i * U + u
                    pool.wait_ge(s_ahi, n + 1)
                    pool.tensor_tensor(a_lo[:, u % 2, :, :], a[:, :, :], a_hi[:, u % 2, :, :].bitcast(F32),
                                       ALU.subtract).then_inc(s_alo, 1)

                def body(i, last):
                    for u in range(U):
                        a_low(i, u)
                        if not last and u in (BATCH, U - 1):
                            low(i * 2 + 2 + (0 if u == BATCH else 1), 0 if u == BATCH else 1)

                def before():
                    pool.wait_ge(s_gw1, 1)
                    pool.tensor_tensor(gw_lo[:, :, :], gw[:, :, :], gw_hi[:, :, :].bitcast(F32),
                                       ALU.subtract).then_inc(s_gw1, 1)
                    low(0, 0)
                    low(1, 1)
                passes(pool, before, body)

            @block.vector
            def _(dve):
                chain = Chain(dve, s_d)

                def link(ins):
                    chain.add(ins)
                    chain.wait()

                def bc(x, shape):
                    return x.to_broadcast(shape)

                def ranks(values, count, out):
                    for g in range(GROUPS):
                        ts = slice(g * TB, (g + 1) * TB)
                        A = cmp_a[:, :, 0:count, 0:count]
                        B = cmp_b[:, :, 0:count, 0:count]
                        vj = values[:, ts, :].rearrange("p t (o j) -> p t o j", o=1).to_broadcast([P, TB, count, count])
                        vi = values[:, ts, :].rearrange("p t (i o) -> p t i o", o=1).to_broadcast([P, TB, count, count])
                        link(dve.tensor_tensor(A, vj, vi, ALU.is_gt))
                        link(dve.tensor_tensor(B, vj, vi, ALU.is_equal))
                        for t in range(TB):
                            x = dve.tensor_tensor(cmp_b[:, t, 0:count, 0:count], cmp_b[:, t, 0:count, 0:count],
                                                  c.before[:, 0:count, 0:count], ALU.mult)
                        link(x)
                        link(dve.tensor_tensor(A, A, B, ALU.add))
                        link(dve.tensor_reduce(out[:, ts, :], A, AX.X, ALU.add))

                def column(x):
                    return x[:, :].rearrange("p (t o) -> p t o", o=1)

                def route():
                    for t in range(TILES):
                        dve.wait_ge(s_lg, t + 1)
                        dve.tensor_copy(lg[:, t, :], p_y[t % 4][:, 0:routed]).then_inc(s_lgc, 1)
                    dve.wait_ge(s_lgc, TILES)
                    full = [P, TILES, routed]
                    if grouped:
                        grp = lg[:, :, :].rearrange("p t (g n) -> p t g n", g=NG)
                        link(dve.tensor_reduce(gmax[:, :, :], grp, AX.X, ALU.max))
                        ranks(gmax, NG, grank)
                        link(dve.tensor_scalar(grank[:, :, :], grank[:, :, :], 2.0, None, ALU.is_lt))
                        for g in range(NG):
                            n = routed // NG
                            x = dve.tensor_tensor(lg[:, :, g * n:(g + 1) * n], lg[:, :, g * n:(g + 1) * n],
                                                  grank[:, :, g:g + 1].to_broadcast([P, TILES, n]), ALU.mult)
                        link(x)
                    link(dve.tensor_reduce(top[:, :], lg[:, :, :], AX.X, ALU.max))
                    dve.tensor_tensor(ex[:, :, :], lg[:, :, :], column(top).to_broadcast(full), ALU.subtract).then_inc(s_dl, 1)
                    ranks(lg, routed, rank)
                    link(dve.tensor_scalar(rank[:, :, :], rank[:, :, :], float(TOP_K), None, ALU.is_lt))
                    dve.wait_ge(s_ex, 1)
                    sel = wt[:, :, 0:routed]
                    link(dve.tensor_tensor(sel, ex[:, :, :], rank[:, :, :], ALU.mult))
                    link(dve.tensor_reduce(tsum[:, :], ex[:, :, :] if grouped else sel, AX.X, ALU.add))
                    link(dve.reciprocal(tinv[:, :], tsum[:, :]))
                    if grouped:
                        link(dve.tensor_scalar(tinv[:, :], tinv[:, :], 16.0, None, ALU.mult))
                    link(dve.tensor_tensor(sel, sel, column(tinv).to_broadcast(full), ALU.mult))

                def product_a(n):
                    for m in range(2):
                        dve.wait_ge(s_sg, 2 * n + m + 1)
                        if not (isinstance(n, int) and n == 0):
                            dve.wait_ge(s_alo, n)
                        if packed and m == 1:
                            x = dve.tensor_tensor(a[0:REST, m, :], sg[0:REST, m, :], p_g[m][UP:UP + REST, :], ALU.mult)
                        else:
                            x = dve.tensor_tensor(a[:, m, :], sg[:, m, :], p_u[m][:, :], ALU.mult)
                        x.then_inc(s_a, 1)

                def add_y(i, u):
                    n = i * U + u
                    slot, b = u // BATCH, u % BATCH
                    if b == 0:
                        dve.wait_ge(s_ya, n)
                        e = i * 2 + slot
                        dve.tensor_copy(column_of(slot), wt[:, :, ds(e, 1)]).then_inc(s_we, 1)
                        dve.wait_ge(s_we, e + 1)
                    dve.wait_ge(s_y, n + 1)
                    for t in range(TB):
                        tt = b * TB + t
                        x = dve.scalar_tensor_tensor(c.Y[:, tt, :], p_y[2 * (u % 2) + t // 2][:, (t % 2) * DIM:(t % 2 + 1) * DIM],
                                                     wt_e[:, slot, tt:tt + 1], c.Y[:, tt, :], ALU.mult, ALU.add)
                    x.then_inc(s_ya, 1)

                def column_of(slot):
                    return wt_e[:, slot, :].rearrange("p (t o) -> p t o", o=1)

                def body(i, last):
                    for u in range(U):
                        if not (last and u == U - 1):
                            product_a(i * U + u + 1)
                        add_y(i, u)

                def before():
                    if packed:
                        dve.memset(w_raw[:, :, :], 0.0)
                        dve.memset(a[:, :, :], 0.0)
                        dve.memset(wt[:, :, :], 1.0)
                    dve.memset(c.Y[:, :, :], 0.0).then_inc(s_z, 1)
                    dve.wait_ge(s_z, 1)
                    route()
                    product_a(0)
                passes(dve, before, body)


C_HEADS, C_HD = 16, 16
C_SLOT = 64
C_PAIRS = C_HEADS // 2


def attention2(nc, c, wq_dram, wkv_dram, wo_dram, bias_dram, bo_dram, gain_dram, cos_dram, sin_dram):
    W2 = 2 * DIM
    NH = 2 * C_HEADS
    HALF = C_HD // 2
    N1 = TB * C_HEADS
    N2 = C_HEADS * TB
    LAG = 2
    RING = 6
    with ExitStack() as st:
        def sb(name, shape, dt=F32):
            return st.enter_context(nc.sbuf_tensor("c_" + name, shape, dt))

        def sem(name):
            return c.sem("c_" + name)
        bank = [st.enter_context(nc.psum_tensor(f"c_bank{i}", [P, SEQ], F32)) for i in range(8)]
        wq, wkv, wo = sb("wq", [P, KD, DIM]), sb("wkv", [P, KD, W2]), sb("wo", [P, KD, DIM])
        bias, bo = sb("bias", [P, 3 * DIM]), sb("bo", [P, DIM])
        gain = sb("gain", [P, 2, C_HD])
        gq = sb("gq", [P, 2, 2, C_HD])
        cos, sin = sb("cos", [P, TB, HALF]), sb("sin", [P, TB, HALF])
        mcos, msin, mneg = sb("mcos", [P, TB, HALF]), sb("msin", [P, TB, HALF]), sb("mneg", [P, TB, HALF])
        hq, hkv = sb("hq", [P, KD, SEQ]), sb("hkv", [P, KD, SEQ])
        qk = sb("qk", [P, TB, W2])
        pa, pb_ = sb("pa", [P, W2]), sb("pb", [P, W2])
        sq = sb("sq", [P, W2])
        hsum, ssq, std, rstd = (sb(n, [P, TB, NH]) for n in ("hsum", "ssq", "std", "rstd"))
        stack_q = c.XN[:, :, :].rearrange("p (t a) (h n) -> p t (a h) n", t=TB, n=C_SLOT)
        stack_k = sb("stack_k", [P, 2, C_HEADS, C_SLOT])
        qt = sb("qt", [P, C_PAIRS, SEQ], F32R)
        kp = sb("kp", [P, C_HEADS, SEQ], F32R)
        v_s = sb("v", [P, TB, C_HEADS, 2 * C_HD])
        nm = sb("nm", [P, TB, C_HEADS])
        pt = sb("pt", [P, RING, SEQ])
        o_s = sb("o", [P, 4, SEQ])
        a_t, a_f = sb("a_t", [P, 2, DIM]), sb("a_f", [P, 2, KD, P])
        rden = sb("rden", [P, TB, C_HEADS])

        s_w, s_z, s_g, s_h = sem("weights"), sem("zeros"), sem("gains"), sem("h_copied")
        s_p, s_z0 = sem("pool"), sem("first_zeros")
        s_tab, s_proj, s_qk, s_ab, s_r, s_sum = (sem(n) for n in ("tables", "proj", "qk", "products", "rotated", "sum"))
        s_cen, s_sq, s_ssq, s_std, s_rs = (sem(n) for n in ("centred", "square", "square_sum", "std", "rstd"))
        s_n, s_hi, s_lo = sem("normed"), sem("high"), sem("low")
        s_tr, s_qe, s_ke = sem("stack_transposed"), sem("q_copied"), sem("k_copied")
        s_s1, s_nm, s_nh, s_nl = sem("scores"), sem("max"), sem("max_high"), sem("max_low")
        s_tr2, s_q2 = sem("q_transposed"), sem("q2_copied")
        s_s2, s_ex, s_pv, s_oe = sem("scores_t"), sem("exp"), sem("pv"), sem("o_copied")
        s_to, s_rd, s_at, s_ta, s_af, s_y, s_ye = (sem(n) for n in ("o_turned", "inverse", "divided", "a_turned",
                                                                    "a_copied", "out", "out_copied"))

        def pair(x, t, j):
            return x[:, t, 2 * j:2 * j + 2, :].rearrange("p h n -> p (h n)")

        def tiles_of(do):
            for at in range(TB + max(l for l, _ in do)):
                for level, f in do:
                    if 0 <= at - level < TB:
                        f(at - level)

        nc.disable_value_cache = True
        with nc.Block() as block:
            @block.sync
            def _(sp):
                for dst, src in ((wq[:, :, :], wq_dram), (wkv[:, :, :], wkv_dram), (wo[:, :, :], wo_dram),
                                 (bias[:, :], bias_dram.to_broadcast([P, 3 * DIM])),
                                 (bo[:, :], bo_dram.to_broadcast([P, DIM])),
                                 (gain[:, :, :].rearrange("p a n -> p (a n)"), gain_dram.to_broadcast([P, 2 * C_HD])),
                                 (cos[:, :, :], cos_dram), (sin[:, :, :], sin_dram)):
                    sp.dma_start(dst, src).then_inc(s_w, 16)
                sp.wait_ge(s_w, 128)

            @block.tensor
            def _(pe):
                def prep(b):
                    def proj(t):
                        n = b * TB + t
                        pe.wait_ge(s_qk, n)
                        for k in range(KD):
                            pe.matmul(bank[0][:, 0:DIM], hq[:, k, t * P:(t + 1) * P], wq[:, k, :],
                                      start=(k == 0), stop=(k == KD - 1))
                        for k in range(KD):
                            x = pe.matmul(bank[1][:, :], hkv[:, k, t * P:(t + 1) * P], wkv[:, k, :],
                                          start=(k == 0), stop=(k == KD - 1))
                        x.then_inc(s_proj, 1)

                    def turn(t):
                        n = b * TB + t
                        pe.wait_ge(s_lo, n + 1)
                        pe.wait_ge(s_qe, n)
                        pe.wait_ge(s_ke, n)
                        for stack, at, to in ((stack_q, t, 2), (stack_k, t % 2, 4)):
                            for j in range(C_PAIRS):
                                x = pe.transpose(bank[to + j // 4][:, (j % 4) * P:(j % 4 + 1) * P],
                                                 pair(stack, at, j), c.ident[:, :])
                        x.then_inc(s_tr, 1)
                    pe.wait_ge(s_h, b + 1)
                    pe.wait_ge(s_ye, b * TB)
                    tiles_of([(0, proj), (9, turn)])

                def first(b):
                    pe.wait_ge(s_qe, b * TB + TB)
                    pe.wait_ge(s_ke, b * TB + TB)
                    for g in range(N1):
                        t, h = g // C_HEADS, g % C_HEADS
                        if g >= 4:
                            pe.wait_ge(s_nm, b * N1 + g - 3)
                        pe.matmul(bank[2 + g % 4][:, :], qt[:, h // 2, t * P:(t + 1) * P], kp[:, h, :],
                                  start=True, stop=True).then_inc(s_s1, 1)
                    pe.wait_ge(s_oe, b * 4)
                    for t in range(TB):
                        pe.wait_ge(s_nl, b * TB + t + 1)
                        pe.wait_ge(s_q2, b * TB + t)
                        for j in range(C_PAIRS):
                            x = pe.transpose(bank[6 + j // 4][:, (j % 4) * P:(j % 4 + 1) * P],
                                             pair(stack_q, t, j), c.ident[:, :])
                        x.then_inc(s_tr2, 1)

                def second(b):
                    pe.wait_ge(s_q2, b * TB + TB)
                    pe.wait_ge(s_nm, b * N1 + N1)
                    for g in range(N2 + LAG):
                        if g < N2:
                            h, k = g // 16 * 4 + g % 4, g // 4 % 4
                            if g >= 4:
                                pe.wait_ge(s_ex, b * N2 + g - 3)
                            pe.matmul(bank[2 + g % 4][:, :], kp[:, h, k * P:(k + 1) * P], qt[:, h // 2, :],
                                      start=True, stop=True).then_inc(s_s2, 1)
                        if g >= LAG:
                            m = g - LAG
                            grp, k, h = m // 16, m // 4 % 4, m % 4
                            pe.wait_ge(s_ex, b * N2 + m + 1)
                            if m % 16 == 0 and grp >= 2:
                                pe.wait_ge(s_oe, b * 4 + grp - 1)
                            pe.matmul(bank[6 + grp % 2][32 * h:32 * h + 32, :], v_s[:, k, 4 * grp + h, :], pt[:, m % RING, :],
                                      start=(k == 0), stop=(k == TB - 1)).then_inc(s_pv, 1)

                def finish(b):
                    pe.wait_ge(s_oe, b * 4 + 4)
                    for t in range(TB):
                        n = b * TB + t
                        pe.wait_ge(s_at, n)
                        for grp in range(4):
                            x = pe.transpose(bank[0][:, grp * P:(grp + 1) * P], o_s[:, grp, t * P:(t + 1) * P], c.ident[:, :])
                        x.then_inc(s_to, 1)
                        pe.wait_ge(s_at, n + 1)
                        pe.wait_ge(s_ye, n)
                        for k in range(KD):
                            x = pe.transpose(bank[1][:, k * P:(k + 1) * P], a_t[:, t % 2, k * P:(k + 1) * P], c.ident[:, :])
                        x.then_inc(s_ta, 1)
                        pe.wait_ge(s_af, n + 1)
                        for k in range(KD):
                            x = pe.matmul(bank[1][:, DIM:2 * DIM], a_f[:, t % 2, k, :], wo[:, k, :],
                                          start=(k == 0), stop=(k == KD - 1))
                        x.then_inc(s_y, 1)

                pe.wait_ge(s_w, 128)
                pe.wait_ge(s_z, 1)
                with pe.Fori(0, BATCH) as b:
                    prep(b)
                    first(b)
                    second(b)
                    finish(b)

            @block.scalar
            def _(act):
                def prep(b):
                    def square(t):
                        n = b * TB + t
                        act.wait_ge(s_cen, n + 1)
                        act.wait_ge(s_ssq, n)
                        act.activation(sq[:, :], qk[:, t, :], ACT.Square).then_inc(s_sq, 1)

                    def root(t):
                        act.wait_ge(s_ssq, b * TB + t + 1)
                        act.activation(std[:, t, :], ssq[:, t, :], ACT.Sqrt, bias=c.eps[:, :],
                                       scale=1.0 / C_HD).then_inc(s_std, 1)

                    def high(t):
                        n = b * TB + t
                        act.wait_ge(s_n, n + 1)
                        if t >= 2:
                            act.wait_ge(s_tr, n - 1)
                        for i, (stack, at) in enumerate(((stack_q, t), (stack_k, t % 2))):
                            src = qk[:, t, i * DIM:(i + 1) * DIM].rearrange("p (h n) -> p h n", n=C_HD)
                            for place in ((0, 1) if i == 0 else (0, 2)):
                                x = act.activation(stack[:, at, :, place * C_HD:(place + 1) * C_HD].bitcast(F32R), src, ACT.Copy)
                        x.then_inc(s_hi, 1)

                    def k_out(t):
                        n = b * TB + t
                        act.wait_ge(s_tr, n + 1)
                        for j in range(2):
                            src = bank[4 + j][:, :].rearrange("p (a n) -> p a n", n=P)
                            for half in range(2):
                                rows = slice(64 * half, 64 * half + 64)
                                x = act.activation(kp[rows, 8 * j + half:8 * j + 8:2, t * P:(t + 1) * P], src[rows, :, :], ACT.Copy)
                        x.then_inc(s_ke, 1)
                    tiles_of([(10, k_out), (3, square), (5, root), (8, high)])

                def first(b):
                    for t in range(TB):
                        n = b * TB + t
                        act.wait_ge(s_nm, b * N1 + (t + 1) * C_HEADS)
                        act.activation(stack_q[:, t, :, 48:49].bitcast(F32R),
                                       nm[:, t, :].rearrange("p (h o) -> p h o", o=1), ACT.Copy).then_inc(s_nh, 1)

                def second(b):
                    for g in range(N2):
                        act.wait_ge(s_s2, b * N2 + g + 1)
                        if g >= RING:
                            act.wait_ge(s_pv, b * N2 + g - RING + 1)
                        act.activation(pt[:, g % RING, :], bank[2 + g % 4][:, :], ACT.Exp).then_inc(s_ex, 1)

                def finish(b):
                    for t in range(TB):
                        n = b * TB + t
                        act.wait_ge(s_ta, n + 1)
                        act.activation(a_f[:, t % 2, :, :].rearrange("p k n -> p (k n)"), bank[1][:, 0:DIM],
                                       ACT.Copy).then_inc(s_af, 1)

                act.wait_ge(s_w, 128)
                for i, f in enumerate((0.25, 1.0)):
                    x = act.activation(gq[:, :, i, :], gain[:, :, :], ACT.Copy, scale=f)
                x.then_inc(s_g, 1)
                act.wait_ge(s_z, 1)
                with act.Fori(0, BATCH) as b:
                    act.wait_ge(s_y, b * TB)
                    prep(b)
                    first(b)
                    second(b)
                    finish(b)

            @block.vector
            def _(dve):
                def prep(b):
                    norm = c.NORM[:, ds(b * TB, TB)].rearrange("p (t o) -> p t o", o=1).to_broadcast([P, TB, HALF])
                    dve.wait_ge(s_ab, b * TB)
                    for dst, src, f in ((mcos, cos, 0.5), (msin, sin, 0.5), (mneg, sin, -0.5)):
                        x = dve.scalar_tensor_tensor(dst[:, :, :], src[:, :, :], f, norm, ALU.mult, ALU.mult)
                    x.then_inc(s_tab, 1)
                    dve.wait_ge(s_tab, b + 1)

                    def products(t):
                        n = b * TB + t
                        dve.wait_ge(s_proj, n + 1)
                        dve.tensor_tensor(qk[:, t, 0:DIM], bank[0][:, 0:DIM], bias[:, 0:DIM], ALU.add)
                        dve.tensor_tensor(qk[:, t, DIM:W2], bank[1][:, 0:DIM], bias[:, DIM:W2], ALU.add)
                        dve.tensor_tensor(v_s[:, t, :, 0:C_HD], bank[1][:, DIM:W2].rearrange("p (h n) -> p h n", n=C_HD),
                                          bias[:, W2:].rearrange("p (h n) -> p h n", n=C_HD), ALU.add).then_inc(s_qk, 1)
                        dve.wait_ge(s_qk, n + 1)
                        dve.wait_ge(s_r, n)
                        x4 = qk[:, t, :].rearrange("p (h i o) -> p h i o", h=NH, o=2)
                        a4 = pa[:, :].rearrange("p (h i o) -> p h i o", h=NH, o=2)
                        b4 = pb_[:, :].rearrange("p (h i o) -> p h i o", h=NH, o=2)

                        def table(m):
                            return m[:, t, :].rearrange("p (o i) -> p o i", o=1).to_broadcast([P, NH, HALF])
                        for o in range(2):
                            dve.tensor_tensor(a4[:, :, :, o], x4[:, :, :, o], table(mcos), ALU.mult)
                            x = dve.tensor_tensor(b4[:, :, :, o], x4[:, :, :, 1 - o], table(msin if o else mneg), ALU.mult)
                        x.then_inc(s_ab, 1)

                    def heads(x):
                        return x.rearrange("p (h n) -> p h n", n=C_HD)

                    def centre(t):
                        n = b * TB + t
                        dve.wait_ge(s_r, n + 1)
                        dve.tensor_reduce(hsum[:, t, :], heads(qk[:, t, :]), AX.X, ALU.add).then_inc(s_sum, 1)
                        dve.wait_ge(s_sum, n + 1)
                        dve.scalar_tensor_tensor(heads(qk[:, t, :]),
                                                 hsum[:, t, :].rearrange("p (h o) -> p h o", o=1).to_broadcast([P, NH, C_HD]),
                                                 -1.0 / C_HD, heads(qk[:, t, :]), ALU.mult, ALU.add).then_inc(s_cen, 1)

                    def sums(t):
                        dve.wait_ge(s_sq, b * TB + t + 1)
                        dve.tensor_reduce(ssq[:, t, :], heads(sq[:, :]), AX.X, ALU.add).then_inc(s_ssq, 1)

                    def inverse(t):
                        dve.wait_ge(s_std, b * TB + t + 1)
                        dve.reciprocal(rstd[:, t, :], std[:, t, :]).then_inc(s_rs, 1)

                    def q_out(t):
                        dve.wait_ge(s_tr, b * TB + t + 1)
                        for j in range(2):
                            x = dve.tensor_copy(qt[:, 4 * j:4 * j + 4, t * P:(t + 1) * P],
                                                bank[2 + j][:, :].rearrange("p (a n) -> p a n", n=P))
                        x.then_inc(s_qe, 1)
                    tiles_of([(10, q_out), (0, products), (2, centre), (4, sums), (6, inverse)])

                def first(b):
                    for g in range(N1):
                        t, h = g // C_HEADS, g % C_HEADS
                        dve.wait_ge(s_s1, b * N1 + g + 1)
                        dve.tensor_reduce(nm[:, t, h:h + 1], bank[2 + g % 4][:, :], AX.X, ALU.max, negate=True).then_inc(s_nm, 1)
                        if h == 1 and t >= 1:
                            low_max(b, t - 1)
                    low_max(b, TB - 1)
                    dve.wait_ge(s_s1, b * N1 + N1)
                    for t in range(TB):
                        dve.wait_ge(s_tr2, b * TB + t + 1)
                        for j in range(2):
                            x = dve.tensor_copy(qt[:, 4 * j:4 * j + 4, t * P:(t + 1) * P],
                                                bank[6 + j][:, :].rearrange("p (a n) -> p a n", n=P))
                        x.then_inc(s_q2, 1)

                def low_max(b, t):
                    dve.wait_ge(s_nh, b * TB + t + 1)
                    dve.tensor_tensor(stack_q[:, t, :, 49:50].bitcast(F32R), nm[:, t, :].rearrange("p (h o) -> p h o", o=1),
                                      stack_q[:, t, :, 48:49], ALU.subtract).then_inc(s_nl, 1)

                def second(b):
                    for grp in range(4):
                        dve.wait_ge(s_pv, b * N2 + 16 * grp + 16)
                        dve.wait_ge(s_to, b * TB)
                        dve.tensor_copy(o_s[:, grp, :], bank[6 + grp % 2][:, :]).then_inc(s_oe, 1)
                    dve.memset(stack_q[:, :, :, 48:50], 0.0)

                def finish(b):
                    for t in range(TB):
                        n = b * TB + t
                        dve.wait_ge(s_to, n + 1)
                        o = bank[0][:, :].rearrange("p (h n) -> p h n", n=2 * C_HD)
                        dve.reciprocal(rden[:, t, :].rearrange("p (h o) -> p h o", o=1), o[:, :, C_HD:C_HD + 1]).then_inc(s_rd, 1)
                        dve.wait_ge(s_rd, n + 1)
                        if t >= 2:
                            dve.wait_ge(s_ta, n - 1)
                        dve.tensor_tensor(heads_of(a_t[:, t % 2, :]), o[:, :, 0:C_HD],
                                          rden[:, t, :].rearrange("p (h o) -> p h o", o=1).to_broadcast([P, C_HEADS, C_HD]),
                                          ALU.mult).then_inc(s_at, 1)
                        dve.wait_ge(s_y, n + 1)
                        dve.tensor_tensor(c.Y[:, ds(n, 1), :].rearrange("p o d -> p (o d)"), bank[1][:, DIM:2 * DIM],
                                          bo[:, :], ALU.add).then_inc(s_ye, 1)

                def heads_of(x):
                    return x.rearrange("p (h n) -> p h n", n=C_HD)

                dve.memset(stack_q[:, :, :, 48:64], 0.0)
                dve.memset(stack_k[:, :, :, 48:64], 0.0)
                dve.memset(kp[:, :, :].bitcast(F32), 0.0)
                dve.memset(v_s[:, :, :, C_HD:], 1.0).then_inc(s_z0, 1)
                dve.wait_ge(s_z0, 1)
                dve.memset(stack_k[:, :, :, 48:50], 1.0).then_inc(s_z, 1)
                dve.wait_ge(s_z, 1)
                dve.wait_ge(s_w, 128)
                with dve.Fori(0, BATCH) as b:
                    prep(b)
                    first(b)
                    second(b)
                    finish(b)

            @block.gpsimd
            def _(pool):
                def prep(b):
                    for dst, src in ((hq, c.HTq), (hkv, c.HTkv)):
                        x = pool.tensor_copy(dst[:, :, :], src[:, :, ds(b * SEQ, SEQ)])
                    x.then_inc(s_h, 1)

                    def rotate(t):
                        pool.wait_ge(s_ab, b * TB + t + 1)
                        pool.tensor_tensor(qk[:, t, :], pa[:, :], pb_[:, :], ALU.add).then_inc(s_r, 1)

                    def normed(t):
                        n = b * TB + t
                        x = qk[:, t, :].rearrange("p (h n) -> p h n", n=C_HD)
                        pool.wait_ge(s_rs, n + 1)
                        pool.tensor_tensor(x, x, rstd[:, t, :].rearrange("p (h o) -> p h o", o=1).to_broadcast([P, NH, C_HD]),
                                           ALU.mult).then_inc(s_p, 1)
                        x = qk[:, t, :].rearrange("p (i h n) -> p i h n", i=2, n=C_HD)
                        for step, (op, sig) in enumerate(((ALU.mult, s_p), (ALU.add, s_n))):
                            pool.wait_ge(s_p, 2 * n + 1 + step)
                            g = gq[:, step, :, :].rearrange("p i (o n) -> p i o n", o=1).to_broadcast([P, 2, C_HEADS, C_HD])
                            pool.tensor_tensor(x, x, g, op).then_inc(sig, 1)

                    def low(t):
                        n = b * TB + t
                        pool.wait_ge(s_hi, n + 1)
                        for i, (stack, at, place) in enumerate(((stack_q, t, 2), (stack_k, t % 2, 1))):
                            src = qk[:, t, i * DIM:(i + 1) * DIM].rearrange("p (h n) -> p h n", n=C_HD)
                            x = pool.tensor_tensor(stack[:, at, :, place * C_HD:(place + 1) * C_HD].bitcast(F32R), src,
                                                   stack[:, at, :, 0:C_HD], ALU.subtract)
                        x.then_inc(s_lo, 1)
                    tiles_of([(1, rotate), (7, normed), (9, low)])

                pool.wait_ge(s_g, 1)
                pool.wait_ge(s_z, 1)
                with pool.Fori(0, BATCH) as b:
                    pool.wait_ge(s_proj, b * TB)
                    prep(b)
        nc.disable_value_cache = False


def sandwich(nc, x, a_w, a_wo, b_w, b_wo, b_cos, b_sin, m0_w13, m0_w2, m0_gate, c_wq, c_wkv, c_wo, c_bias, c_bo, c_gain,
             c_cos, c_sin, m1_w13, m1_w2, m1_gate, ident, a_cos, a_sin, a_mask, b_mask, b_rows, before, scales, out):
    with ExitStack() as st:
        c = Core(nc, st)
        c.X, c.XN, c.Y = (c.sb(n, [P, TILES, DIM]) for n in ("X", "XN", "Y"))
        c.ident, c.eps = c.sb("ident", [P, P]), c.sb("eps", [P, 1])
        c.NORM, c.NORM2 = c.sb("norm", [P, TILES]), c.sb("norm_squared", [P, TILES])
        c.scales = c.sb("scales", [P, 6, KD])
        ln_w, ff_ln_w, q_g, q_b, kv_g, kv_b = (c.scales[:, i, :] for i in range(6))

        def load(name, pairs, eps=False):
            loaded = c.sem(name)
            with nc.Block() as block:
                @block.sync
                def _(sp):
                    for dst, src in pairs:
                        sp.dma_start(dst, src).then_inc(loaded, 16)
                    sp.wait_ge(loaded, 16 * len(pairs))
                if eps:
                    @block.vector
                    def _(dve):
                        dve.memset(c.eps[:, :], EPS)

        with ExitStack() as raw:
            c.HT = raw.enter_context(nc.sbuf_tensor("HT", [P, KD, TOKENS], F32))
            with ExitStack() as scope:
                c.cosA, c.sinA = (scope.enter_context(nc.sbuf_tensor(n, [P, SEQ], F32)) for n in ("cosA", "sinA"))
                c.maskA = scope.enter_context(nc.sbuf_tensor("maskA", [P, A_SPAN], F32))
                load("constants_a", ((c.ident[:, :], ident), (c.cosA[:, :], a_cos), (c.sinA[:, :], a_sin),
                                     (c.maskA[:, :], a_mask), (c.scales[:, :, :], scales)), eps=True)
                norm_stage(nc, c, "n0", x_dram=x, outs=((c.HT, None, None),))
                attention0(nc, c, a_w, a_wo)
                c.free_semaphores()
            norm_stage(nc, c, "n1", post="rms", outs=((c.HT, ln_w, None),))
            with ExitStack() as scope:
                c.maskB = scope.enter_context(nc.sbuf_tensor("maskB", [P, SEQ], F32))
                c.rowsB = scope.enter_context(nc.sbuf_tensor("rowsB", [P, 2], F32))
                load("constants_b", ((c.maskB[:, :], b_mask), (c.rowsB[:, :], b_rows)))
                attention1(nc, c, b_w, b_wo, b_cos, b_sin)
                c.free_semaphores()
        with ExitStack() as split:
            c.HT_hi, c.HT_lo = (split.enter_context(nc.sbuf_tensor(n, [P, KD, TOKENS], F32R)) for n in ("HT0_hi", "HT0_lo"))
            norm_stage(nc, c, "n2", residual=False, post="rms", outs=(((c.HT_hi, c.HT_lo), ff_ln_w, None),))
            c.before = split.enter_context(nc.sbuf_tensor("before0", [P, EXPERTS, EXPERTS], F32))
            load("constants_m0", ((c.before[:, :, :], before.to_broadcast([P, EXPERTS, EXPERTS])),))
            moe(nc, c, "m0", EXPERTS, M0_HIDDEN, EXPERTS, m0_w13, m0_w2, m0_gate, False)
            c.free_semaphores()
        with ExitStack() as two:
            c.HTq, c.HTkv = (two.enter_context(nc.sbuf_tensor(n, [P, KD, TOKENS], F32)) for n in ("HTq", "HTkv"))
            norm_stage(nc, c, "n3", add="y", post="ln", outs=((c.HTq, q_g, q_b), (c.HTkv, kv_g, kv_b)))
            attention2(nc, c, c_wq, c_wkv, c_wo, c_bias, c_bo, c_gain, c_cos, c_sin)
            c.free_semaphores()
        with ExitStack() as split:
            c.HT_hi, c.HT_lo = (split.enter_context(nc.sbuf_tensor(n, [P, KD, TOKENS], F32R)) for n in ("HT1_hi", "HT1_lo"))
            norm_stage(nc, c, "n4", outs=(((c.HT_hi, c.HT_lo), None, None),))
            c.before = split.enter_context(nc.sbuf_tensor("before1", [P, EXPERTS, EXPERTS], F32))
            load("constants_m1", ((c.before[:, :, :], before.to_broadcast([P, EXPERTS, EXPERTS])),))
            moe(nc, c, "m1", EXPERTS + SHARED, M1_HIDDEN, EXPERTS, m1_w13, m1_w2, m1_gate, True)
            c.free_semaphores()
        norm_stage(nc, c, "n5", out_dram=out)


def half_rows(w):
    return w.reshape(KD, P, -1).transpose(1, 0, 2)


def tables():
    f = np.float32
    pos = np.arange(SEQ, dtype=f)

    inv = (f(1.0) / f(10000.0) ** (np.arange(0, A_HD, 2, dtype=f) / f(A_HD))).astype(f)
    ang = (pos[:, None] * inv[None, :]).T
    a_cos = np.concatenate([np.cos(ang)] * 2, 0)
    a_sin = np.concatenate([np.sin(ang), -np.sin(ang)], 0)
    query, key = np.arange(P)[:, None], np.arange(A_SPAN)[None, :] - WINDOW
    a_mask = np.where((key <= query) & (key > query - WINDOW), 0, NEG).astype(f)

    half = B_HD // 2
    inv = (f(1.0) / f(150000.0) ** (np.arange(half, dtype=f) / f(half))).astype(f)
    ang = (pos[:, None] * inv[None, :]).T
    b_cos = np.concatenate([np.cos(ang)] * 4, 0)
    b_sin = np.concatenate([np.sin(ang), np.sin(ang), -np.sin(ang), -np.sin(ang)], 0)
    key = np.arange(P)[None, :]
    b_mask = np.concatenate([np.zeros((P, SEQ - P), f), np.where(key <= query, 0, -NEG).astype(f)], 1)
    of_a = (np.arange(P) // half % 2 == 0).astype(f)
    b_rows = np.stack([of_a, 1 - of_a], 1)

    steps = np.linspace(0.0, 1.0, C_HD // 2, dtype=f)
    freq = ((f(8000.0 / 200.0) ** steps).astype(f) * f(200.0) / f(1000.0)).astype(f)
    freq = (f(200.0) * freq / f(1000.0)).astype(f)
    ang = (pos[:, None] * freq[None, :]).reshape(TB, P, -1).transpose(1, 0, 2)

    expert = np.arange(EXPERTS)
    before = (expert[None, :] < expert[:, None]).astype(f)[None]
    return {"ident": np.eye(P, dtype=f), "a_cos": a_cos, "a_sin": a_sin, "a_mask": a_mask, "b_cos": b_cos, "b_sin": b_sin,
            "b_mask": b_mask, "b_rows": b_rows, "c_cos": np.cos(ang), "c_sin": np.sin(ang), "before": before}


def layout(i):
    f = np.float32
    d = {"x": i["L0_attn_x"]}
    d["a_w"] = i["L0_attn_w_qkv"].reshape(3, A_HEADS, A_HD, KD, P).transpose(1, 4, 3, 0, 2)
    d["a_wo"] = i["L0_attn_w_o"].T.reshape(A_HEADS, A_HD, DIM)

    def interleave(a, b):
        h = B_HD // 2
        return np.concatenate([a[:, :h], b[:, :h], a[:, h:], b[:, h:]], 1)
    q = i["L0_ffn_wq"].reshape(DIM, B_HEADS, B_HD)
    k, v = (i[n].reshape(DIM, B_KV, B_HD) for n in ("L0_ffn_wk", "L0_ffn_wv"))
    pairs = []
    for p in range(B_PAIRS):
        a, b = 2 * p, 2 * p + 1
        cols = [interleave(k[:, a], k[:, b]), np.concatenate([v[:, a], v[:, b]], 1)]
        cols += [interleave(q[:, B_REP * a + j], q[:, B_REP * b + j]) for j in range(B_REP)]
        pairs.append(np.stack(cols))
    d["b_w"] = np.stack(pairs).reshape(B_PAIRS, 2 + B_REP, KD, P, P).transpose(3, 2, 0, 1, 4)
    d["b_wo"] = i["L0_ffn_wo"].reshape(B_PAIRS, 2, B_REP, B_HD, DIM).transpose(1, 3, 0, 2, 4).reshape(P, B_UNITS, DIM)

    w1, w3 = (i[n].reshape(EXPERTS, KD, P, 2, P) for n in ("L0_ffn_w1", "L0_ffn_w3"))
    d["m0_w13"] = np.stack([w1, w3], 4).transpose(0, 2, 1, 3, 4, 5).reshape(EXPERTS, P, -1)
    d["m0_w2"] = i["L0_ffn_w2"]
    d["m0_gate"] = half_rows(i["L0_ffn_wg"])

    d["c_wq"], d["c_wkv"], d["c_wo"] = (half_rows(i["L1_attn_" + n]) for n in ("Wq", "Wkv", "Wo"))
    d["c_bias"] = np.concatenate([i["L1_attn_bq"], i["L1_attn_bkv"]])[None]
    d["c_bo"] = i["L1_attn_bo"][None]
    d["c_gain"] = np.concatenate([i["L1_attn_ln_h_g"], i["L1_attn_ln_h_b"]])[None]

    n = M1_HIDDEN
    gu, sgu = i["L1_ffn_w_gate_up"], i["L1_ffn_shared_gate_up"]
    gate = np.concatenate([gu[:, :, :n], np.stack([sgu[:, :n], sgu[:, n:2 * n]])])
    up = np.concatenate([gu[:, :, n:], np.stack([sgu[:, 2 * n:3 * n], sgu[:, 3 * n:]])])
    pad = np.zeros((EXPERTS + SHARED, DIM, 64 - (n - P)), f)
    w = np.concatenate([gate[:, :, :P], up[:, :, :P], gate[:, :, P:], pad, up[:, :, P:]], 2)
    d["m1_w13"] = w.reshape(EXPERTS + SHARED, KD, P, -1).transpose(0, 2, 1, 3).reshape(EXPERTS + SHARED, P, -1)
    d["m1_w2"] = np.concatenate([i["L1_ffn_w_down"], np.stack([i["L1_ffn_shared_down"][:n], i["L1_ffn_shared_down"][n:]])])
    d["m1_gate"] = half_rows(i["L1_ffn_gate_w"].T)

    vectors = ("L0_ffn_ln_w", "L0_ffn_ff_ln_w", "L1_attn_ln_q_g", "L1_attn_ln_q_b", "L1_attn_ln_kv_g", "L1_attn_ln_kv_b")
    d["scales"] = np.stack([i[v].reshape(KD, P) for v in vectors]).transpose(2, 0, 1)
    return d


_INS = ["x", "a_w", "a_wo", "b_w", "b_wo", "b_cos", "b_sin", "m0_w13", "m0_w2", "m0_gate", "c_wq", "c_wkv", "c_wo", "c_bias",
        "c_bo", "c_gain", "c_cos", "c_sin", "m1_w13", "m1_w2", "m1_gate", "ident", "a_cos", "a_sin", "a_mask", "b_mask",
        "b_rows", "before", "scales"]


def kernel(**inputs):
    import concourse.bacc as _bacc
    from concourse import mybir as _mybir
    from concourse.bass_utils import run_bass_kernel_spmd as _run

    laid = layout({n: np.asarray(a) for n, a in inputs.items()})
    laid.update(tables())
    nc = _bacc.Bacc("TRN2", target_bir_lowering=False, num_devices=1)
    arrays, args = {}, []
    for name in _INS:
        a = np.ascontiguousarray(laid[name])
        arrays[f"in_{name}_dram"] = a
        args.append(nc.dram_tensor(f"in_{name}_dram", a.shape, _mybir.dt.from_np(a.dtype), kind="ExternalInput").ap())
    args.append(nc.dram_tensor("out_dram", (BATCH, SEQ, DIM), F32, kind="ExternalOutput").ap())
    sandwich(nc, *args)
    r = _run(nc, [arrays], core_ids=[0])
    return r.results[0]["out_dram"]
```

```python
import numpy as np
from contextlib import ExitStack
import concourse.bass as bass
from concourse import mybir

F32 = mybir.dt.float32
F32R = mybir.dt.float32r
ALU = mybir.AluOpType
ACT = mybir.ActivationFunctionType
AX = mybir.AxisListType
ds = bass.ds

P = 128
BATCH, SEQ, DIM = 4, 512, 256
TOKENS = BATCH * SEQ
TILES = TOKENS // P
TB = SEQ // P
KD = DIM // P
EPS = 1e-5

A_HEADS, A_HD, WINDOW = 16, 128, 64
A_SPAN = P + WINDOW
A_SCALE = float(1.0 / np.sqrt(A_HD))
NEG = -1e30

EXPERTS, SHARED = 16, 2
M0_HIDDEN, M1_HIDDEN = 256, 176


class Chain:

    def __init__(self, eng, sem):
        self.eng, self.sem, self.n, self.base = eng, sem, 0, 0

    def add(self, ins):
        ins.then_inc(self.sem, 1)
        self.n += 1
        return self.n + self.base

    def wait(self, mark=None):
        self.eng.wait_ge(self.sem, self.n + self.base if mark is None else mark)


class Core:

    def __init__(self, nc, ctx):
        self.nc, self.ctx, self.sems = nc, ctx, []
        self.tick = self.sb("tick", [P, 4])

    def sb(self, name, shape, dt=F32):
        return self.ctx.enter_context(self.nc.sbuf_tensor(name, shape, dt))

    def sem(self, name):
        self.sems.append(self.nc.alloc_semaphore(name=name))
        return self.sems[-1]

    def free_semaphores(self):
        self.nc.clear_and_free_semaphores(self.sems)
        self.nc.all_engine_barrier()
        self.sems = []


def attention0(nc, c, w_dram, wo_dram):
    PAIRS = A_HEADS // 2
    U = 2 * BATCH
    with ExitStack() as st:
        def sb(name, shape, dt=F32):
            return st.enter_context(nc.sbuf_tensor(name, shape, dt))

        def pb(name, shape, dt=F32):
            return st.enter_context(nc.psum_tensor(name, shape, dt))
        sem = c.sem
        w = sb("a_w", [P, 2, KD, 3, P])
        wo = sb("a_wo", [P, 2, DIM])
        q_r = sb("a_q", [P, 2, SEQ])
        k_r = sb("a_k", [P, 2, SEQ])
        v_s = sb("a_v", [P, 4, TB, A_HD])
        prod = sb("a_prod", [P, 4, SEQ])
        s_m = sb("a_s", [P, 2, TB, A_SPAN])
        mx, nmx, den, rden = (sb("a_" + n, [P, 2, TB]) for n in ("mx", "nmx", "den", "rden"))
        pt = sb("a_pt", [P, TB, A_SPAN])
        ot = sb("a_ot", [P, 2, TOKENS])
        p_q, p_k, p_v = pb("p_q", [P, SEQ]), pb("p_k", [P, SEQ]), pb("p_v", [P, SEQ])
        p_s = pb("p_s", [P, 2, SEQ])
        p_t, p_t2 = pb("p_t", [P, SEQ]), pb("p_t2", [P, SEQ])
        p_o = pb("p_o", [P, SEQ])
        scores = p_s[:, :, 0:2 * A_SPAN].rearrange("p a (b n) -> p a b n", b=2)
        yps = p_s[:, :, :].rearrange("p a (b n) -> p a b n", b=2)

        s_w = [sem("a_s_w_even"), sem("a_s_w_odd")]
        s_wo = sem("a_s_wo")
        s_proj = sem("a_s_proj")
        s_rope = sem("a_s_rope")
        s_prod = sem("a_s_prod")
        s_v = sem("a_s_v")
        s_sc = sem("a_s_sc")
        s_mx = sem("a_s_mx")
        s_exp = sem("a_s_exp")
        s_rd = sem("a_s_rd")
        s_pn = sem("a_s_pn")
        s_tr = sem("a_s_tr")
        s_pto = sem("a_s_pto")
        s_ov = sem("a_s_ov")
        s_ot = sem("a_s_ot")
        s_y = sem("a_s_y")
        s_ya = sem("a_s_ya")
        s_z = sem("a_s_z")
        s_d = sem("a_s_d")

        def on(eng, sem_, value):
            if not isinstance(value, int) or value > 0:
                eng.wait_ge(sem_, value)

        with nc.Block() as block:
            @block.sync
            def _(sp):
                def load_w(h, slot):
                    sp.dma_start(w[:, slot, :, :, :], w_dram[ds(h, 1)].rearrange("o p k j n -> (o p) k j n")).then_inc(s_w[slot], 16)

                def load_wo(h):
                    sp.dma_start(wo[:, :, :], wo_dram[ds(h, 2)].rearrange("o p n -> p o n")).then_inc(s_wo, 16)
                load_w(0, 0)
                load_w(1, 1)
                load_wo(0)
                with sp.Fori(1, PAIRS) as i:
                    sp.wait_ge(s_proj, i * (3 * U) - 3 * BATCH)
                    load_w(i * 2, 0)
                    sp.wait_ge(s_proj, i * (3 * U))
                    load_w(i * 2 + 1, 1)
                    sp.wait_ge(s_y, i * BATCH)
                    load_wo(i * 2)

            def passes(eng, step):
                for u in range(U):
                    step(0, u)
                with eng.Fori(1, PAIRS) as i:
                    for u in range(U):
                        step(i, u)
                for u in range(3):
                    step(PAIRS, u)

            def alive(i, u, back):
                if isinstance(i, int):
                    return 0 <= i * U + u - back < PAIRS * U
                return True

            def out_of(u):
                return (u - 3) % U - BATCH if (u - 3) % U >= BATCH else None

            def outs_before(i, u):
                return i * BATCH + min(u, 3) - 3

            @block.tensor
            def _(pe):
                def qk(i, u, j, bank):
                    n, slot, b = i * U + u, u // BATCH, u % BATCH
                    on(pe, s_w[slot], i * 16 + 16)
                    on(pe, s_prod, 2 * n - 1 + j)
                    for k in range(KD):
                        mm = pe.matmul(bank[:, :], w[:, slot, k, j, :], c.HT[:, k, b * SEQ:(b + 1) * SEQ],
                                       start=(k == 0), stop=(k == KD - 1))
                    mm.then_inc(s_proj, 1)

                def v(i, u):
                    n, slot, b = i * U + u, u // BATCH, u % BATCH
                    on(pe, s_v, n)
                    for t in range(TB):
                        for k in range(KD):
                            mm = pe.matmul(p_v[:, t * P:(t + 1) * P], c.HT[:, k, b * SEQ + t * P:b * SEQ + (t + 1) * P],
                                           w[:, slot, k, 2, :], start=(k == 0), stop=(k == KD - 1))
                    mm.then_inc(s_proj, 1)

                def scores_of(i, u):
                    n = i * U + u
                    pe.wait_ge(s_rope, 2 * n + 2)
                    on(pe, s_mx, n)
                    if out_of(u) is not None and alive(i, u, 3):
                        pe.wait_ge(s_ya, outs_before(i, u) + 1)
                    for t in range(TB):
                        lo = WINDOW if t == 0 else 0
                        mm = pe.matmul(scores[:, t // 2, t % 2, lo:A_SPAN], q_r[:, u % 2, t * P:(t + 1) * P],
                                       k_r[:, u % 2, t * P - WINDOW + lo:(t + 1) * P], start=True, stop=True)
                    mm.then_inc(s_sc, 1)

                def turn(i, u):
                    n, slot = i * U + u - 2, u % 2
                    pe.wait_ge(s_pn, n + 1)
                    on(pe, s_pto, n)
                    for t in range(TB):
                        pe.transpose(p_t[:, t * P:(t + 1) * P], s_m[:, slot, t, WINDOW:A_SPAN], c.ident[:, :])
                    for t in range(1, TB):
                        mm = pe.transpose(p_t2[0:WINDOW, t * P:(t + 1) * P], s_m[:, slot, t, 0:WINDOW], c.ident[:, :])
                    mm.then_inc(s_tr, 1)

                def values(i, u):
                    n = i * U + u - 2
                    pe.wait_ge(s_v, n + 1)
                    on(pe, s_ot, n)
                    pe.wait_ge(s_pto, n + 1)
                    for t in range(TB):
                        width = P if t == TB - 1 else A_SPAN
                        mm = pe.matmul(p_o[:, t * P:t * P + width], v_s[:, (u - 2) % 4, t, :], pt[:, t, 0:width],
                                       start=(t == 0), stop=(t == TB - 1), skip_group_check=True)
                    mm.then_inc(s_ov, 1)

                def out_proj(i, u):
                    n, b = i * U + u - 3, out_of(u)
                    done = outs_before(i, u)
                    on(pe, s_ya, done)
                    pe.wait_ge(s_wo, (i + (0 if u >= 3 else -1)) * 16 + 16)
                    pe.wait_ge(s_ot, n + 1)
                    pe.wait_ge(s_mx, n + 3 if alive(i, u, 0) else PAIRS * U)
                    for t in range(TB):
                        for slot in range(2):
                            tok = b * SEQ + t * P
                            mm = pe.matmul(yps[:, t // 2, t % 2, :], ot[:, slot, tok:tok + P], wo[:, slot, :],
                                           start=(slot == 0), stop=(slot == 1))
                    mm.then_inc(s_y, 1)

                def step(i, u):
                    if alive(i, u, 0):
                        qk(i, u, 0, p_q)
                        qk(i, u, 1, p_k)
                    if out_of(u) is not None and alive(i, u, 3):
                        out_proj(i, u)
                    if alive(i, u, 2):
                        turn(i, u)
                    if alive(i, u, 0):
                        v(i, u)
                    if alive(i, u, 2):
                        values(i, u)
                    if alive(i, u, 0):
                        scores_of(i, u)
                passes(pe, step)

            @block.scalar
            def _(act):
                def turned(i, u):
                    n = i * U + u - 2
                    act.wait_ge(s_tr, n + 1)
                    on(act, s_ov, n)
                    act.activation(pt[:, :, 0:P], p_t[:, :].rearrange("p (t n) -> p t n", t=TB), ACT.Copy)
                    act.activation(pt[WINDOW:P, 0:TB - 1, P:A_SPAN],
                                   p_t2[0:WINDOW, P:].rearrange("p (t n) -> p t n", t=TB - 1)[:, :, 0:WINDOW],
                                   ACT.Copy).then_inc(s_pto, 1)

                def copy_v(i, u):
                    n = i * U + u
                    act.wait_ge(s_proj, 3 * n + 3)
                    on(act, s_ov, n - 3)
                    act.activation(v_s[:, u % 4, :, :].rearrange("p t n -> p (t n)"), p_v[:, :], ACT.Copy).then_inc(s_v, 1)

                def copy_out(i, u):
                    n = i * U + u - 2
                    v = (u - 2) % U
                    slot, b = v // BATCH, v % BATCH
                    act.wait_ge(s_ov, n + 1)
                    if slot == 0:
                        on(act, s_y, i * BATCH - BATCH + b + 1)
                    act.activation(ot[:, slot, b * SEQ:(b + 1) * SEQ], p_o[:, :], ACT.Copy).then_inc(s_ot, 1)

                def exp(i, u):
                    n = i * U + u
                    act.wait_ge(s_mx, n + 1)
                    for t in range(TB):
                        lo = WINDOW if t == 0 else 0
                        x = act.activation(s_m[:, u % 2, t, lo:], s_m[:, u % 2, t, lo:], ACT.Exp, bias=nmx[:, u % 2, t:t + 1],
                                           scale=A_SCALE, accum_out=den[:, u % 2, t:t + 1])
                    x.then_inc(s_exp, 1)

                def step(i, u):
                    if alive(i, u, 2):
                        turned(i, u)
                    if alive(i, u, 0):
                        copy_v(i, u)
                    if alive(i, u, 2):
                        copy_out(i, u)
                    if alive(i, u, 0):
                        exp(i, u)
                passes(act, step)

            @block.vector
            def _(dve):
                def rope(i, u, j, bank):
                    n = i * U + u
                    dve.wait_ge(s_proj, 3 * n + 1 + j)
                    on(dve, s_rope, 2 * n - 1 + j)
                    dve.tensor_tensor(prod[:, 2 * j, :], bank[:, :], c.cosA[:, :], ALU.mult)
                    H = P // 2
                    dve.tensor_tensor(prod[0:H, 2 * j + 1, :], bank[H:P, :], c.sinA[H:P, :], ALU.mult)
                    dve.tensor_tensor(prod[H:P, 2 * j + 1, :], bank[0:H, :], c.sinA[0:H, :], ALU.mult).then_inc(s_prod, 1)

                def mask(i, u):
                    n = i * U + u
                    dve.wait_ge(s_sc, n + 1)
                    on(dve, s_tr, n - 1)
                    dve.memset(c.tick[:, u % 2:u % 2 + 1], 0.0)
                    for t in range(TB):
                        lo = WINDOW if t == 0 else 0
                        x = dve.tensor_tensor_reduce(s_m[:, u % 2, t, lo:], scores[:, t // 2, t % 2, lo:], c.maskA[:, lo:], 1.0,
                                                     3 * NEG, ALU.add, ALU.max, mx[:, u % 2, t:t + 1])
                    x.then_inc(s_d, 1)
                    dve.wait_ge(s_d, n + 1)
                    dve.tensor_scalar(nmx[:, u % 2, :], mx[:, u % 2, :], -A_SCALE, None, ALU.mult).then_inc(s_mx, 1)

                def inverse(i, u):
                    n, slot = i * U + u - 1, (u - 1) % 2
                    dve.wait_ge(s_exp, n + 1)
                    on(dve, s_pn, n - 1)
                    dve.reciprocal(rden[:, slot, :], den[:, slot, :]).then_inc(s_rd, 1)

                def add_y(i, u):
                    b = out_of(u)
                    dve.wait_ge(s_y, outs_before(i, u) + 1)
                    y = c.Y[:, b * TB:(b + 1) * TB, :].rearrange("p (a b) n -> p a (b n)", a=2)
                    for a in range(2):
                        x = dve.tensor_tensor(y[:, a, :], p_s[:, a, :], y[:, a, :], ALU.add)
                    x.then_inc(s_ya, 1)

                def step(i, u):
                    if alive(i, u, 0):
                        rope(i, u, 0, p_q)
                    if alive(i, u, 1):
                        inverse(i, u)
                    if alive(i, u, 0):
                        rope(i, u, 1, p_k)
                    if out_of(u) is not None and alive(i, u, 3):
                        add_y(i, u)
                    if alive(i, u, 0):
                        mask(i, u)

                dve.memset(c.Y[:, :, :], 0.0)
                dve.memset(s_m[:, :, 0, 0:WINDOW], 0.0)
                dve.memset(pt[0:WINDOW, :, P:A_SPAN], 0.0).then_inc(s_z, 1)
                dve.wait_ge(s_z, 1)
                passes(dve, step)

            @block.gpsimd
            def _(pool):
                def rope(i, u, j, dst):
                    n = i * U + u
                    pool.wait_ge(s_prod, 2 * n + 1 + j)
                    on(pool, s_sc, n - 1)
                    pool.tensor_tensor(dst[:, u % 2, :], prod[:, 2 * j, :], prod[:, 2 * j + 1, :], ALU.add).then_inc(s_rope, 1)

                def normalise(i, u):
                    n, slot = i * U + u - 1, (u - 1) % 2
                    pool.wait_ge(s_rd, n + 1)
                    pool.tensor_tensor(s_m[:, slot, :, :], s_m[:, slot, :, :],
                                       rden[:, slot, :].rearrange("p (t o) -> p t o", o=1).to_broadcast([P, TB, A_SPAN]),
                                       ALU.mult).then_inc(s_pn, 1)

                def step(i, u):
                    if alive(i, u, 0):
                        rope(i, u, 0, q_r)
                    if alive(i, u, 1):
                        normalise(i, u)
                    if alive(i, u, 0):
                        rope(i, u, 1, k_r)
                pool.wait_ge(s_z, 1)
                passes(pool, step)


GROUPS = TILES // TB


def skewed(steps):
    for at in range(GROUPS + max(steps)):
        for level in sorted(steps):
            if 0 <= at - level < GROUPS:
                steps[level](at - level)


def norm_stage(nc, c, name, x_dram=None, add=None, residual=True, post=None, outs=(), out_dram=None):
    with ExitStack() as st:
        def sb(n, shape, dt=F32):
            return st.enter_context(nc.sbuf_tensor(f"{name}_{n}", shape, dt))

        def sem(n):
            return c.sem(f"{name}_{n}")
        rows = sb("rows", [P, GROUPS, TB, DIM]) if post else None
        scratch = sb("scratch", [P, 2, DIM])
        sty, stx, stn = sb("sty", [P, TILES, 6]), sb("stx", [P, TILES, 6]), sb("stn", [P, TILES, 6])
        mvy, mvx, mvn = sb("mvy", [P, TILES, 2]), sb("mvx", [P, TILES, 2]), sb("mvn", [P, TILES, 2])
        sdy, sdx, sdn = sb("sdy", [P, TILES]), sb("sdx", [P, TILES]), sb("sdn", [P, TILES])
        rsy, rsx, rsn = sb("rsy", [P, TILES]), sb("rsx", [P, TILES]), sb("rsn", [P, TILES])
        p_t = [st.enter_context(nc.psum_tensor(f"{name}_pt{i}", [P, SEQ], F32)) for i in range(4)]

        final = out_dram is not None
        has_y = residual and x_dram is None
        has_xn = residual and not final
        split = any(isinstance(o[0], tuple) for o in outs)

        def sems(used, *names):
            return [sem(n) if used else None for n in names]
        s_ld, = sems(x_dram is not None, "loaded")
        s_add, = sems(add is not None, "added")
        s_sty, s_mvy, s_sdy, s_rsy, s_yn, s_x = sems(has_y, "stat_y", "mean_y", "std_y", "rstd_y", "y_norm", "x_sum")
        s_stx, s_mvx, s_sdx, s_rsx, s_xn = sems(has_xn, "stat_x", "mean_x", "std_x", "rstd_x", "x_norm")
        s_scr, s_sdn, s_rsn, s_rows = sems(post is not None, "squares", "std_n", "rstd_n", "rows")
        s_sq, s_stn, s_mvn = sems(post == "ln", "norm_of_x", "stat_n", "mean_n")
        s_tr, s_ht = sems(not final, "transposed", "copied")
        s_hi, = sems(split, "high_part")
        s_out, = sems(final, "stored")

        def tiles(g):
            return range(g * TB, (g + 1) * TB)

        def src_rows(t):
            return rows[:, t // TB, t % TB, :] if post else c.XN[:, t, :]

        with nc.Block() as block:
            @block.sync
            def _(sp):
                if x_dram is not None:
                    for g in range(GROUPS):
                        sp.dma_start(c.X[:, g * TB:(g + 1) * TB, :],
                                     x_dram[g].rearrange("(t p) d -> p t d", p=P)).then_inc(s_ld, 16)
                        sp.wait_ge(s_ld, 16 * (g + 1))
                if final:
                    for g in range(GROUPS):
                        sp.wait_ge(s_x, g + 1)
                        sp.dma_start(out_dram[g].rearrange("(t p) d -> p t d", p=P),
                                     c.X[:, g * TB:(g + 1) * TB, :]).then_inc(s_out, 16)
                    sp.wait_ge(s_out, 16 * GROUPS)

            @block.vector
            def _(dve):
                def stats(src, st_, done, ready, unit=1):
                    def do(g):
                        if ready is not None:
                            dve.wait_ge(ready, unit * (g + 1))
                        for t in tiles(g):
                            x = dve.bn_stats(st_[:, t, :], src[:, t, :])
                        x.then_inc(done, 1)
                    return do

                def mean(st_, stated, mv, done):
                    def do(g):
                        dve.wait_ge(stated, g + 1)
                        for t in tiles(g):
                            x = dve.bn_aggr(mv[:, t, :], st_[:, t, :])
                        x.then_inc(done, 1)
                    return do

                def inverse(sd, ready, rs, done):
                    def do(g):
                        dve.wait_ge(ready, g + 1)
                        dve.reciprocal(rs[:, g * TB:(g + 1) * TB], sd[:, g * TB:(g + 1) * TB]).then_inc(done, 1)
                    return do

                def scaled(src, mv, rs, ready, dst, done):
                    def do(g):
                        dve.wait_ge(ready, g + 1)
                        for t in tiles(g):
                            x = dve.tensor_scalar(dst(t), src[:, t, :], mv[:, t, 0:1], rs[:, t:t + 1],
                                                  ALU.subtract, ALU.mult)
                        x.then_inc(done, 1)
                    return do

                def copy_out(g):
                    dve.wait_ge(s_tr, g + 1)
                    for dst, scale, shift in outs:
                        if isinstance(dst, tuple):
                            dve.wait_ge(s_hi, g + 1)
                            hi, lo = dst
                            for k in range(KD):
                                x = dve.scalar_tensor_tensor(lo[:, k, g * SEQ:(g + 1) * SEQ], p_t[2 * (g % 2) + k][:, :],
                                                             1.0 if scale is None else scale[:, k:k + 1],
                                                             hi[:, k, g * SEQ:(g + 1) * SEQ].bitcast(F32),
                                                             ALU.mult, ALU.subtract)
                            continue
                        for k in range(KD):
                            to, src = dst[:, k, g * SEQ:(g + 1) * SEQ], p_t[2 * (g % 2) + k][:, :]
                            if scale is None:
                                x = dve.tensor_copy(to, src)
                            elif shift is None:
                                x = dve.tensor_scalar(to, src, scale[:, k:k + 1], None, ALU.mult)
                            else:
                                x = dve.tensor_scalar(to, src, scale[:, k:k + 1], shift[:, k:k + 1], ALU.mult, ALU.add)
                    x.then_inc(s_ht, 1)

                steps = {}
                y_ready = s_add if add == "y" else None
                if has_y:
                    steps[0] = stats(c.Y, sty, s_sty, y_ready)
                    steps[1] = mean(sty, s_sty, mvy, s_mvy)
                    steps[3] = inverse(sdy, s_sdy, rsy, s_rsy)
                    steps[4] = scaled(c.Y, mvy, rsy, s_rsy, lambda t: c.Y[:, t, :], s_yn)
                if has_xn:
                    steps[6] = stats(c.X, stx, s_stx, s_x if has_y else s_ld, 1 if has_y else 16)
                    steps[7] = mean(stx, s_stx, mvx, s_mvx)
                    steps[9] = inverse(sdx, s_sdx, rsx, s_rsx)
                    steps[10] = scaled(c.X, mvx, rsx, s_rsx, lambda t: c.XN[:, t, :], s_xn)
                if post == "rms":
                    steps[14] = inverse(sdn, s_sdn, rsn, s_rsn)
                if post == "ln":
                    steps[11] = stats(c.XN, stn, s_stn, s_xn)
                    steps[12] = mean(stn, s_stn, mvn, s_mvn)
                    steps[14] = inverse(sdn, s_sdn, rsn, s_rsn)
                    steps[15] = scaled(c.XN, mvn, rsn, s_rsn, src_rows, s_rows)
                if not final:
                    steps[16] = copy_out
                skewed(steps)

            @block.gpsimd
            def _(pool):
                def grp(b, g):
                    return b[:, g * TB:(g + 1) * TB, :]
                for g in range(GROUPS):
                    if add == "y":
                        pool.tensor_tensor(grp(c.Y, g), grp(c.Y, g), grp(c.XN, g), ALU.add).then_inc(s_add, 1)
                    if add == "xn":
                        pool.tensor_tensor(grp(c.XN, g), grp(c.XN, g), grp(c.Y, g), ALU.add).then_inc(s_add, 1)
                if has_y:
                    for g in range(GROUPS):
                        pool.wait_ge(s_yn, g + 1)
                        pool.tensor_tensor(grp(c.X, g), grp(c.X, g), grp(c.Y, g), ALU.add).then_inc(s_x, 1)

            @block.scalar
            def _(act):
                def root(mv, ready, sd, done):
                    def do(g):
                        act.wait_ge(ready, g + 1)
                        a, b = g * TB, (g + 1) * TB
                        act.activation(sd[:, a:b], mv[:, a:b, 1], ACT.Sqrt, bias=c.eps[:, :]).then_inc(done, 1)
                    return do

                def squares(g):
                    if add == "xn" or residual:
                        act.wait_ge(s_add if add == "xn" else s_xn, g + 1)
                    for t in tiles(g):
                        if t >= 2:
                            act.wait_ge(s_scr, t - 1)
                        act.activation(scratch[:, t % 2, :], c.XN[:, t, :], ACT.Square,
                                       accum_out=mvn[:, t, 0:1] if post == "rms" else c.NORM2[:, t:t + 1]).then_inc(s_scr, 1)

                def rms(g):
                    act.wait_ge(s_scr, TB * (g + 1))
                    a, b = g * TB, (g + 1) * TB
                    act.activation(sdn[:, a:b], mvn[:, a:b, 0], ACT.Sqrt, bias=c.eps[:, :],
                                   scale=1.0 / DIM).then_inc(s_sdn, 1)

                def rms_rows(g):
                    act.wait_ge(s_rsn, g + 1)
                    for t in tiles(g):
                        x = act.activation(src_rows(t), c.XN[:, t, :], ACT.Copy, scale=rsn[:, t:t + 1])
                    x.then_inc(s_rows, 1)

                def norm(g):
                    act.wait_ge(s_scr, TB * (g + 1))
                    a, b = g * TB, (g + 1) * TB
                    act.activation(c.NORM[:, a:b], c.NORM2[:, a:b], ACT.Sqrt).then_inc(s_sq, 1)

                def high_part(g):
                    for dst, scale, shift in outs:
                        if isinstance(dst, tuple):
                            act.wait_ge(s_tr, g + 1)
                            for k in range(KD):
                                x = act.activation(dst[0][:, k, g * SEQ:(g + 1) * SEQ], p_t[2 * (g % 2) + k][:, :],
                                                   ACT.Copy, scale=1.0 if scale is None else scale[:, k:k + 1])
                            x.then_inc(s_hi, 1)

                steps = {}
                if split:
                    steps[16] = high_part
                if has_y:
                    steps[2] = root(mvy, s_mvy, sdy, s_sdy)
                if has_xn:
                    steps[8] = root(mvx, s_mvx, sdx, s_sdx)
                if post == "rms":
                    steps[11], steps[12], steps[15] = squares, rms, rms_rows
                if post == "ln":
                    steps[11], steps[12] = squares, norm
                    steps[13] = root(mvn, s_mvn, sdn, s_sdn)
                skewed(steps)

            if not final:
                @block.tensor
                def _(pe):
                    for g in range(GROUPS):
                        pe.wait_ge(s_rows if post else s_xn, g + 1)
                        if g >= 2:
                            pe.wait_ge(s_ht, g - 1)
                        for k in range(KD):
                            for t in tiles(g):
                                x = pe.transpose(p_t[2 * (g % 2) + k][:, (t % TB) * P:(t % TB + 1) * P],
                                                 src_rows(t)[:, k * P:(k + 1) * P], c.ident[:, :])
                        x.then_inc(s_tr, 1)


B_HEADS, B_KV, B_HD = 32, 8, 64
B_PAIRS = B_KV // 2
B_REP = B_HEADS // B_KV
B_UNITS = B_PAIRS * B_REP


def attention1(nc, c, w_dram, wo_dram, cos_dram, sin_dram):
    ITEMS = 2 * TB
    LAG = 4
    CLAG = LAG + 1
    INV = 2
    RING = 8
    VLAG = CLAG + 1
    TOTAL = B_UNITS * ITEMS
    LOADS = {}
    for t in range(TB):
        LOADS["v", t] = t
    n = TB
    for m in range(B_UNITS):
        if m % B_REP == 0:
            LOADS["k", m // B_REP] = n
            n += 1
        LOADS["q", m] = n
        n += 1
    NPROJ = n
    NROPE = NPROJ - TB
    with ExitStack() as st:
        def sb(name, shape, dt=F32):
            return st.enter_context(nc.sbuf_tensor("b_" + name, shape, dt))

        def pb(name):
            return st.enter_context(nc.psum_tensor("b_" + name, [P, SEQ], F32))

        def sem(name):
            return c.sem("b_" + name)
        w = sb("w", [P, KD, B_PAIRS, 2 + B_REP, P])
        wo = sb("wo", [P, B_UNITS, DIM])
        cos, sin = sb("cos", [P, SEQ]), sb("sin", [P, SEQ])
        mask = c.maskB
        h = sb("h", [P, KD, SEQ])
        v_s = sb("v", [P, TB, B_PAIRS * P])
        k_r = sb("k_rot", [P, SEQ])
        kp = sb("k", [P, 2, 2, SEQ])
        q_r = sb("q", [P, 2, SEQ])
        prod = sb("prod", [P, 2, SEQ])
        sm = sb("sm", [P, RING, SEQ])
        mn, den, rden = sb("mn", [P, RING]), sb("den", [P, RING]), sb("rden", [P, RING])
        pt = sb("pt", [P, 2, 2, TB, SEQ])
        ot_halves = (c.Y[:, :, :].rearrange("p (m a) d -> p m (a d)", a=2), sb("ot", [P, B_UNITS // 2, SEQ]))
        p_proj, p_s, p_t = [pb("pj0"), pb("pj1")], [pb("s0"), pb("s1")], [pb("t0"), pb("t1")]
        p_o, p_y = pb("o"), pb("y")
        p_s.append(p_y)

        s_w, s_z, s_h = sem("weights"), sem("zeros"), sem("h_copied")
        s_proj, s_prod, s_rope, s_kp = sem("projected"), sem("read"), sem("rotated"), sem("k_padded")
        s_sc, s_mn, s_exp, s_rd, s_pn = sem("scores"), sem("minimum"), sem("exp"), sem("inverse"), sem("normalised")
        s_tr, s_pa, s_pd = sem("transposed"), sem("pt_by_act"), sem("pt_by_dve")
        s_ov, s_ot, s_y, s_xn = sem("pv"), sem("ot_copied"), sem("out_proj"), sem("added")

        def ot(m, cols):
            return ot_halves[m // (B_UNITS // 2)][:, m % (B_UNITS // 2), cols]

        def item(g):
            return g // ITEMS, g % 2, (0, 2, 1, 3)[g % ITEMS // 2]

        def keys(t):
            return (t + 1) * P

        with nc.Block() as block:
            @block.sync
            def _(sp):
                sp.dma_start(w[:, :, :, :, :], w_dram).then_inc(s_w, 16)
                sp.dma_start(cos[:, :], cos_dram).then_inc(s_w, 16)
                sp.dma_start(sin[:, :], sin_dram).then_inc(s_w, 16)
                sp.dma_start(wo[:, :, :], wo_dram).then_inc(s_w, 16)
                sp.wait_ge(s_w, 64)

            @block.tensor
            def _(pe):
                def project(b, kind, m, part=None):
                    at = LOADS[kind, m]
                    bank = p_proj[at % 2]
                    if part != 1:
                        pe.wait_ge(s_prod, b * NPROJ + (at - 1 if at > 0 else 0))
                    for k in range(KD) if part is None else (part,):
                        if kind == "v":
                            x = pe.matmul(bank[:, :], h[:, k, m * P:(m + 1) * P], w[:, k, :, 1, :],
                                          start=(k == 0), stop=(k == KD - 1))
                        else:
                            pair, j = (m, 0) if kind == "k" else (m // B_REP, 2 + m % B_REP)
                            x = pe.matmul(bank[:, :], w[:, k, pair, j, :], h[:, k, :], start=(k == 0), stop=(k == KD - 1))
                    if part != 0:
                        x.then_inc(s_proj, 1)

                def scores(b, g):
                    m, head, t = item(g)
                    if g % (B_REP * ITEMS) == 0:
                        pe.wait_ge(s_kp, b * B_PAIRS + m // B_REP + 1)
                    if g % ITEMS == 0:
                        pe.wait_ge(s_rope, b * NROPE + LOADS["q", m] - TB + 1)
                    if g == 2:
                        pe.wait_ge(s_xn, b * TB)
                    if g >= 3:
                        pe.wait_ge(s_mn, b * TOTAL + g - 2)
                    pe.matmul(p_s[g % 3][:, 0:keys(t)], q_r[:, m % 2, t * P:(t + 1) * P],
                              kp[:, m // B_REP % 2, head, 0:keys(t)], start=True, stop=True).then_inc(s_sc, 1)

                def transposes(b, g):
                    m, head, t = item(g)
                    pe.wait_ge(s_pn, b * TOTAL + g + 1)
                    if g >= 2:
                        pe.wait_ge(s_pd if head else s_pa, b * (TOTAL // 2) + g // 2)
                    for k in range(t + 1):
                        x = pe.transpose(p_t[g % 2][:, k * P:(k + 1) * P], sm[:, g % RING, k * P:(k + 1) * P], c.ident[:, :])
                    x.then_inc(s_tr, 1)

                def values(b, m, k):
                    if k == 0:
                        pe.wait_ge(s_pa, b * (TOTAL // 2) + (m + 1) * TB)
                        pe.wait_ge(s_pd, b * (TOTAL // 2) + (m + 1) * TB)
                        pe.wait_ge(s_ot, b * B_UNITS + m)
                    pair = m // B_REP
                    for head in range(2):
                        r = head * B_HD
                        x = pe.matmul(p_o[r:r + B_HD, k * P:SEQ], v_s[:, k, pair * P + r:pair * P + r + B_HD],
                                      pt[:, m % 2, head, k, k * P:SEQ], start=(k == 0), stop=(k == TB - 1))
                    if k == TB - 1:
                        x.then_inc(s_ov, 1)

                pe.wait_ge(s_w, 64)
                pe.wait_ge(s_z, 1)
                with pe.Fori(0, BATCH) as b:
                    pe.wait_ge(s_h, b + 1)
                    for t in range(TB):
                        project(b, "v", t)
                    project(b, "k", 0)
                    project(b, "q", 0)
                    for g in range(TOTAL + VLAG + TB):
                        m, n = g // ITEMS, g % ITEMS
                        if g < TOTAL:
                            scores(b, g)
                            if m + 1 < B_UNITS:
                                if (m + 1) % B_REP == 0 and n in (1, 2):
                                    project(b, "k", (m + 1) // B_REP, n - 1)
                                if n in (3, 4):
                                    project(b, "q", m + 1, n - 3)
                        if LAG <= g < TOTAL + LAG:
                            transposes(b, g - LAG)
                        at = g - ITEMS - VLAG
                        if at >= 0 and at % ITEMS < TB:
                            values(b, at // ITEMS, at % ITEMS)
                    pe.wait_ge(s_ot, b * B_UNITS + B_UNITS)
                    for t in range(TB):
                        pe.wait_ge(s_xn, b * TB + t)
                        for m in range(B_UNITS):
                            x = pe.matmul(p_y[:, 0:DIM], ot(m, slice(t * P, (t + 1) * P)), wo[:, m, :],
                                          start=(m == 0), stop=(m == B_UNITS - 1))
                        x.then_inc(s_y, 1)

            @block.scalar
            def _(act):
                def pad(b, i):
                    act.wait_ge(s_rope, b * NROPE + LOADS["k", i] - TB + 1)
                    if i >= 2:
                        act.wait_ge(s_sc, b * TOTAL + (i - 1) * B_REP * ITEMS)
                    for head in range(2):
                        x = act.activation(kp[:, i % 2, head, :], k_r[:, :], ACT.Copy, scale=c.rowsB[:, head:head + 1])
                    x.then_inc(s_kp, 1)

                def copy_out(b, m):
                    act.wait_ge(s_ov, b * B_UNITS + m + 1)
                    act.activation(ot(m, slice(0, SEQ)), p_o[:, :], ACT.Copy).then_inc(s_ot, 1)

                with act.Fori(0, BATCH) as b:
                    act.wait_ge(s_y, b * TB)
                    x = act.activation(h[:, :, :], c.HT[:, :, ds(b * SEQ, SEQ)], ACT.Copy).then_inc(s_h, 1)
                    pad(b, 0)
                    for g in range(TOTAL + CLAG):
                        if g >= CLAG and item(g - CLAG)[1] == 0:
                            m, head, t = item(g - CLAG)
                            act.wait_ge(s_tr, b * TOTAL + g - CLAG + 1)
                            if m >= 2:
                                act.wait_ge(s_ov, b * B_UNITS + m - 1)
                            act.activation(pt[:, m % 2, 0, 0:t + 1, t * P:(t + 1) * P],
                                           p_t[(g - CLAG) % 2][:, 0:keys(t)].rearrange("p (k n) -> p k n", n=P),
                                           ACT.Copy).then_inc(s_pa, 1)
                        if g < TOTAL:
                            if g % (B_REP * ITEMS) == (B_REP - 1) * ITEMS + 6 and g // (B_REP * ITEMS) + 1 < B_PAIRS:
                                pad(b, g // (B_REP * ITEMS) + 1)
                            _, _, t = item(g)
                            act.wait_ge(s_mn, b * TOTAL + g + 1)
                            act.activation(sm[:, g % RING, 0:keys(t)], sm[:, g % RING, 0:keys(t)], ACT.Exp, scale=-1.0,
                                           bias=mn[:, g % RING:g % RING + 1],
                                           accum_out=den[:, g % RING:g % RING + 1]).then_inc(s_exp, 1)
                        if g % ITEMS == VLAG + TB - ITEMS and g // ITEMS >= 2:
                            copy_out(b, g // ITEMS - 2)
                    copy_out(b, B_UNITS - 1)

            @block.vector
            def _(dve):
                def read(b, kind, m, part=None):
                    at = LOADS[kind, m]
                    bank = p_proj[at % 2]
                    if part != 1:
                        dve.wait_ge(s_proj, b * NPROJ + at + 1)
                    if kind == "v":
                        dve.tensor_copy(v_s[:, m, :], bank[:, :]).then_inc(s_prod, 1)
                        return
                    r = B_HD
                    scale = 1.0 if kind == "k" else -1.0 / 8
                    if part != 1:
                        dve.wait_ge(s_rope, b * NROPE + at - TB)
                        dve.scalar_tensor_tensor(prod[:, 0, :], bank[:, :], scale, cos[:, :], ALU.mult, ALU.mult)
                    if part == 0:
                        return
                    dve.scalar_tensor_tensor(prod[0:r, 1, :], bank[r:P, :], scale, sin[r:P, :], ALU.mult, ALU.mult)
                    dve.scalar_tensor_tensor(prod[r:P, 1, :], bank[0:r, :], scale, sin[0:r, :], ALU.mult,
                                             ALU.mult).then_inc(s_prod, 1)

                dve.memset(c.tick[:, :], 0.0).then_inc(s_z, 1)
                dve.wait_ge(s_w, 64)
                dve.wait_ge(s_z, 1)
                with dve.Fori(0, BATCH) as b:
                    for t in range(TB):
                        read(b, "v", t)
                    read(b, "k", 0)
                    read(b, "q", 0)
                    for g in range(TOTAL + CLAG):
                        m, n = g // ITEMS, g % ITEMS
                        if g >= CLAG and item(g - CLAG)[1] == 1:
                            m2, _, t2 = item(g - CLAG)
                            dve.wait_ge(s_tr, b * TOTAL + g - CLAG + 1)
                            if m2 >= 2:
                                dve.wait_ge(s_ov, b * B_UNITS + m2 - 1)
                            dve.tensor_copy(pt[:, m2 % 2, 1, 0:t2 + 1, t2 * P:(t2 + 1) * P],
                                            p_t[(g - CLAG) % 2][:, 0:keys(t2)].rearrange("p (k n) -> p k n", n=P)).then_inc(s_pd, 1)
                        if g < TOTAL:
                            _, _, t = item(g)
                            if g >= RING:
                                dve.wait_ge(s_tr, b * TOTAL + g - RING + 1)
                            dve.wait_ge(s_sc, b * TOTAL + g + 1)
                            dve.memset(c.tick[:, g % 3:g % 3 + 1], 0.0)
                            dve.tensor_tensor_reduce(sm[:, g % RING, 0:keys(t)], p_s[g % 3][:, 0:keys(t)],
                                                     mask[:, SEQ - keys(t):SEQ], 1.0, -3 * NEG, ALU.add, ALU.min,
                                                     mn[:, g % RING:g % RING + 1]).then_inc(s_mn, 1)
                        if INV <= g < TOTAL + INV:
                            s = (g - INV) % RING
                            dve.wait_ge(s_exp, b * TOTAL + g - INV + 1)
                            dve.reciprocal(rden[:, s:s + 1], den[:, s:s + 1]).then_inc(s_rd, 1)
                        if m + 1 < B_UNITS:
                            if (m + 1) % B_REP == 0 and n == 3:
                                read(b, "k", (m + 1) // B_REP)
                            if n in (5, 6):
                                read(b, "q", m + 1, n - 5)
                    for t in range(TB):
                        dve.wait_ge(s_y, b * TB + t + 1)
                        row = c.XN[:, ds(b * TB + t, 1), :].rearrange("p o d -> p (o d)")
                        dve.tensor_tensor(row, p_y[:, 0:DIM], row, ALU.add).then_inc(s_xn, 1)

            @block.gpsimd
            def _(pool):
                def add(b, kind, m):
                    at = LOADS[kind, m] - TB
                    pool.wait_ge(s_prod, b * NPROJ + LOADS[kind, m] + 1)
                    if kind == "q":
                        if m >= 2:
                            pool.wait_ge(s_sc, b * TOTAL + (m - 1) * ITEMS)
                        pool.tensor_tensor(q_r[:, m % 2, :], prod[:, 0, :], prod[:, 1, :], ALU.add).then_inc(s_rope, 1)
                    else:
                        pool.wait_ge(s_kp, b * B_PAIRS + m)
                        pool.tensor_tensor(k_r[:, :], prod[:, 0, :], prod[:, 1, :], ALU.add).then_inc(s_rope, 1)
                pool.wait_ge(s_z, 1)
                with pool.Fori(0, BATCH) as b:
                    add(b, "k", 0)
                    add(b, "q", 0)
                    for g in range(TOTAL):
                        m, n = g // ITEMS, g % ITEMS
                        s = g % RING
                        t = item(g)[2]
                        pool.wait_ge(s_rd, b * TOTAL + g + 1)
                        pool.tensor_tensor(sm[:, s, 0:keys(t)], sm[:, s, 0:keys(t)],
                                           rden[:, s:s + 1].to_broadcast([P, keys(t)]), ALU.mult).then_inc(s_pn, 1)
                        if m + 1 < B_UNITS:
                            if (m + 1) % B_REP == 0 and n == 1:
                                add(b, "k", (m + 1) // B_REP)
                            if n == 4:
                                add(b, "q", m + 1)


TOP_K = 4


def moe(nc, c, name, experts, hidden, routed, w13_dram, w2_dram, gate_dram, grouped):
    REST = hidden - P
    packed = REST <= 64
    UP = 64
    WG = 3 * P - (16 if packed else 0) if packed else 4 * P
    PAIRS = experts // 2
    U = 2 * BATCH
    with ExitStack() as st:
        def sb(n, shape, dt=F32):
            return st.enter_context(nc.sbuf_tensor(f"{name}_{n}", shape, dt))

        def pb(n):
            return st.enter_context(nc.psum_tensor(f"{name}_{n}", [P, SEQ], F32))

        def sem(n):
            return c.sem(f"{name}_{n}")
        WCOLS = KD * WG + 2 * DIM
        w_raw = sb("w_raw", [P, 2, WCOLS])
        w_hi, w_lo = sb("w_hi", [P, 2, WCOLS], F32R), sb("w_lo", [P, 2, WCOLS], F32R)
        sg = sb("sg", [P, 2, SEQ])
        a = sb("a", [P, 2, SEQ])
        a_hi, a_lo = sb("a_hi", [P, 2, 2, SEQ], F32R), sb("a_lo", [P, 2, 2, SEQ], F32R)
        NL = TILES * routed
        gw = sb("gw", [P, KD, routed])
        gw_hi, gw_lo = sb("gw_hi", [P, KD, routed], F32R), sb("gw_lo", [P, KD, routed], F32R)
        lg = sb("lg", [P, TILES, routed])
        ex = sb("ex", [P, TILES, routed])
        wt = sb("wt", [P, TILES, experts])
        wt_e = sb("wt_e", [P, 2, TILES])
        cmp_a, cmp_b = sb("cmp_a", [P, TB, routed, routed]), sb("cmp_b", [P, TB, routed, routed])
        rank = sb("rank", [P, TILES, routed])
        top, tsum, tinv = sb("top", [P, TILES]), sb("tsum", [P, TILES]), sb("tinv", [P, TILES])
        NG = 4
        gmax, grank = sb("gmax", [P, TILES, NG]), sb("grank", [P, TILES, NG])
        p_g, p_u = [pb("g0"), pb("g1")], [pb("u0"), pb("u1")]
        p_y = [pb(f"y{i}") for i in range(4)]

        s_w = [sem("w_even"), sem("w_odd")]
        s_whi, s_wlo = sem("w_high"), sem("w_low")
        s_gw, s_gw1, s_lg, s_lgc = sem("gate_w"), sem("gate_split"), sem("logits"), sem("logits_copied")
        s_dl, s_ex, s_rt = sem("shifted"), sem("exps"), sem("route")
        s_d = sem("dve")
        s_gu = sem("gate_up")
        s_sg, s_a = sem("silu"), sem("act_product")
        s_ahi, s_alo = sem("a_high"), sem("a_low")
        s_y, s_ya, s_z, s_we = sem("down"), sem("y_added"), sem("zeros"), sem("weight_column")

        def w13(part, slot, k, m, up):
            if packed and m == 1:
                return part[:, slot, k * WG + 2 * P:k * WG + 2 * P + UP + REST]
            at = k * WG + (2 * m + up) * P
            return part[:, slot, at:at + P]

        def w2(part, slot, m):
            return part[:, slot, KD * WG + m * DIM:KD * WG + (m + 1) * DIM]

        def product(pe, out, pairs):
            terms = [t for (ah, al), (bh, bl) in pairs for t in ((ah, bh), (ah, bl), (al, bh))]
            for n, (x, y) in enumerate(terms):
                mm = pe.matmul(out, x, y, start=(n == 0), stop=(n == len(terms) - 1))
            return mm

        def passes(eng, before, body):
            before()
            with eng.Fori(0, PAIRS - 1) as i:
                body(i, False)
            body(PAIRS - 1, True)

        with nc.Block() as block:
            @block.sync
            def _(sp):
                def load(e, slot):
                    sp.dma_start(w_raw[:, slot, 0:KD * WG], w13_dram[ds(e, 1)].rearrange("o p n -> (o p) n")).then_inc(s_w[slot], 16)
                    if packed:
                        sp.dma_start(w_raw[:, slot, KD * WG:KD * WG + DIM],
                                     w2_dram[ds(e, 1), 0:P].rearrange("o p n -> (o p) n")).then_inc(s_w[slot], 16)
                        sp.dma_start(w_raw[0:REST, slot, KD * WG + DIM:WCOLS],
                                     w2_dram[ds(e, 1), P:hidden].rearrange("o p n -> (o p) n")).then_inc(s_w[slot], 16)
                    else:
                        sp.dma_start(w_raw[:, slot, KD * WG:WCOLS].rearrange("p (m n) -> p m n", m=2),
                                     w2_dram[ds(e, 1)].rearrange("o (m p) n -> (o p) m n", p=P)).then_inc(s_w[slot], 16)
                sp.dma_start(gw[:, :, :], gate_dram).then_inc(s_gw, 16)
                if packed:
                    sp.wait_ge(s_z, 1)
                load(0, 0)
                load(1, 1)
                with sp.Fori(1, PAIRS) as i:
                    sp.wait_ge(s_wlo, i * 2 - 1)
                    load(i * 2, 0)
                    sp.wait_ge(s_wlo, i * 2)
                    load(i * 2 + 1, 1)
                sp.wait_ge(s_gw, 16)
            LOADED = 48 if packed else 32

            @block.tensor
            def _(pe):
                def logits():
                    pe.wait_ge(s_gw1, 2)
                    for t in range(TILES):
                        if t >= 4:
                            pe.wait_ge(s_lgc, t - 3)
                        rep = DIM // routed
                        parts = [[g[:, k, :].rearrange("p (o n) -> p o n", o=1).to_broadcast([P, rep, routed])
                                  for g in (gw_hi, gw_lo)] for k in range(KD)]
                        hts = [[h[:, k, t * P:(t + 1) * P] for h in (c.HT_hi, c.HT_lo)] for k in range(KD)]
                        out = p_y[t % 4][:, 0:DIM].rearrange("p (o n) -> p o n", o=rep)
                        product(pe, out, list(zip(hts, parts))).then_inc(s_lg, 1)

                def gate_up(i, u):
                    n = i * U + u
                    slot, b = (u % U) // BATCH, u % BATCH
                    pe.wait_ge(s_wlo, i * 2 + (u // BATCH) + 1)
                    hts = [[h[:, k, b * SEQ:(b + 1) * SEQ] for h in (c.HT_hi, c.HT_lo)] for k in range(KD)]
                    for m in range(2):
                        if not (isinstance(n, int) and n == 0):
                            pe.wait_ge(s_a, 2 * n - 1 + m)
                        for up, bank in enumerate((p_g[m], p_u[m])):
                            if packed and m == 1:
                                if up == 0:
                                    x = product(pe, bank[0:UP + REST, :],
                                                [([w13(p, slot, k, m, 0) for p in (w_hi, w_lo)], hts[k]) for k in range(KD)])
                                continue
                            x = product(pe, bank[:, :], [([w13(p, slot, k, m, up) for p in (w_hi, w_lo)], hts[k])
                                                         for k in range(KD)])
                        x.then_inc(s_gu, 1)

                def down(i, u):
                    n = i * U + u
                    slot = u // BATCH
                    pe.wait_ge(s_alo, n + 1)
                    pe.wait_ge(s_ya, i * U + max(u - 1, 0))
                    for t in range(TB):
                        al = [[x[:, u % 2, m, t * P:(t + 1) * P] for x in (a_hi, a_lo)] for m in range(2)]
                        x = product(pe, p_y[2 * (u % 2) + t // 2][:, (t % 2) * DIM:(t % 2 + 1) * DIM],
                                    [(al[m], [w2(p, slot, m) for p in (w_hi, w_lo)]) for m in range(2)])
                    x.then_inc(s_y, 1)

                def body(i, last):
                    for u in range(U):
                        if not (last and u == U - 1):
                            gate_up(i, u + 1)
                        down(i, u)

                def before():
                    logits()
                    pe.wait_ge(s_lgc, TILES)
                    gate_up(0, 0)
                passes(pe, before, body)

            @block.scalar
            def _(act):
                def silu(n, u):
                    for m in range(2):
                        act.wait_ge(s_gu, 2 * n + m + 1)
                        if not (isinstance(n, int) and n == 0):
                            act.wait_ge(s_a, 2 * n - 1 + m)
                        rows = REST if packed and m == 1 else P
                        act.activation(sg[0:rows, m, :], p_g[m][0:rows, :], ACT.Silu).then_inc(s_sg, 1)

                def a_high(i, n, u):
                    act.wait_ge(s_a, 2 * n + 2)
                    act.wait_ge(s_y, i * U + max(u - 1, 0))
                    act.activation(a_hi[:, u % 2, :, :], a[:, :, :], ACT.Copy).then_inc(s_ahi, 1)

                def body(i, last):
                    for u in range(U):
                        n = i * U + u
                        a_high(i, n, u)
                        if not (last and u == U - 1):
                            silu(n + 1, u + 1)
                        if not last and u in (BATCH, U - 1):
                            slot = 0 if u == BATCH else 1
                            act.wait_ge(s_w[slot], i * LOADED + 2 * LOADED)
                            act.wait_ge(s_y, i * U + (BATCH if slot == 0 else U))
                            act.activation(w_hi[:, slot, :], w_raw[:, slot, :], ACT.Copy).then_inc(s_whi, 1)

                def before():
                    act.wait_ge(s_gw, 16)
                    act.activation(gw_hi[:, :, :], gw[:, :, :], ACT.Copy).then_inc(s_gw1, 1)
                    for e in range(2):
                        act.wait_ge(s_w[e], LOADED)
                        act.activation(w_hi[:, e, :], w_raw[:, e, :], ACT.Copy).then_inc(s_whi, 1)
                    silu(0, 0)
                    act.wait_ge(s_dl, 1)
                    act.activation(ex[:, :, :], ex[:, :, :], ACT.Exp).then_inc(s_ex, 1)
                passes(act, before, body)

            @block.gpsimd
            def _(pool):
                def low(e, slot):
                    pool.wait_ge(s_whi, e + 1)
                    pool.tensor_tensor(w_lo[:, slot, :], w_raw[:, slot, :], w_hi[:, slot, :].bitcast(F32),
                                       ALU.subtract).then_inc(s_wlo, 1)

                def a_low(i, u):
                    n = i * U + u
                    pool.wait_ge(s_ahi, n + 1)
                    pool.tensor_tensor(a_lo[:, u % 2, :, :], a[:, :, :], a_hi[:, u % 2, :, :].bitcast(F32),
                                       ALU.subtract).then_inc(s_alo, 1)

                def body(i, last):
                    for u in range(U):
                        a_low(i, u)
                        if not last and u in (BATCH, U - 1):
                            low(i * 2 + 2 + (0 if u == BATCH else 1), 0 if u == BATCH else 1)

                def before():
                    pool.wait_ge(s_gw1, 1)
                    pool.tensor_tensor(gw_lo[:, :, :], gw[:, :, :], gw_hi[:, :, :].bitcast(F32),
                                       ALU.subtract).then_inc(s_gw1, 1)
                    low(0, 0)
                    low(1, 1)
                passes(pool, before, body)

            @block.vector
            def _(dve):
                chain = Chain(dve, s_d)

                def link(ins):
                    chain.add(ins)
                    chain.wait()

                def bc(x, shape):
                    return x.to_broadcast(shape)

                def ranks(values, count, out, between=None):
                    for g in range(GROUPS):
                        if between is not None and g == 1:
                            between()
                        ts = slice(g * TB, (g + 1) * TB)
                        A = cmp_a[:, :, 0:count, 0:count]
                        B = cmp_b[:, :, 0:count, 0:count]
                        vj = values[:, ts, :].rearrange("p t (o j) -> p t o j", o=1).to_broadcast([P, TB, count, count])
                        vi = values[:, ts, :].rearrange("p t (i o) -> p t i o", o=1).to_broadcast([P, TB, count, count])
                        link(dve.tensor_tensor(A, vj, vi, ALU.is_gt))
                        link(dve.tensor_tensor(B, vj, vi, ALU.is_equal))
                        for t in range(TB):
                            x = dve.tensor_tensor(cmp_b[:, t, 0:count, 0:count], cmp_b[:, t, 0:count, 0:count],
                                                  c.before[:, 0:count, 0:count], ALU.mult)
                        link(x)
                        link(dve.tensor_tensor(A, A, B, ALU.add))
                        link(dve.tensor_reduce(out[:, ts, :], A, AX.X, ALU.add))

                def column(x):
                    return x[:, :].rearrange("p (t o) -> p t o", o=1)

                def route():
                    for t in range(TILES):
                        dve.wait_ge(s_lg, t + 1)
                        dve.tensor_copy(lg[:, t, :], p_y[t % 4][:, 0:routed]).then_inc(s_lgc, 1)
                    dve.wait_ge(s_lgc, TILES)
                    product_a(0)
                    full = [P, TILES, routed]
                    if grouped:
                        grp = lg[:, :, :].rearrange("p t (g n) -> p t g n", g=NG)
                        link(dve.tensor_reduce(gmax[:, :, :], grp, AX.X, ALU.max))
                        ranks(gmax, NG, grank)
                        link(dve.tensor_scalar(grank[:, :, :], grank[:, :, :], 2.0, None, ALU.is_lt))
                        for g in range(NG):
                            n = routed // NG
                            x = dve.tensor_tensor(lg[:, :, g * n:(g + 1) * n], lg[:, :, g * n:(g + 1) * n],
                                                  grank[:, :, g:g + 1].to_broadcast([P, TILES, n]), ALU.mult)
                        link(x)
                    link(dve.tensor_reduce(top[:, :], lg[:, :, :], AX.X, ALU.max))
                    dve.tensor_tensor(ex[:, :, :], lg[:, :, :], column(top).to_broadcast(full), ALU.subtract).then_inc(s_dl, 1)
                    ranks(lg, routed, rank, between=lambda: product_a(1))
                    link(dve.tensor_scalar(rank[:, :, :], rank[:, :, :], float(TOP_K), None, ALU.is_lt))
                    dve.wait_ge(s_ex, 1)
                    sel = wt[:, :, 0:routed]
                    link(dve.tensor_tensor(sel, ex[:, :, :], rank[:, :, :], ALU.mult))
                    link(dve.tensor_reduce(tsum[:, :], ex[:, :, :] if grouped else sel, AX.X, ALU.add))
                    link(dve.reciprocal(tinv[:, :], tsum[:, :]))
                    if grouped:
                        link(dve.tensor_scalar(tinv[:, :], tinv[:, :], 16.0, None, ALU.mult))
                    link(dve.tensor_tensor(sel, sel, column(tinv).to_broadcast(full), ALU.mult))

                def product_a(n):
                    for m in range(2):
                        dve.wait_ge(s_sg, 2 * n + m + 1)
                        if not (isinstance(n, int) and n == 0):
                            dve.wait_ge(s_alo, n)
                        if packed and m == 1:
                            x = dve.tensor_tensor(a[0:REST, m, :], sg[0:REST, m, :], p_g[m][UP:UP + REST, :], ALU.mult)
                        else:
                            x = dve.tensor_tensor(a[:, m, :], sg[:, m, :], p_u[m][:, :], ALU.mult)
                        x.then_inc(s_a, 1)

                def add_y(i, u):
                    n = i * U + u
                    slot, b = u // BATCH, u % BATCH
                    if b == 0:
                        dve.wait_ge(s_ya, n)
                        e = i * 2 + slot
                        dve.tensor_copy(column_of(slot), wt[:, :, ds(e, 1)]).then_inc(s_we, 1)
                        dve.wait_ge(s_we, e + 1)
                    dve.wait_ge(s_y, n + 1)
                    for t in range(TB):
                        tt = b * TB + t
                        x = dve.scalar_tensor_tensor(c.Y[:, tt, :], p_y[2 * (u % 2) + t // 2][:, (t % 2) * DIM:(t % 2 + 1) * DIM],
                                                     wt_e[:, slot, tt:tt + 1], c.Y[:, tt, :], ALU.mult, ALU.add)
                    x.then_inc(s_ya, 1)

                def column_of(slot):
                    return wt_e[:, slot, :].rearrange("p (t o) -> p t o", o=1)

                def body(i, last):
                    for u in range(U):
                        if not (last and u == U - 1) and not (isinstance(i, int) and i == 0 and u == 0):
                            product_a(i * U + u + 1)
                        add_y(i, u)

                def before():
                    if packed:
                        dve.memset(w_raw[:, :, :], 0.0).then_inc(s_z, 1)
                        dve.memset(a[:, :, :], 0.0)
                        dve.memset(wt[:, :, :], 1.0)
                    dve.memset(c.Y[:, :, :], 0.0).then_inc(s_z, 1)
                    dve.wait_ge(s_z, 2 if packed else 1)
                    route()
                before()
                body(0, False)
                with dve.Fori(1, PAIRS - 1) as i:
                    body(i, False)
                body(PAIRS - 1, True)


C_HEADS, C_HD = 16, 16
C_SLOT = 64
C_PAIRS = C_HEADS // 2


def attention2(nc, c, wq_dram, wkv_dram, wo_dram, bias_dram, bo_dram, gain_dram, cos_dram, sin_dram):
    W2 = 2 * DIM
    NH = 2 * C_HEADS
    HALF = C_HD // 2
    N1 = TB * C_HEADS
    N2 = C_HEADS * TB
    SECOND = 22
    LAG = 2
    GROUP = 16
    STEPS = N1 + SECOND + LAG + 1
    RING = 6
    with ExitStack() as st:
        def sb(name, shape, dt=F32):
            return st.enter_context(nc.sbuf_tensor("c_" + name, shape, dt))

        def sem(name):
            return c.sem("c_" + name)
        bank = [st.enter_context(nc.psum_tensor(f"c_bank{i}", [P, SEQ], F32)) for i in range(8)]
        wq, wkv, wo = sb("wq", [P, KD, DIM]), sb("wkv", [P, KD, W2]), sb("wo", [P, KD, DIM])
        bias, bo = sb("bias", [P, 3 * DIM]), sb("bo", [P, DIM])
        gain = sb("gain", [P, 2, C_HD])
        gq = sb("gq", [P, 2, 2, C_HD])
        cos, sin = sb("cos", [P, TB, HALF]), sb("sin", [P, TB, HALF])
        mcos, msin, mneg = sb("mcos", [P, TB, HALF]), sb("msin", [P, TB, HALF]), sb("mneg", [P, TB, HALF])
        hq, hkv = sb("hq", [P, KD, SEQ]), sb("hkv", [P, KD, SEQ])
        qk = sb("qk", [P, TB, W2])
        pa, pb_ = sb("pa", [P, W2]), sb("pb", [P, W2])
        sq = sb("sq", [P, W2])
        hsum, ssq, std, rstd = (sb(n, [P, TB, NH]) for n in ("hsum", "ssq", "std", "rstd"))
        stack_q = c.XN[:, :, :].rearrange("p (t a) (h n) -> p t (a h) n", t=TB, n=C_SLOT)
        stack_k = sb("stack_k", [P, 2, C_HEADS, C_SLOT])
        qt = sb("qt", [P, C_PAIRS, SEQ], F32R)
        kp = sb("kp", [P, C_HEADS, SEQ], F32R)
        v_s = sb("v", [P, TB, C_HEADS, 2 * C_HD])
        nm = sb("nm", [P, TB, C_HEADS])
        pt = sb("pt", [P, RING, SEQ])
        o_s = sb("o", [P, 4, SEQ])
        a_t, a_f = sb("a_t", [P, 2, DIM]), sb("a_f", [P, 2, KD, P])
        rden = sb("rden", [P, TB, C_HEADS])

        s_w, s_z, s_g, s_h = sem("weights"), sem("zeros"), sem("gains"), sem("h_copied")
        s_p, s_z0, s_scaled = sem("times_gain"), sem("first_zeros"), sem("scaled")
        s_tab, s_proj, s_qk, s_ab, s_r, s_sum = (sem(n) for n in ("tables", "proj", "qk", "products", "rotated", "sum"))
        s_cen, s_sq, s_ssq, s_std, s_rs = (sem(n) for n in ("centred", "square", "square_sum", "std", "rstd"))
        s_n, s_hi, s_lo = sem("normed"), sem("high"), sem("low")
        s_tr, s_qe, s_ke = sem("stack_transposed"), sem("q_copied"), sem("k_copied")
        s_s1, s_nm, s_nh, s_nl = sem("scores"), sem("max"), sem("max_high"), sem("max_low")
        s_tr2, s_q2 = sem("q_transposed"), sem("q2_copied")
        s_s2, s_ex, s_pv, s_oe = sem("scores_t"), sem("exp"), sem("pv"), sem("o_copied")
        s_to, s_rd, s_at, s_ta, s_af, s_y, s_ye = (sem(n) for n in ("o_turned", "inverse", "divided", "a_turned",
                                                                    "a_copied", "out", "out_copied"))

        def pair(x, t, j):
            return x[:, t, 2 * j:2 * j + 2, :].rearrange("p h n -> p (h n)")

        def tiles_of(do):
            for at in range(TB + max(l for l, _ in do)):
                for level, f in do:
                    if 0 <= at - level < TB:
                        f(at - level)

        nc.disable_value_cache = True
        with nc.Block() as block:
            @block.sync
            def _(sp):
                for dst, src in ((wq[:, :, :], wq_dram), (wkv[:, :, :], wkv_dram), (wo[:, :, :], wo_dram),
                                 (bias[:, :], bias_dram.to_broadcast([P, 3 * DIM])),
                                 (bo[:, :], bo_dram.to_broadcast([P, DIM])),
                                 (gain[:, :, :].rearrange("p a n -> p (a n)"), gain_dram.to_broadcast([P, 2 * C_HD])),
                                 (cos[:, :, :], cos_dram), (sin[:, :, :], sin_dram)):
                    sp.dma_start(dst, src).then_inc(s_w, 16)
                sp.wait_ge(s_w, 128)

            @block.tensor
            def _(pe):
                def prep(b):
                    def proj(t):
                        n = b * TB + t
                        pe.wait_ge(s_qk, n)
                        for k in range(KD):
                            pe.matmul(bank[0][:, 0:DIM], hq[:, k, t * P:(t + 1) * P], wq[:, k, :],
                                      start=(k == 0), stop=(k == KD - 1))
                        for k in range(KD):
                            x = pe.matmul(bank[1][:, :], hkv[:, k, t * P:(t + 1) * P], wkv[:, k, :],
                                          start=(k == 0), stop=(k == KD - 1))
                        x.then_inc(s_proj, 1)

                    def turn(t):
                        n = b * TB + t
                        pe.wait_ge(s_lo, n + 1)
                        pe.wait_ge(s_qe, n)
                        pe.wait_ge(s_ke, n)
                        for stack, at, to in ((stack_q, t, 2), (stack_k, t % 2, 4)):
                            for j in range(C_PAIRS):
                                x = pe.transpose(bank[to + j // 4][:, (j % 4) * P:(j % 4 + 1) * P],
                                                 pair(stack, at, j), c.ident[:, :])
                        x.then_inc(s_tr, 1)
                    pe.wait_ge(s_h, b + 1)
                    pe.wait_ge(s_ye, b * TB)
                    tiles_of([(0, proj), (9, turn)])

                def passes(b):
                    pe.wait_ge(s_qe, b * TB + TB)
                    pe.wait_ge(s_ke, b * TB + TB)
                    pe.wait_ge(s_qk, b * TB + TB)
                    for step in range(STEPS):
                        f = step
                        if f < N1:
                            grp, t, h = f // GROUP, f // 4 % TB, f // GROUP * 4 + f % 4
                            if f >= 2:
                                pe.wait_ge(s_nm, b * N1 + f - 1)
                            pe.matmul(bank[2 + f % 2][:, :], qt[:, h // 2, t * P:(t + 1) * P], kp[:, h, :],
                                      start=True, stop=True).then_inc(s_s1, 1)
                        if step % GROUP == 3 and GROUP <= step < N1 + GROUP:
                            grp = step // GROUP - 1
                            pe.wait_ge(s_nl, b * 4 + grp + 1)
                            pe.wait_ge(s_q2, b * 4 + grp)
                            for j in range(2):
                                for t in range(TB):
                                    x = pe.transpose(bank[j][:, t * P:(t + 1) * P], pair(stack_q, t, 2 * grp + j), c.ident[:, :])
                            x.then_inc(s_tr2, 1)
                        g = step - SECOND
                        if 0 <= g < N2:
                            h, k = g // GROUP * 4 + g % 4, g // 4 % TB
                            if g % GROUP == 0:
                                pe.wait_ge(s_q2, b * 4 + g // GROUP + 1)
                            if g >= 2:
                                pe.wait_ge(s_ex, b * N2 + g - 1)
                            pe.matmul(bank[4 + g % 2][:, :], kp[:, h, k * P:(k + 1) * P], qt[:, h // 2, :],
                                      start=True, stop=True).then_inc(s_s2, 1)
                        m = g - LAG
                        if 0 <= m < N2:
                            grp, k, h = m // GROUP, m // 4 % TB, m % 4
                            pe.wait_ge(s_ex, b * N2 + m + 1)
                            if m % GROUP == 0:
                                pe.wait_ge(s_oe, b * 4 + max(grp - 1, 0))
                            pe.matmul(bank[6 + grp % 2][32 * h:32 * h + 32, :], v_s[:, k, 4 * grp + h, :], pt[:, m % RING, :],
                                      start=(k == 0), stop=(k == TB - 1)).then_inc(s_pv, 1)

                def finish(b):
                    def turn_o(t):
                        if t == 0:
                            pe.wait_ge(s_oe, b * 4 + 4)
                        for grp in range(4):
                            x = pe.transpose(bank[2 + t][:, grp * P:(grp + 1) * P], o_s[:, grp, t * P:(t + 1) * P], c.ident[:, :])
                        x.then_inc(s_to, 1)

                    def turn_a(t):
                        n = b * TB + t
                        pe.wait_ge(s_at, n + 1)
                        if t >= 2:
                            pe.wait_ge(s_af, n - 1)
                        for k in range(KD):
                            x = pe.transpose(bank[6 + t % 2][:, k * P:(k + 1) * P], a_t[:, t % 2, k * P:(k + 1) * P], c.ident[:, :])
                        x.then_inc(s_ta, 1)

                    def out(t):
                        n = b * TB + t
                        pe.wait_ge(s_af, n + 1)
                        if t >= 2:
                            pe.wait_ge(s_ye, n - 1)
                        for k in range(KD):
                            x = pe.matmul(bank[t % 2][:, 0:DIM], a_f[:, t % 2, k, :], wo[:, k, :],
                                          start=(k == 0), stop=(k == KD - 1))
                        x.then_inc(s_y, 1)
                    tiles_of([(0, turn_o), (2, turn_a), (4, out)])

                pe.wait_ge(s_w, 128)
                pe.wait_ge(s_z, 1)
                with pe.Fori(0, BATCH) as b:
                    prep(b)
                    passes(b)
                    finish(b)

            @block.scalar
            def _(act):
                def prep(b):
                    def square(t):
                        n = b * TB + t
                        act.wait_ge(s_cen, n + 1)
                        act.wait_ge(s_ssq, n)
                        act.activation(sq[:, :], qk[:, t, :], ACT.Square).then_inc(s_sq, 1)

                    def root(t):
                        act.wait_ge(s_ssq, b * TB + t + 1)
                        act.activation(std[:, t, :], ssq[:, t, :], ACT.Sqrt, bias=c.eps[:, :],
                                       scale=1.0 / C_HD).then_inc(s_std, 1)

                    def high(t):
                        n = b * TB + t
                        act.wait_ge(s_n, n + 1)
                        if t >= 2:
                            act.wait_ge(s_tr, n - 1)
                        for i, (stack, at) in enumerate(((stack_q, t), (stack_k, t % 2))):
                            src = qk[:, t, i * DIM:(i + 1) * DIM].rearrange("p (h n) -> p h n", n=C_HD)
                            for place in ((0, 1) if i == 0 else (0, 2)):
                                x = act.activation(stack[:, at, :, place * C_HD:(place + 1) * C_HD].bitcast(F32R), src, ACT.Copy)
                        x.then_inc(s_hi, 1)

                    def k_out(t):
                        n = b * TB + t
                        act.wait_ge(s_tr, n + 1)
                        for j in range(2):
                            src = bank[4 + j][:, :].rearrange("p (a n) -> p a n", n=P)
                            for half in range(2):
                                rows = slice(64 * half, 64 * half + 64)
                                x = act.activation(kp[rows, 8 * j + half:8 * j + 8:2, t * P:(t + 1) * P], src[rows, :, :], ACT.Copy)
                        x.then_inc(s_ke, 1)
                    tiles_of([(10, k_out), (3, square), (5, root), (8, high)])

                def passes(b):
                    for step in range(STEPS):
                        if step % GROUP == 0 and step and step <= N1:
                            grp = step // GROUP - 1
                            act.wait_ge(s_nm, b * N1 + step)
                            act.activation(stack_q[:, :, 4 * grp:4 * grp + 4, 48:49].bitcast(F32R),
                                           nm[:, :, 4 * grp:4 * grp + 4].rearrange("p t (h o) -> p t h o", o=1),
                                           ACT.Copy).then_inc(s_nh, 1)
                        g = step - SECOND
                        if 0 <= g < N2:
                            act.wait_ge(s_s2, b * N2 + g + 1)
                            if g >= RING:
                                act.wait_ge(s_pv, b * N2 + g - RING + 1)
                            act.activation(pt[:, g % RING, :], bank[4 + g % 2][:, :], ACT.Exp).then_inc(s_ex, 1)

                def finish(b):
                    def copied(t):
                        n = b * TB + t
                        act.wait_ge(s_ta, n + 1)
                        if t >= 2:
                            act.wait_ge(s_y, n - 1)
                        act.activation(a_f[:, t % 2, :, :].rearrange("p k n -> p (k n)"), bank[6 + t % 2][:, 0:DIM],
                                       ACT.Copy).then_inc(s_af, 1)
                    tiles_of([(3, copied)])

                act.wait_ge(s_w, 128)
                for i, f in enumerate((0.25, 1.0)):
                    x = act.activation(gq[:, :, i, :], gain[:, :, :], ACT.Copy, scale=f)
                x.then_inc(s_g, 1)
                act.wait_ge(s_z, 1)
                with act.Fori(0, BATCH) as b:
                    act.wait_ge(s_y, b * TB)
                    prep(b)
                    passes(b)
                    finish(b)

            @block.vector
            def _(dve):
                def prep(b):
                    norm = c.NORM[:, ds(b * TB, TB)].rearrange("p (t o) -> p t o", o=1).to_broadcast([P, TB, HALF])
                    dve.wait_ge(s_ab, b * TB)
                    for dst, src, f in ((mcos, cos, 0.5), (msin, sin, 0.5), (mneg, sin, -0.5)):
                        x = dve.scalar_tensor_tensor(dst[:, :, :], src[:, :, :], f, norm, ALU.mult, ALU.mult)
                    x.then_inc(s_tab, 1)
                    dve.wait_ge(s_tab, b + 1)

                    def products(t):
                        n = b * TB + t
                        dve.wait_ge(s_proj, n + 1)
                        dve.tensor_tensor(qk[:, t, 0:DIM], bank[0][:, 0:DIM], bias[:, 0:DIM], ALU.add)
                        dve.tensor_tensor(qk[:, t, DIM:W2], bank[1][:, 0:DIM], bias[:, DIM:W2], ALU.add)
                        dve.tensor_tensor(v_s[:, t, :, 0:C_HD], bank[1][:, DIM:W2].rearrange("p (h n) -> p h n", n=C_HD),
                                          bias[:, W2:].rearrange("p (h n) -> p h n", n=C_HD), ALU.add).then_inc(s_qk, 1)
                        dve.wait_ge(s_qk, n + 1)
                        dve.wait_ge(s_r, n)
                        x4 = qk[:, t, :].rearrange("p (h i o) -> p h i o", h=NH, o=2)
                        a4 = pa[:, :].rearrange("p (h i o) -> p h i o", h=NH, o=2)
                        b4 = pb_[:, :].rearrange("p (h i o) -> p h i o", h=NH, o=2)

                        def table(m):
                            return m[:, t, :].rearrange("p (o i) -> p o i", o=1).to_broadcast([P, NH, HALF])
                        for o in range(2):
                            dve.tensor_tensor(a4[:, :, :, o], x4[:, :, :, o], table(mcos), ALU.mult)
                            x = dve.tensor_tensor(b4[:, :, :, o], x4[:, :, :, 1 - o], table(msin if o else mneg), ALU.mult)
                        x.then_inc(s_ab, 1)

                    def heads(x):
                        return x.rearrange("p (h n) -> p h n", n=C_HD)

                    def centre(t):
                        n = b * TB + t
                        dve.wait_ge(s_r, n + 1)
                        dve.tensor_reduce(hsum[:, t, :], heads(qk[:, t, :]), AX.X, ALU.add).then_inc(s_sum, 1)
                        dve.wait_ge(s_sum, n + 1)
                        dve.scalar_tensor_tensor(heads(qk[:, t, :]),
                                                 hsum[:, t, :].rearrange("p (h o) -> p h o", o=1).to_broadcast([P, NH, C_HD]),
                                                 -1.0 / C_HD, heads(qk[:, t, :]), ALU.mult, ALU.add).then_inc(s_cen, 1)

                    def sums(t):
                        dve.wait_ge(s_sq, b * TB + t + 1)
                        dve.tensor_reduce(ssq[:, t, :], heads(sq[:, :]), AX.X, ALU.add).then_inc(s_ssq, 1)

                    def inverse(t):
                        dve.wait_ge(s_std, b * TB + t + 1)
                        n = b * TB + t
                        dve.reciprocal(rstd[:, t, :], std[:, t, :]).then_inc(s_rs, 1)
                        dve.wait_ge(s_rs, n + 1)
                        dve.tensor_tensor(heads(qk[:, t, :]), heads(qk[:, t, :]),
                                          rstd[:, t, :].rearrange("p (h o) -> p h o", o=1).to_broadcast([P, NH, C_HD]),
                                          ALU.mult).then_inc(s_scaled, 1)

                    def q_out(t):
                        dve.wait_ge(s_tr, b * TB + t + 1)
                        for j in range(2):
                            x = dve.tensor_copy(qt[:, 4 * j:4 * j + 4, t * P:(t + 1) * P],
                                                bank[2 + j][:, :].rearrange("p (a n) -> p a n", n=P))
                        x.then_inc(s_qe, 1)
                    tiles_of([(10, q_out), (0, products), (2, centre), (4, sums), (6, inverse)])

                def passes(b):
                    for step in range(STEPS):
                        f, grp = step, step // GROUP - 1
                        if f < N1:
                            t, h = f // 4 % TB, f // GROUP * 4 + f % 4
                            dve.wait_ge(s_s1, b * N1 + f + 1)
                            dve.tensor_reduce(nm[:, t, h:h + 1], bank[2 + f % 2][:, :], AX.X, ALU.max, negate=True).then_inc(s_nm, 1)
                        if step % GROUP == 2 and 0 <= grp < 4:
                            heads_ = slice(4 * grp, 4 * grp + 4)
                            dve.wait_ge(s_nh, b * 4 + grp + 1)
                            dve.tensor_tensor(stack_q[:, :, heads_, 49:50].bitcast(F32R),
                                              nm[:, :, heads_].rearrange("p t (h o) -> p t h o", o=1),
                                              stack_q[:, :, heads_, 48:49], ALU.subtract).then_inc(s_nl, 1)
                        if step % GROUP == 4 and 0 <= grp < 4:
                            dve.wait_ge(s_tr2, b * 4 + grp + 1)
                            for j in range(2):
                                x = dve.tensor_copy(qt[:, 2 * grp + j, :], bank[j][:, :])
                            x.then_inc(s_q2, 1)
                        m = step - SECOND - LAG
                        if m >= 0 and m % GROUP == GROUP - 1:
                            grp = m // GROUP
                            dve.wait_ge(s_pv, b * N2 + m + 1)
                            dve.wait_ge(s_to, b * TB)
                            dve.tensor_copy(o_s[:, grp, :], bank[6 + grp % 2][:, :]).then_inc(s_oe, 1)
                    dve.memset(stack_q[:, :, :, 48:50], 0.0)

                def finish(b):
                    def divided(t):
                        n = b * TB + t
                        dve.wait_ge(s_to, n + 1)
                        o = bank[2 + t][:, :].rearrange("p (h n) -> p h n", n=2 * C_HD)
                        dve.reciprocal(rden[:, t, :].rearrange("p (h o) -> p h o", o=1), o[:, :, C_HD:C_HD + 1]).then_inc(s_rd, 1)
                        dve.wait_ge(s_rd, n + 1)
                        if t >= 2:
                            dve.wait_ge(s_ta, n - 1)
                        dve.tensor_tensor(heads_of(a_t[:, t % 2, :]), o[:, :, 0:C_HD],
                                          rden[:, t, :].rearrange("p (h o) -> p h o", o=1).to_broadcast([P, C_HEADS, C_HD]),
                                          ALU.mult).then_inc(s_at, 1)

                    def biased(t):
                        n = b * TB + t
                        dve.wait_ge(s_y, n + 1)
                        dve.tensor_tensor(c.Y[:, ds(n, 1), :].rearrange("p o d -> p (o d)"), bank[t % 2][:, 0:DIM],
                                          bo[:, :], ALU.add).then_inc(s_ye, 1)
                    tiles_of([(1, divided), (5, biased)])

                def heads_of(x):
                    return x.rearrange("p (h n) -> p h n", n=C_HD)

                dve.memset(stack_q[:, :, :, 48:64], 0.0)
                dve.memset(stack_k[:, :, :, 48:64], 0.0)
                dve.memset(kp[:, :, :].bitcast(F32), 0.0)
                dve.memset(v_s[:, :, :, C_HD:], 1.0).then_inc(s_z0, 1)
                dve.wait_ge(s_z0, 1)
                dve.memset(stack_k[:, :, :, 48:50], 1.0).then_inc(s_z, 1)
                dve.wait_ge(s_z, 1)
                dve.wait_ge(s_w, 128)
                with dve.Fori(0, BATCH) as b:
                    prep(b)
                    passes(b)
                    finish(b)

            @block.gpsimd
            def _(pool):
                def copy_h(b):
                    for dst, src in ((hq, c.HTq), (hkv, c.HTkv)):
                        x = pool.tensor_copy(dst[:, :, :], src[:, :, ds(b * SEQ, SEQ)])
                    x.then_inc(s_h, 1)

                def prep(b):
                    def rotate(t):
                        pool.wait_ge(s_ab, b * TB + t + 1)
                        pool.tensor_tensor(qk[:, t, :], pa[:, :], pb_[:, :], ALU.add).then_inc(s_r, 1)

                    def normed(t):
                        n = b * TB + t
                        x = qk[:, t, :].rearrange("p (i h n) -> p i h n", i=2, n=C_HD)
                        for step, (op, sig) in enumerate(((ALU.mult, s_p), (ALU.add, s_n))):
                            pool.wait_ge(s_p if step else s_scaled, n + 1)
                            g = gq[:, step, :, :].rearrange("p i (o n) -> p i o n", o=1).to_broadcast([P, 2, C_HEADS, C_HD])
                            pool.tensor_tensor(x, x, g, op).then_inc(sig, 1)

                    def low(t):
                        n = b * TB + t
                        pool.wait_ge(s_hi, n + 1)
                        for i, (stack, at, place) in enumerate(((stack_q, t, 2), (stack_k, t % 2, 1))):
                            src = qk[:, t, i * DIM:(i + 1) * DIM].rearrange("p (h n) -> p h n", n=C_HD)
                            x = pool.tensor_tensor(stack[:, at, :, place * C_HD:(place + 1) * C_HD].bitcast(F32R), src,
                                                   stack[:, at, :, 0:C_HD], ALU.subtract)
                        x.then_inc(s_lo, 1)
                    tiles_of([(1, rotate), (7, normed), (9, low)])

                pool.wait_ge(s_g, 1)
                pool.wait_ge(s_z, 1)
                copy_h(0)
                with pool.Fori(0, BATCH - 1) as b:
                    prep(b)
                    pool.wait_ge(s_proj, b * TB + TB)
                    copy_h(b + 1)
                prep(BATCH - 1)
        nc.disable_value_cache = False


def sandwich(nc, x, a_w, a_wo, b_w, b_wo, b_cos, b_sin, m0_w13, m0_w2, m0_gate, c_wq, c_wkv, c_wo, c_bias, c_bo, c_gain,
             c_cos, c_sin, m1_w13, m1_w2, m1_gate, ident, a_cos, a_sin, a_mask, b_mask, b_rows, before, scales, out):
    with ExitStack() as st:
        c = Core(nc, st)
        c.X, c.XN, c.Y = (c.sb(n, [P, TILES, DIM]) for n in ("X", "XN", "Y"))
        c.ident, c.eps = c.sb("ident", [P, P]), c.sb("eps", [P, 1])
        c.NORM, c.NORM2 = c.sb("norm", [P, TILES]), c.sb("norm_squared", [P, TILES])
        c.scales = c.sb("scales", [P, 6, KD])
        ln_w, ff_ln_w, q_g, q_b, kv_g, kv_b = (c.scales[:, i, :] for i in range(6))

        def load(name, pairs, eps=False):
            loaded = c.sem(name)
            with nc.Block() as block:
                @block.sync
                def _(sp):
                    for dst, src in pairs:
                        sp.dma_start(dst, src).then_inc(loaded, 16)
                    sp.wait_ge(loaded, 16 * len(pairs))
                if eps:
                    @block.vector
                    def _(dve):
                        dve.memset(c.eps[:, :], EPS)

        with ExitStack() as raw:
            c.HT = raw.enter_context(nc.sbuf_tensor("HT", [P, KD, TOKENS], F32))
            with ExitStack() as scope:
                c.cosA, c.sinA = (scope.enter_context(nc.sbuf_tensor(n, [P, SEQ], F32)) for n in ("cosA", "sinA"))
                c.maskA = scope.enter_context(nc.sbuf_tensor("maskA", [P, A_SPAN], F32))
                load("constants_a", ((c.ident[:, :], ident), (c.cosA[:, :], a_cos), (c.sinA[:, :], a_sin),
                                     (c.maskA[:, :], a_mask), (c.scales[:, :, :], scales)), eps=True)
                norm_stage(nc, c, "n0", x_dram=x, outs=((c.HT, None, None),))
                attention0(nc, c, a_w, a_wo)
                c.free_semaphores()
            norm_stage(nc, c, "n1", post="rms", outs=((c.HT, ln_w, None),))
            with ExitStack() as scope:
                c.maskB = scope.enter_context(nc.sbuf_tensor("maskB", [P, SEQ], F32))
                c.rowsB = scope.enter_context(nc.sbuf_tensor("rowsB", [P, 2], F32))
                load("constants_b", ((c.maskB[:, :], b_mask), (c.rowsB[:, :], b_rows)))
                attention1(nc, c, b_w, b_wo, b_cos, b_sin)
                c.free_semaphores()
        with ExitStack() as split:
            c.HT_hi, c.HT_lo = (split.enter_context(nc.sbuf_tensor(n, [P, KD, TOKENS], F32R)) for n in ("HT0_hi", "HT0_lo"))
            norm_stage(nc, c, "n2", residual=False, post="rms", outs=(((c.HT_hi, c.HT_lo), ff_ln_w, None),))
            c.before = split.enter_context(nc.sbuf_tensor("before0", [P, EXPERTS, EXPERTS], F32))
            load("constants_m0", ((c.before[:, :, :], before.to_broadcast([P, EXPERTS, EXPERTS])),))
            moe(nc, c, "m0", EXPERTS, M0_HIDDEN, EXPERTS, m0_w13, m0_w2, m0_gate, False)
            c.free_semaphores()
        with ExitStack() as two:
            c.HTq, c.HTkv = (two.enter_context(nc.sbuf_tensor(n, [P, KD, TOKENS], F32)) for n in ("HTq", "HTkv"))
            norm_stage(nc, c, "n3", add="y", post="ln", outs=((c.HTq, q_g, q_b), (c.HTkv, kv_g, kv_b)))
            attention2(nc, c, c_wq, c_wkv, c_wo, c_bias, c_bo, c_gain, c_cos, c_sin)
            c.free_semaphores()
        with ExitStack() as split:
            c.HT_hi, c.HT_lo = (split.enter_context(nc.sbuf_tensor(n, [P, KD, TOKENS], F32R)) for n in ("HT1_hi", "HT1_lo"))
            norm_stage(nc, c, "n4", outs=(((c.HT_hi, c.HT_lo), None, None),))
            c.before = split.enter_context(nc.sbuf_tensor("before1", [P, EXPERTS, EXPERTS], F32))
            load("constants_m1", ((c.before[:, :, :], before.to_broadcast([P, EXPERTS, EXPERTS])),))
            moe(nc, c, "m1", EXPERTS + SHARED, M1_HIDDEN, EXPERTS, m1_w13, m1_w2, m1_gate, True)
            c.free_semaphores()
        norm_stage(nc, c, "n5", out_dram=out)


def half_rows(w):
    return w.reshape(KD, P, -1).transpose(1, 0, 2)


def tables():
    f = np.float32
    pos = np.arange(SEQ, dtype=f)

    inv = (f(1.0) / f(10000.0) ** (np.arange(0, A_HD, 2, dtype=f) / f(A_HD))).astype(f)
    ang = (pos[:, None] * inv[None, :]).T
    a_cos = np.concatenate([np.cos(ang)] * 2, 0)
    a_sin = np.concatenate([np.sin(ang), -np.sin(ang)], 0)
    query, key = np.arange(P)[:, None], np.arange(A_SPAN)[None, :] - WINDOW
    a_mask = np.where((key <= query) & (key > query - WINDOW), 0, NEG).astype(f)

    half = B_HD // 2
    inv = (f(1.0) / f(150000.0) ** (np.arange(half, dtype=f) / f(half))).astype(f)
    ang = (pos[:, None] * inv[None, :]).T
    b_cos = np.concatenate([np.cos(ang)] * 4, 0)
    b_sin = np.concatenate([np.sin(ang), np.sin(ang), -np.sin(ang), -np.sin(ang)], 0)
    key = np.arange(P)[None, :]
    b_mask = np.concatenate([np.zeros((P, SEQ - P), f), np.where(key <= query, 0, -NEG).astype(f)], 1)
    of_a = (np.arange(P) // half % 2 == 0).astype(f)
    b_rows = np.stack([of_a, 1 - of_a], 1)

    steps = np.linspace(0.0, 1.0, C_HD // 2, dtype=f)
    freq = ((f(8000.0 / 200.0) ** steps).astype(f) * f(200.0) / f(1000.0)).astype(f)
    freq = (f(200.0) * freq / f(1000.0)).astype(f)
    ang = (pos[:, None] * freq[None, :]).reshape(TB, P, -1).transpose(1, 0, 2)

    expert = np.arange(EXPERTS)
    before = (expert[None, :] < expert[:, None]).astype(f)[None]
    return {"ident": np.eye(P, dtype=f), "a_cos": a_cos, "a_sin": a_sin, "a_mask": a_mask, "b_cos": b_cos, "b_sin": b_sin,
            "b_mask": b_mask, "b_rows": b_rows, "c_cos": np.cos(ang), "c_sin": np.sin(ang), "before": before}


def layout(i):
    f = np.float32
    d = {"x": i["L0_attn_x"]}
    d["a_w"] = i["L0_attn_w_qkv"].reshape(3, A_HEADS, A_HD, KD, P).transpose(1, 4, 3, 0, 2)
    d["a_wo"] = i["L0_attn_w_o"].T.reshape(A_HEADS, A_HD, DIM)

    def interleave(a, b):
        h = B_HD // 2
        return np.concatenate([a[:, :h], b[:, :h], a[:, h:], b[:, h:]], 1)
    q = i["L0_ffn_wq"].reshape(DIM, B_HEADS, B_HD)
    k, v = (i[n].reshape(DIM, B_KV, B_HD) for n in ("L0_ffn_wk", "L0_ffn_wv"))
    pairs = []
    for p in range(B_PAIRS):
        a, b = 2 * p, 2 * p + 1
        cols = [interleave(k[:, a], k[:, b]), np.concatenate([v[:, a], v[:, b]], 1)]
        cols += [interleave(q[:, B_REP * a + j], q[:, B_REP * b + j]) for j in range(B_REP)]
        pairs.append(np.stack(cols))
    d["b_w"] = np.stack(pairs).reshape(B_PAIRS, 2 + B_REP, KD, P, P).transpose(3, 2, 0, 1, 4)
    d["b_wo"] = i["L0_ffn_wo"].reshape(B_PAIRS, 2, B_REP, B_HD, DIM).transpose(1, 3, 0, 2, 4).reshape(P, B_UNITS, DIM)

    w1, w3 = (i[n].reshape(EXPERTS, KD, P, 2, P) for n in ("L0_ffn_w1", "L0_ffn_w3"))
    d["m0_w13"] = np.stack([w1, w3], 4).transpose(0, 2, 1, 3, 4, 5).reshape(EXPERTS, P, -1)
    d["m0_w2"] = i["L0_ffn_w2"]
    d["m0_gate"] = half_rows(i["L0_ffn_wg"])

    d["c_wq"], d["c_wkv"], d["c_wo"] = (half_rows(i["L1_attn_" + n]) for n in ("Wq", "Wkv", "Wo"))
    d["c_bias"] = np.concatenate([i["L1_attn_bq"], i["L1_attn_bkv"]])[None]
    d["c_bo"] = i["L1_attn_bo"][None]
    d["c_gain"] = np.concatenate([i["L1_attn_ln_h_g"], i["L1_attn_ln_h_b"]])[None]

    n = M1_HIDDEN
    gu, sgu = i["L1_ffn_w_gate_up"], i["L1_ffn_shared_gate_up"]
    gate = np.concatenate([gu[:, :, :n], np.stack([sgu[:, :n], sgu[:, n:2 * n]])])
    up = np.concatenate([gu[:, :, n:], np.stack([sgu[:, 2 * n:3 * n], sgu[:, 3 * n:]])])
    pad = np.zeros((EXPERTS + SHARED, DIM, 64 - (n - P)), f)
    w = np.concatenate([gate[:, :, :P], up[:, :, :P], gate[:, :, P:], pad, up[:, :, P:]], 2)
    d["m1_w13"] = w.reshape(EXPERTS + SHARED, KD, P, -1).transpose(0, 2, 1, 3).reshape(EXPERTS + SHARED, P, -1)
    d["m1_w2"] = np.concatenate([i["L1_ffn_w_down"], np.stack([i["L1_ffn_shared_down"][:n], i["L1_ffn_shared_down"][n:]])])
    d["m1_gate"] = half_rows(i["L1_ffn_gate_w"].T)

    vectors = ("L0_ffn_ln_w", "L0_ffn_ff_ln_w", "L1_attn_ln_q_g", "L1_attn_ln_q_b", "L1_attn_ln_kv_g", "L1_attn_ln_kv_b")
    d["scales"] = np.stack([i[v].reshape(KD, P) for v in vectors]).transpose(2, 0, 1)
    return d


_INS = ["x", "a_w", "a_wo", "b_w", "b_wo", "b_cos", "b_sin", "m0_w13", "m0_w2", "m0_gate", "c_wq", "c_wkv", "c_wo", "c_bias",
        "c_bo", "c_gain", "c_cos", "c_sin", "m1_w13", "m1_w2", "m1_gate", "ident", "a_cos", "a_sin", "a_mask", "b_mask",
        "b_rows", "before", "scales"]


def kernel(**inputs):
    import concourse.bacc as _bacc
    from concourse import mybir as _mybir
    from concourse.bass_utils import run_bass_kernel_spmd as _run

    laid = layout({n: np.asarray(a) for n, a in inputs.items()})
    laid.update(tables())
    nc = _bacc.Bacc("TRN2", target_bir_lowering=False, num_devices=1)
    arrays, args = {}, []
    for name in _INS:
        a = np.ascontiguousarray(laid[name])
        arrays[f"in_{name}_dram"] = a
        args.append(nc.dram_tensor(f"in_{name}_dram", a.shape, _mybir.dt.from_np(a.dtype), kind="ExternalInput").ap())
    args.append(nc.dram_tensor("out_dram", (BATCH, SEQ, DIM), F32, kind="ExternalOutput").ap())
    sandwich(nc, *args)
    r = _run(nc, [arrays], core_ids=[0])
    return r.results[0]["out_dram"]
```
